# Optimizing a Trainium2 kernel written in Bass

```python
import numpy as np
import jax
import jax.numpy as jnp

def _softmax(x, axis=-1):
    return jax.nn.softmax(x, axis=axis)

def _gelu(x):
    return jax.nn.gelu(x, approximate=True)

def _silu(x):
    return jax.nn.silu(x)

def _sigmoid(x):
    return jax.nn.sigmoid(x)

def _layernorm(x, axis=-1, eps=1e-05):
    m = jnp.mean(x, axis=axis, keepdims=True)
    v = jnp.var(x, axis=axis, keepdims=True)
    return (x - m) / jnp.sqrt(v + eps)

def _scatter_add(tgt, idx, src, axis=0):
    return tgt.at[idx].add(src)

def _segment_sum(src, seg, n):
    return jax.ops.segment_sum(src, seg, n)
kernel_name = 'mk_adj_preln_d4_adj_r2_af1c97'

def setup_inputs(seed: int=0):
    np.random.seed(seed)
    _w = jnp.asarray

    def _rec_inputs():
        import jax
        import jax.numpy as jnp
        _gk = jax.random.key(seed)
        x = 7.22e-05 + 1 * jax.random.normal(jax.random.fold_in(_gk, 1), (1354, 256), jnp.float32)
        _w = (1.0 + jnp.arange(1354, dtype=jnp.float32)) ** (-0.5)
        _w = _w / _w.mean()
        _pij = jnp.clip(0.00295421 * _w[:, None] * _w[None, :], 0.0, 1.0)
        _a = jax.random.uniform(jax.random.fold_in(_gk, 2), (1354, 1354)) < _pij
        _a = jnp.logical_or(_a, jnp.eye(1354, dtype=bool))
        _af = _a.astype(jnp.float32)
        _af = _af * jax.random.uniform(jax.random.fold_in(_gk, 3), (1354, 1354), jnp.float32, 0.05, 1)
        adj = _af
        return (x, adj)
    x, adj = _rec_inputs()

    def _L0_gnn_setup():
        import jax, jax.numpy as jnp
        import numpy as np
        N = 8192
        IN_F = 256
        OUT_F = 256
        key = jax.random.key(seed)
        k1, k2, k3, k4, k5 = jax.random.split(key, 5)
        stdv = 1.0 / np.sqrt(OUT_F)
        inp = {'input': jax.random.normal(k1, (N, IN_F), dtype=jnp.float32), 'adj': jax.random.uniform(k2, (N, N), dtype=jnp.float32), 'weight': jax.random.uniform(k3, (IN_F, OUT_F), dtype=jnp.float32, minval=-stdv, maxval=stdv), 'learnable_diag_1': 0.01 * jax.random.normal(k4, (IN_F,), dtype=jnp.float32), 'bias': jax.random.uniform(k5, (OUT_F,), dtype=jnp.float32, minval=-stdv, maxval=stdv)}
        return inp
    _L0_gnn_all = _L0_gnn_setup()
    _L0_gnn_in = {k: v for k, v in _L0_gnn_all.items() if k in ('weight', 'learnable_diag_1', 'bias')}
    del _L0_gnn_all

    def _L1_gnn_setup():
        import jax, jax.numpy as jnp
        import numpy as np
        N = 3072
        D_IN = 256
        D_OUT = 256
        DENSITY = 0.005
        key = jax.random.key(seed)
        ks = jax.random.split(key, 12)
        x = jax.random.normal(ks[0], (N, D_IN), dtype=jnp.float32)
        adj_a = (jax.random.uniform(ks[1], (N, N)) < DENSITY).astype(jnp.float32)
        adj_b = (jax.random.uniform(ks[2], (N, N)) < DENSITY).astype(jnp.float32)
        W_sa = jax.random.normal(ks[3], (D_IN, D_OUT), dtype=jnp.float32) * (1.414 / np.sqrt(D_IN + D_OUT))
        a_sa = jax.random.normal(ks[4], (1, 2 * D_OUT), dtype=jnp.float32) * (1.414 / np.sqrt(1 + 2 * D_OUT))
        stdv = 1.0 / np.sqrt(D_OUT)
        W_gcnb = jax.random.uniform(ks[5], (D_IN, D_OUT), minval=-stdv, maxval=stdv, dtype=jnp.float32)
        b_gcnb = jax.random.uniform(ks[6], (D_OUT,), minval=-stdv, maxval=stdv, dtype=jnp.float32)
        s = 1.0 / np.sqrt(2 * D_IN)
        Wa = jax.random.uniform(ks[7], (1, 2 * D_IN), minval=-s, maxval=s, dtype=jnp.float32)
        ba = jax.random.uniform(ks[8], (1,), minval=-s, maxval=s, dtype=jnp.float32)
        Wb = jax.random.uniform(ks[9], (1, 2 * D_IN), minval=-s, maxval=s, dtype=jnp.float32)
        bb = jax.random.uniform(ks[10], (1,), minval=-s, maxval=s, dtype=jnp.float32)
        return {'x': x, 'adj_a': adj_a, 'adj_b': adj_b, 'W_sa': W_sa, 'a_sa': a_sa, 'W_gcnb': W_gcnb, 'b_gcnb': b_gcnb, 'Wa': Wa, 'ba': ba, 'Wb': Wb, 'bb': bb}
    _L1_gnn_all = _L1_gnn_setup()
    _L1_gnn_in = {k: v for k, v in _L1_gnn_all.items() if k in ('W_sa', 'a_sa', 'W_gcnb', 'b_gcnb', 'Wa', 'ba', 'Wb', 'bb')}
    del _L1_gnn_all

    def _L2_gnn_setup():
        import jax, jax.numpy as jnp
        import numpy as np
        N = 4096
        D = 256
        L = 2
        NEG_SLOPE = 0.01

        def _gat_layer(x, W, adj):
            proj = x @ W
            Wh, Ws = jnp.split(proj, 2, axis=-1)
            scores = Wh @ Ws.T
            a = jax.nn.softmax(scores, axis=-1) * adj
            out = a @ Wh
            out = out + x
            return jax.nn.leaky_relu(out, NEG_SLOPE)
        key = jax.random.key(seed)
        k1, k2, k3 = jax.random.split(key, 3)
        inputs = jax.random.normal(k1, (N, D), dtype=jnp.float32)
        adj = jax.random.randint(k2, (N, N), 0, 2).astype(jnp.float32)
        W_stack = jax.random.normal(k3, (L, D, 2 * D), dtype=jnp.float32) * (1.0 / np.sqrt(D))
        return {'inputs': inputs, 'adj': adj, 'W_stack': W_stack}
    _L2_gnn_all = _L2_gnn_setup()
    _L2_gnn_in = {k: v for k, v in _L2_gnn_all.items() if k in ('W_stack',)}
    del _L2_gnn_all

    def _L3_gnn_setup():
        import jax, jax.numpy as jnp
        import numpy as np
        N, D_IN, D_ATTN, STEPS, P_NUC, TAU = (2048, 256, 64, 2, 0.9, 1.0)
        LN_EPS = 1e-05

        def _xavier(key, shape):
            fan_in, fan_out = (shape[-2], shape[-1])
            lim = np.sqrt(6.0 / (fan_in + fan_out))
            return jax.random.uniform(key, shape, jnp.float32, -lim, lim)

        def _adj_from_feats(Xa, W1, W2, W3):
            Q = Xa @ W1
            K = Xa @ W3
            logits = Q @ W2 @ K.T / TAU
            idx = jnp.argsort(-logits, axis=1)
            vals = jnp.take_along_axis(logits, idx, axis=1)
            csum = jnp.cumsum(jax.nn.softmax(vals, axis=1), axis=1)
            k_i = jnp.sum(csum < P_NUC, axis=1) + 1
            ranks = jnp.arange(logits.shape[1])[None, :]
            keep_sorted = ranks < k_i[:, None]
            inv = jnp.argsort(idx, axis=1)
            keep = jnp.take_along_axis(keep_sorted, inv, axis=1)
            masked = jnp.where(keep, logits, -jnp.inf)
            return jax.nn.softmax(masked, axis=1)
        key = jax.random.key(seed)
        ks = jax.random.split(key, 9)
        return {'X': jax.random.normal(ks[0], (N, D_IN), jnp.float32), 'S': jax.random.uniform(ks[1], (N, N), jnp.float32), 'W1': _xavier(ks[2], (D_IN, D_ATTN)), 'W2': _xavier(ks[3], (D_ATTN, D_ATTN)), 'W3': _xavier(ks[4], (D_IN, D_ATTN)), 'U1': _xavier(ks[5], (STEPS, D_IN, D_IN)), 'U2': _xavier(ks[6], (STEPS, D_IN, D_IN)), 'U3': _xavier(ks[7], (STEPS, D_IN, D_IN)), 'gamma': jnp.ones((D_IN,), jnp.float32), 'beta': jnp.zeros((D_IN,), jnp.float32)}
    _L3_gnn_all = _L3_gnn_setup()
    _L3_gnn_in = {k: v for k, v in _L3_gnn_all.items() if k in ('W1', 'W2', 'W3', 'U1', 'U2', 'U3', 'gamma', 'beta')}
    del _L3_gnn_all
    return {'x': x, 'adj': adj, 'L0_gnn_weight': _L0_gnn_in['weight'], 'L0_gnn_learnable_diag_1': _L0_gnn_in['learnable_diag_1'], 'L0_gnn_bias': _L0_gnn_in['bias'], 'L1_gnn_W_sa': _L1_gnn_in['W_sa'], 'L1_gnn_a_sa': _L1_gnn_in['a_sa'], 'L1_gnn_W_gcnb': _L1_gnn_in['W_gcnb'], 'L1_gnn_b_gcnb': _L1_gnn_in['b_gcnb'], 'L1_gnn_Wa': _L1_gnn_in['Wa'], 'L1_gnn_ba': _L1_gnn_in['ba'], 'L1_gnn_Wb': _L1_gnn_in['Wb'], 'L1_gnn_bb': _L1_gnn_in['bb'], 'L2_gnn_W_stack': _L2_gnn_in['W_stack'], 'L3_gnn_W1': _L3_gnn_in['W1'], 'L3_gnn_W2': _L3_gnn_in['W2'], 'L3_gnn_W3': _L3_gnn_in['W3'], 'L3_gnn_U1': _L3_gnn_in['U1'], 'L3_gnn_U2': _L3_gnn_in['U2'], 'L3_gnn_U3': _L3_gnn_in['U3'], 'L3_gnn_gamma': _L3_gnn_in['gamma'], 'L3_gnn_beta': _L3_gnn_in['beta']}

def reference(x, adj, L0_gnn_weight, L0_gnn_learnable_diag_1, L0_gnn_bias, L1_gnn_W_sa, L1_gnn_a_sa, L1_gnn_W_gcnb, L1_gnn_b_gcnb, L1_gnn_Wa, L1_gnn_ba, L1_gnn_Wb, L1_gnn_bb, L2_gnn_W_stack, L3_gnn_W1, L3_gnn_W2, L3_gnn_W3, L3_gnn_U1, L3_gnn_U2, L3_gnn_U3, L3_gnn_gamma, L3_gnn_beta):
    import jax
    import jax.numpy as jnp

    def _L0_gnn_ref(input, adj, weight, learnable_diag_1, bias):
        import jax, jax.numpy as jnp
        import numpy as np
        N = 8192
        IN_F = 256
        OUT_F = 256
        e1 = jnp.matmul(adj, input)
        e2 = e1 * (learnable_diag_1 + 1.0)
        return jnp.matmul(input - e2, weight) + bias

    def _L1_gnn_ref(x, adj_a, adj_b, W_sa, a_sa, W_gcnb, b_gcnb, Wa, ba, Wb, bb):
        import jax, jax.numpy as jnp
        import numpy as np
        N = 3072
        D_IN = 256
        D_OUT = 256
        DENSITY = 0.005
        type_sum_a = adj_a @ x
        type_sum_b = adj_b @ x
        attn_a = jax.nn.sigmoid(jnp.concatenate([type_sum_a, x], axis=1) @ Wa.T + ba)
        attn_b = jax.nn.sigmoid(jnp.concatenate([type_sum_b, x], axis=1) @ Wb.T + bb)
        h = x @ W_sa
        Hd = h.shape[1]
        s_left = h @ a_sa[0, :Hd]
        s_right = h @ a_sa[0, Hd:]
        scores = s_left[:, None] + s_right[None, :]
        e = jnp.where(adj_a != 0, jnp.exp(-jax.nn.leaky_relu(scores, 0.01)), 0.0)
        attn = e / (jnp.sum(e, axis=1, keepdims=True) + 1e-05)
        x_a = attn @ h
        x_b = adj_b @ (x @ W_gcnb) + b_gcnb
        return jax.nn.sigmoid(attn_a * x_a + attn_b * x_b)

    def _L2_gnn_ref(inputs, adj, W_stack):
        import jax, jax.numpy as jnp
        import numpy as np
        N = 4096
        D = 256
        L = 2
        NEG_SLOPE = 0.01

        def _gat_layer(x, W, adj):
            proj = x @ W
            Wh, Ws = jnp.split(proj, 2, axis=-1)
            scores = Wh @ Ws.T
            a = jax.nn.softmax(scores, axis=-1) * adj
            out = a @ Wh
            out = out + x
            return jax.nn.leaky_relu(out, NEG_SLOPE)
        x = inputs
        for l in range(W_stack.shape[0]):
            x = _gat_layer(x, W_stack[l], adj)
        return x

    def _L3_gnn_ref(X, S, W1, W2, W3, U1, U2, U3, gamma, beta):
        import jax, jax.numpy as jnp
        import numpy as np
        N, D_IN, D_ATTN, STEPS, P_NUC, TAU = (2048, 256, 64, 2, 0.9, 1.0)
        LN_EPS = 1e-05

        def _xavier(key, shape):
            fan_in, fan_out = (shape[-2], shape[-1])
            lim = np.sqrt(6.0 / (fan_in + fan_out))
            return jax.random.uniform(key, shape, jnp.float32, -lim, lim)

        def _adj_from_feats(Xa, W1, W2, W3):
            Q = Xa @ W1
            K = Xa @ W3
            logits = Q @ W2 @ K.T / TAU
            idx = jnp.argsort(-logits, axis=1)
            vals = jnp.take_along_axis(logits, idx, axis=1)
            csum = jnp.cumsum(jax.nn.softmax(vals, axis=1), axis=1)
            k_i = jnp.sum(csum < P_NUC, axis=1) + 1
            ranks = jnp.arange(logits.shape[1])[None, :]
            keep_sorted = ranks < k_i[:, None]
            inv = jnp.argsort(idx, axis=1)
            keep = jnp.take_along_axis(keep_sorted, inv, axis=1)
            masked = jnp.where(keep, logits, -jnp.inf)
            return jax.nn.softmax(masked, axis=1)
        n = X.shape[0]
        S = S + jnp.eye(n, dtype=X.dtype)
        Rf = S / jnp.clip(S.sum(axis=1, keepdims=True), 1e-12)
        Rb = S / jnp.clip(S.sum(axis=0), 1e-12)[:, None]
        Xf, Xb, Xa = (X, X, X)
        Z = jnp.zeros_like(X)
        for s in range(STEPS):
            A = _adj_from_feats(Xa, W1, W2, W3)
            Xf = Rf @ Xf
            Xb = Rb @ Xb
            Xa = A @ Xa
            Z = Z + (Xf @ U1[s] + Xb @ U2[s] + Xa @ U3[s])
        Y = X + Z
        mu = Y.mean(axis=-1, keepdims=True)
        var = Y.var(axis=-1, keepdims=True)
        return (Y - mu) / jnp.sqrt(var + LN_EPS) * gamma + beta
    h = jnp.maximum(_layernorm(x, axis=-1), 0.0)
    x = x + _L0_gnn_ref(h, adj, L0_gnn_weight, L0_gnn_learnable_diag_1, L0_gnn_bias)
    h = jnp.maximum(_layernorm(x, axis=-1), 0.0)
    x = x + _L1_gnn_ref(h, adj, adj, L1_gnn_W_sa, L1_gnn_a_sa, L1_gnn_W_gcnb, L1_gnn_b_gcnb, L1_gnn_Wa, L1_gnn_ba, L1_gnn_Wb, L1_gnn_bb)
    h = jnp.maximum(_layernorm(x, axis=-1), 0.0)
    x = x + _L2_gnn_ref(h, adj, L2_gnn_W_stack)
    h = jnp.maximum(_layernorm(x, axis=-1), 0.0)
    x = x + _L3_gnn_ref(h, adj, L3_gnn_W1, L3_gnn_W2, L3_gnn_W3, L3_gnn_U1, L3_gnn_U2, L3_gnn_U3, L3_gnn_gamma, L3_gnn_beta)
    return x

_drawn_inputs = setup_inputs


def setup_inputs(seed=0):
    import zlib

    import numpy as np

    out = dict(_drawn_inputs(seed))
    spreads = {'L3_gnn_gamma': (1.0, 0.2), 'L3_gnn_beta': (0.0, 0.1)}
    factors = {'L0_gnn_learnable_diag_1': 5.644,
     'L1_gnn_a_sa': 4.005,
     'L1_gnn_b_gcnb': 7.942,
     'L1_gnn_Wa': 3.981,
     'L2_gnn_W_stack': 4.307}
    for name, (base, spread) in spreads.items():
        noise = np.random.default_rng([zlib.crc32(name.encode()), seed]).standard_normal(out[name].shape)
        drawn = base * np.exp(spread * noise) if base else spread * noise
        out[name] = jnp.asarray(drawn.astype(out[name].dtype))
    for name, factor in factors.items():
        out[name] = (out[name] * factor).astype(out[name].dtype)
    return out
```

```python
from contextlib import ExitStack

import concourse.bass as bass
from concourse import mybir

F32 = mybir.dt.float32
F32R = mybir.dt.float32r
U32 = mybir.dt.uint32
ALU = mybir.AluOpType
ACT = mybir.ActivationFunctionType
AX = mybir.AxisListType

P = 128
N = 1354
NT = -(-N // P)
NP = NT * P
D = 256
KB = D // P
BANK = 512
CHUNKS = [(c, min(BANK, N - c)) for c in range(0, N, BANK)]
LN_EPS = 1e-5
SLOPE = 0.01
P_NUC = 0.9
BASE_BITS = 0x38000000
TOP_BIT = 26
SEARCH_BITS = 22

PJ = {name: NT * k for k, name in enumerate(["L0", "L1", "L2a", "L2b", "L3s", "L3q", "L3a"])}
GA = {name: NT * k for k, name in enumerate(["L0", "L1b", "L1a", "L2a", "L2b", "L3s", "L3t", "A0", "A1"])}
SCO = {name: NT * k for k, name in enumerate(["L2a", "L2b", "A0", "A1"])}
MSK = {name: NT * k for k, name in enumerate(["L1a", "L2a", "L2b"])}
KEEP = {name: NT * k for k, name in enumerate(["A0", "A1"])}
WPREP = {name: k + 1 for k, name in enumerate(["L0", "L1", "L1r", "L2a", "L2b", "L3s", "L3u", "L3q", "L3a"])}
NORM = {name: k + 1 for k, name in enumerate(["L0", "L1", "L2", "L3", "end"])}


def wait(eng, sem, value):
    if isinstance(value, int) and value <= 0:
        return
    eng.wait_ge(sem, value)


def pipeline(eng, *steps):
    def turn(t, parity, static):
        for lag, step in enumerate(steps):
            if static and not 0 <= t - lag < NT:
                continue
            step(t - lag, (parity + lag) % 2)

    for t in range(3):
        turn(t, t % 2, True)
    with eng.Fori(3, NT - 1, 2) as t:
        turn(t, 1, False)
        turn(t + 1, 0, False)
    for t in range(NT, NT + len(steps) - 1):
        turn(t, t % 2, True)


def each_tile(eng, step):
    with eng.Fori(0, NT, 1) as t:
        step(t)


def build(nc, x, adjT, w0, d0, b0, w_sa, a_sa, w_gc, b_gc, wa, ba, wb, bb, w_l2, w1, w2, w3, u1, u2, u3, gamma,
          beta, out):
    with ExitStack() as ctx:
        def sb(name, shape, dt=F32, at=ctx):
            return at.enter_context(nc.sbuf_tensor(name, shape, dt))

        def sem(name):
            return ctx.enter_context(nc.semaphore(name))

        X = sb("x_rows", [P, NT, D])
        H = sb("h_rows", [P, NT, D])
        Y = sb("y_rows", [P, NT, D])
        FH = sb("feat_hi", [P, NT, D + 2], F32R)
        FL = sb("feat_lo", [P, NT, D + 2], F32R)
        SH = sb("strip_hi_buf", [P, 2, NT, P], F32R)
        SL = sb("strip_lo_buf", [P, 2, NT, P], F32R)
        TMP = sb("tmp", [P, NP])
        WH = sb("w_hi_buf", [P, KB, 520], F32R)
        WL = sb("w_lo_buf", [P, KB, 520], F32R)
        W12 = sb("w12", [P, KB, 64])
        ident = sb("ident", [P, P])
        onezero = sb("onezero", [P, NT, 2])
        ticks = sb("ticks", [P, 1])
        bcast = sb("bcast", [P, D])
        stats = sb("stats", [P, NT, 6])
        mv = sb("mean_var", [P, NT, 2])
        var = sb("var_eps", [P, NT])
        std = sb("std", [P, NT])
        rstd = sb("rstd", [P, NT])
        nmr = sb("neg_mean_rstd", [P, NT])
        small = sb("small", [P, 24, NT])
        nmax, zsum, rz, rowsum, rrow, colsum, rcol = (small[:, k, :] for k in range(7))
        cut, mass, bits, cand, keep, zkept, rkept, target = (small[:, 7 + k, :] for k in range(8))
        den, rden, ra, rowsc, colsc = (small[:, 15 + k, :] for k in range(5))
        vab = sb("vab", [P, NT, 3])
        tab = sb("tab", [P, NT, 2])
        bab = sb("bab", [P, 2])
        d1 = sb("d1", [P, KB])
        hT_H = SH[:, :, 0:KB, :]
        hT_L = SL[:, :, 0:KB, :]
        rows_in = TMP[:, 0:2 * D].rearrange("p (b d) -> p b d", b=2)
        raw = TMP[:, 0:KB * 520].rearrange("p (k n) -> p k n", k=KB)
        strip = TMP[:, :].rearrange("p (j i) -> p j i", j=NT)
        expt = [Y[:, :, :].rearrange("p t d -> p (t d)")[:, b * NP:(b + 1) * NP] for b in range(2)]

        with ExitStack() as scope:
            AT = sb("adj_t", [P, NT, NP], F32, scope)
            with ExitStack() as s1:
                F2H = sb("feat2_hi", [P, NT, D + 2], F32R, s1)
                F2L = sb("feat2_lo", [P, NT, D + 2], F32R, s1)
                SLB = sb("s_left", [P, NP], F32, s1)
                WrH = sb("w_left_hi", [P, KB, P], F32R, s1)
                WrL = sb("w_left_lo", [P, KB, P], F32R, s1)
                wlr = sb("w_left_right", [P, KB, 2], F32, s1)
                abc = sb("a_bcast", [P, 2 * D], F32, s1)
                bgc = sb("b_gcnb_bcast", [P, D], F32, s1)
                junk = sb("junk", [P, D], F32, s1)
                U1B = sb("u_rows_l1", [P, NT, D], F32, s1)
            with ExitStack() as s2:
                TH = sb("whs_t_hi", [P, 4, NP], F32R, s2)
                TL = sb("whs_t_lo", [P, 4, NP], F32R, s2)
                QH = sb("q_hi", [P, 2, KB, P], F32R, s2)
                QL = sb("q_lo", [P, 2, KB, P], F32R, s2)
                vrow = sb("vrow", [P, D], F32, s2)
            with ExitStack() as s3:
                G2H = sb("feat3_hi", [P, NT, D], F32R, s3)
                G2L = sb("feat3_lo", [P, NT, D], F32R, s3)
                UG = sb("u_rows_l3", [P, NT, D], F32, s3)
                VH = sb("v_hi", [P, KB, BANK], F32R, s3)
                VL = sb("v_lo", [P, KB, BANK], F32R, s3)
        with ExitStack() as scope:
            E = sb("e_rows", [P, NT, N], F32, scope)
            TQH = sb("qk_t_hi", [P, 2, NP], F32R, scope)
            TQL = sb("qk_t_lo", [P, 2, NP], F32R, scope)
            AQH = sb("aq_hi", [P, 2, P], F32R, scope)
            AQL = sb("aq_lo", [P, 2, P], F32R, scope)
            VQH = sb("wqk_hi", [P, KB, D], F32R, scope)
            VQL = sb("wqk_lo", [P, KB, D], F32R, scope)
            UA = sb("u_rows_a", [P, NT, D], F32, scope)
            ET2 = sb("kept_tile", [P, NP], F32, scope)
            gam = sb("gamma_bcast", [P, D], F32, scope)
            bet = sb("beta_bcast", [P, D], F32, scope)
        kept_t = [TMP[:, :], ET2[:, :]]

        SC = ctx.enter_context(nc.psum_tensor("scores", [P, 3 * BANK], F32))
        TP = ctx.enter_context(nc.psum_tensor("turned_ps", [P, 3 * BANK], F32))
        OUT = [ctx.enter_context(nc.psum_tensor(f"out{b}", [P, BANK], F32)) for b in range(2)]
        pbank = [[SC[:, 0:BANK], SC[:, BANK:2 * BANK], SC[:, 2 * BANK:]],
                 [OUT[0][:, :], OUT[1][:, :], TP[:, 2 * BANK:]]]
        TPS = TP[:, 0:NP].rearrange("p (j i) -> p j i", j=NT)

        ld_x, ld_adj, ld_small, ld_w, ld_late, stored = (sem(n) for n in (
            "ld_x", "ld_adj", "ld_small", "ld_w", "ld_late", "stored"))
        consts = sem("consts")
        d_made = sem("d_made")
        raw_ready = sem("raw_ready")
        w_hi, w_lo = sem("w_hi"), sem("w_lo")
        w12_t, w12_c, w12_m, w12_d = (sem(n) for n in ("w12_t", "w12_c", "w12_m", "w12_d"))
        var_ready, std_ready, norm_ready = sem("var_ready"), sem("std_ready"), sem("norm_ready")
        h_rows = sem("h_made")
        f_hi = sem("f_hi")
        staged = sem("rows_staged")
        turned = sem("rows_turned")
        turn_hi, turn_lo = sem("turn_hi"), sem("turn_lo")
        projected = sem("projected")
        proj_hi, proj_read = sem("proj_hi"), sem("proj_read")
        strip_hi, strip_lo = sem("strip_hi"), sem("strip_lo")
        gathered, gather_read = sem("gathered"), sem("gather_read")
        q_staged, scored, maxed, exped = (sem(n) for n in ("q_staged", "scored", "maxed", "exped"))
        strip_turned, masked, kept = sem("strip_turned"), sem("masked"), sem("kept")
        scored_z, e_raw = sem("lrelu_made"), sem("e_raw")
        gate_in, gate_out = sem("gate_in"), sem("gate_out")
        sig_out, x_l1 = sem("sig_out"), sem("x_l1")
        adj_plus = sem("adj_plus")
        pads = sem("pads")
        fin = sem("final_rows")
        dve_lead, dve_mid, dve_tail, dve_seq = (sem(n) for n in ("dve_lead", "dve_mid", "dve_tail", "dve_seq"))
        fin_a = sem("final_scaled")

        block = ctx.enter_context(nc.Block())

        def w_rows(w):
            return w.rearrange("(k p) n -> p k n", p=P)

        def cols(t):
            return bass.ds(t * P, P)

        @block.sync
        def _(sp):
            sp.dma_start(X[:, :, :], x.rearrange("(t p) d -> p t d", p=P)).then_inc(ld_x, 16)
            sp.dma_start(d1[:, :], d0.rearrange("(k p) -> p k", p=P), allow_slow_non_contiguous=True).then_inc(ld_small, 16)
            sp.dma_start(bcast[:, :], b0.rearrange("(a n) -> a n", a=1).broadcast_to([P, D])).then_inc(ld_small, 16)
            sp.dma_start(raw[:, :, 0:D], w_rows(w0)).then_inc(ld_w, 16)
            for t in range(NT):
                sp.dma_start(AT[:, t, :], adjT[t * P:(t + 1) * P, :]).then_inc(ld_adj, 16)
            sp.dma_start(abc[:, :], a_sa.broadcast_to([P, 2 * D])).then_inc(ld_small, 16)
            sp.dma_start(bgc[:, :], b_gc.rearrange("(a n) -> a n", a=1).broadcast_to([P, D])).then_inc(ld_small, 16)
            sp.dma_start(bab[:, 0:1], ba.rearrange("(a n) -> a n", a=1).broadcast_to([P, 1])).then_inc(ld_small, 16)
            sp.dma_start(bab[:, 1:2], bb.rearrange("(a n) -> a n", a=1).broadcast_to([P, 1])).then_inc(ld_small, 16)
            sp.wait_ge(turned, PJ["L0"] + NT)
            sp.dma_start(raw[:, :, 0:D], w_rows(w_gc)).then_inc(ld_w, 16)
            sp.dma_start(raw[:, :, D + 6:D + 6 + D], w_rows(w_sa)).then_inc(ld_w, 16)
            for c, (w, half) in enumerate([(wa, 0), (wb, 0), (wa, 1), (wb, 1)]):
                sp.dma_start(raw[:, :, D + c:D + c + 1],
                             w[0:1, half * D:(half + 1) * D].rearrange("a (k p) -> p k a", p=P),
                             allow_slow_non_contiguous=True).then_inc(ld_w, 16)
            sp.wait_ge(turned, PJ["L1"] + NT)
            sp.dma_start(raw[:, :, 0:64], w_rows(w1)).then_inc(ld_w, 16)
            sp.dma_start(raw[0:64, 0, 64:128], w2).then_inc(ld_w, 16)
            sp.wait_ge(w12_m, 1)
            sp.dma_start(raw[:, :, 0:2 * D], w_rows(w_l2[0])).then_inc(ld_w, 16)
            sp.wait_ge(strip_lo, GA["L2a"] + NT)
            sp.wait_ge(strip_hi, GA["L2a"] + NT)
            sp.dma_start(raw[:, :, 0:2 * D], w_rows(w_l2[1])).then_inc(ld_w, 16)
            sp.wait_ge(strip_lo, GA["L2b"] + NT)
            sp.wait_ge(strip_hi, GA["L2b"] + NT)
            sp.dma_start(raw[:, :, 0:D], w_rows(u1[0])).then_inc(ld_w, 16)
            sp.dma_start(raw[:, :, D:2 * D], w_rows(u2[0])).then_inc(ld_w, 16)
            sp.wait_ge(w_hi, WPREP["L3s"])
            sp.wait_ge(w_lo, WPREP["L3s"])
            sp.dma_start(raw[:, :, 0:D], w_rows(u1[1])).then_inc(ld_w, 16)
            sp.dma_start(raw[:, :, D:2 * D], w_rows(u2[1])).then_inc(ld_w, 16)
            sp.wait_ge(gathered, GA["L3t"] + NT)
            sp.dma_start(raw[:, :, 128:192], w_rows(w3)).then_inc(ld_w, 16)
            sp.dma_start(gam[:, :], gamma.rearrange("(a n) -> a n", a=1).broadcast_to([P, D])).then_inc(ld_late, 16)
            sp.dma_start(bet[:, :], beta.rearrange("(a n) -> a n", a=1).broadcast_to([P, D])).then_inc(ld_late, 16)
            sp.wait_ge(strip_turned, SCO["A0"] + NT)
            sp.dma_start(raw[:, :, 0:D], w_rows(u3[0])).then_inc(ld_w, 16)
            sp.dma_start(raw[:, :, D:2 * D], w_rows(u3[1])).then_inc(ld_w, 16)
            for t in range(NT):
                rows = min(P, N - t * P)
                sp.wait_ge(fin, t + 1)
                sp.dma_start(out[t * P:t * P + rows, :], Y[0:rows, t, :]).then_inc(stored, 16)
            sp.wait_ge(stored, 16 * NT)

        LD = {}
        n = 0
        for name, count in (("L0", 1), ("L1", 6), ("L1r", 2), ("L2a", 1), ("L2b", 1), ("L3s", 2), ("L3u", 2),
                            ("L3q", 1), ("L3a", 2)):
            n += 16 * count
            LD[name] = n

        @block.gpsimd
        def _(pool):
            pool.memset(ident[:, :], 0.0).then_inc(consts, 1)
            pool.memset(onezero[:, :, :], 0.0).then_inc(consts, 1)
            pool.wait_ge(consts, 2)
            pool.affine_select(out=ident[:, :], in_=ident[:, :], compare_op=ALU.not_equal, fill=1.0, base=0,
                               pattern=[[-1, P]], channel_multiplier=1).then_inc(consts, 1)
            pool.memset(onezero[:, :, 0:1], 1.0).then_inc(consts, 1)

            def lo_of_adj(g0):
                def step(t, b):
                    wait(pool, strip_hi, g0 + t + 1)
                    wait(pool, gathered, g0 + t - 1)
                    pool.tensor_tensor(SL[:, b, :, :], AT[:, :, cols(t)], SH[:, b, :, :].bitcast(F32),
                                       ALU.subtract).then_inc(strip_lo, 1)
                return step

            def lo_of_tmp(g0):
                def step(t, b):
                    wait(pool, strip_hi, g0 + t + 1)
                    wait(pool, gathered, g0 + t - 1)
                    pool.tensor_tensor(SL[:, b, :, :], strip, SH[:, b, :, :].bitcast(F32),
                                       ALU.subtract).then_inc(strip_lo, 1)
                return step

            def stage_q(s0, kb, src_hi, src_lo, dst_hi, dst_lo):
                def step(t, b):
                    wait(pool, scored, s0 + t - 1)
                    pool.tensor_copy(dst_hi(b), src_hi[:, 0:kb, cols(t)])
                    pool.tensor_copy(dst_lo(b), src_lo[:, 0:kb, cols(t)]).then_inc(q_staged, 1)
                return step

            def q_l2(s0):
                return stage_q(s0, KB, TH, TL, lambda b: QH[:, b, :, :], lambda b: QL[:, b, :, :])

            def q_a(s0):
                return stage_q(s0, 1, TQH, TQL, lambda b: AQH[:, b:b + 1, :], lambda b: AQL[:, b:b + 1, :])

            pool.wait_ge(ld_adj, 16 * NT)
            pool.wait_ge(projected, PJ["L0"] + NT)
            pipeline(pool, lo_of_adj(GA["L0"]))
            pool.wait_ge(projected, PJ["L1"] + NT)
            pipeline(pool, lo_of_adj(GA["L1b"]))
            pipeline(pool, lo_of_tmp(GA["L1a"]))
            for name in ("L2a", "L2b"):
                pool.wait_ge(proj_read, PJ[name] + NT)
                pool.wait_ge(proj_hi, PJ[name] + NT)
                pipeline(pool, q_l2(SCO[name]), lo_of_tmp(GA[name]))
            pool.wait_ge(adj_plus, 1)
            pipeline(pool, lo_of_adj(GA["L3s"]))
            pool.wait_ge(projected, PJ["L3s"] + NT)
            pipeline(pool, lo_of_adj(GA["L3t"]))
            for name, pj in (("A0", "L3q"), ("A1", "L3a")):
                pool.wait_ge(proj_read, PJ[pj] + NT)
                pool.wait_ge(proj_hi, PJ[pj] + NT)
                pipeline(pool, q_a(SCO[name]))

        @block.scalar
        def _(act):
            def split_w(name, dst, src):
                act.wait_ge(raw_ready, WPREP[name])
                act.activation(dst, src, ACT.Copy).then_inc(w_hi, 1)

            def root(name):
                act.wait_ge(var_ready, NORM[name])
                act.activation(std[:, :], var[:, :], ACT.Sqrt).then_inc(std_ready, 1)
                act.wait_ge(norm_ready, NORM[name])

            def stage_norm(p0):
                def step(t, b):
                    wait(act, turned, p0 + t - 1)
                    act.activation(rows_in[:, b:b + 1, :], X[:, bass.ds(t, 1), :], ACT.Relu,
                                   bias=nmr[:, bass.ds(t, 1)], scale=rstd[:, bass.ds(t, 1)]).then_inc(staged, 1)
                return step

            def stage_copy(p0, src):
                def step(t, b):
                    wait(act, turned, p0 + t - 1)
                    act.activation(rows_in[:, b:b + 1, :], src[:, bass.ds(t, 1), :], ACT.Copy).then_inc(staged, 1)
                return step

            def turn(p0):
                def step(t, b):
                    wait(act, turned, p0 + t + 1)
                    wait(act, projected, p0 + t - 1)
                    act.activation(hT_H[:, b, :, :].rearrange("p k i -> p (k i)"),
                                   TP[:, BANK * b:BANK * b + D], ACT.Copy).then_inc(turn_hi, 1)
                return step

            def evac(p0, *parts):
                def step(t, b):
                    wait(act, projected, p0 + t + 1)
                    for k, part in enumerate(parts):
                        ins = part(t, b)
                    ins.then_inc(proj_hi, 1)
                return step

            def copy_part(dst, bank, c0, n, scale=None):
                def part(t, b):
                    if scale is None:
                        return act.activation(dst(t), pbank[b][bank][:, c0:c0 + n], ACT.Copy)
                    return act.activation(dst(t), pbank[b][bank][:, c0:c0 + n], ACT.Copy,
                                          scale=scale[:, bass.ds(t, 1)])
                return part

            def hi_of_adj(g0):
                def step(t, b):
                    wait(act, gathered, g0 + t - 1)
                    act.activation(SH[:, b, :, :], AT[:, :, cols(t)], ACT.Copy).then_inc(strip_hi, 1)
                return step

            def hi_of_tmp(g0, m0):
                def step(t, b):
                    wait(act, masked, m0 + t + 1)
                    wait(act, gathered, g0 + t - 1)
                    act.activation(SH[:, b, :, :], strip, ACT.Copy).then_inc(strip_hi, 1)
                return step

            def exp_l2(s0):
                def step(t, b):
                    wait(act, maxed, s0 + t + 1)
                    wait(act, strip_turned, s0 + t - 1)
                    act.activation(expt[b][:, 0:N], SC[:, 0:N], ACT.Exp, bias=nmax[:, bass.ds(t, 1)],
                                   accum_out=zsum[:, bass.ds(t, 1)]).then_inc(exped, 1)
                return step

            fh = lambda n: (lambda t: FH[:, t, 0:n] if isinstance(t, int) else FH[:, bass.ds(t, 1), 0:n])

            split_w("L0", WH[:, :, 0:2 * D], raw[:, :, 0:2 * D])
            act.wait_ge(ld_x, 16)
            root("L0")
            act.wait_ge(w_lo, WPREP["L0"])
            pipeline(act, stage_norm(PJ["L0"]), turn(PJ["L0"]), evac(
                PJ["L0"], copy_part(lambda t: FH[:, bass.ds(t, 1), 0:D], 0, D, D)))
            act.wait_ge(projected, PJ["L0"] + NT)
            split_w("L1", WH[:, :, 0:D + 6 + D], raw[:, :, 0:D + 6 + D])
            act.activation(WrH[:, :, :], wlr[:, :, 0:1].broadcast_to([P, KB, P]), ACT.Copy).then_inc(w_hi, 1)
            act.activation(F2H[:, :, D:D + 2], onezero[:, :, :], ACT.Copy)
            act.wait_ge(ld_adj, 16 * NT)
            pipeline(act, hi_of_adj(GA["L0"]))
            act.wait_ge(gathered, GA["L0"] + NT)
            root("L1")
            act.wait_ge(w_lo, WPREP["L1r"])
            pipeline(act, stage_norm(PJ["L1"]), turn(PJ["L1"]), evac(
                PJ["L1"], copy_part(lambda t: FH[:, bass.ds(t, 1), 0:D + 2], 0, 0, D + 2),
                copy_part(lambda t: F2H[:, bass.ds(t, 1), 0:D], 1, 0, D),
                copy_part(lambda t: SLB[:, cols(t)], 2, 0, P)))
            act.wait_ge(projected, PJ["L1"] + NT)
            pipeline(act, hi_of_adj(GA["L1b"]))
            split_w("L2a", WH[:, :, 0:2 * D], raw[:, :, 0:2 * D])
            act.wait_ge(gate_in, 1)
            act.activation(tab[:, :, :], tab[:, :, :], ACT.Sigmoid).then_inc(gate_out, 1)

            def exp_l1(t, b):
                wait(act, scored_z, t + 1)
                act.activation(TMP[:, :], TMP[:, :], ACT.Exp, scale=-1.0).then_inc(e_raw, 1)

            def l1a(t, b):
                exp_l1(t, b)
                hi_of_tmp(GA["L1a"], MSK["L1a"])(t, b)

            pipeline(act, l1a)

            def sig(t):
                act.wait_ge(gather_read, GA["L1a"] + NT)
                act.activation(U1B[:, bass.ds(t, 1), :], U1B[:, bass.ds(t, 1), :], ACT.Sigmoid).then_inc(sig_out, 1)

            each_tile(act, sig)
            root("L2")
            act.wait_ge(x_l1, 1)

            def norm_h(t):
                act.activation(H[:, bass.ds(t, 1), :], X[:, bass.ds(t, 1), :], ACT.Relu, bias=nmr[:, bass.ds(t, 1)],
                               scale=rstd[:, bass.ds(t, 1)]).then_inc(h_rows, 1)

            each_tile(act, norm_h)
            act.wait_ge(h_rows, NT)
            for name in ("L2a", "L2b"):
                if name == "L2b":
                    split_w("L2b", WH[:, :, 0:2 * D], raw[:, :, 0:2 * D])
                    act.wait_ge(gather_read, GA["L2a"] + NT)
                act.wait_ge(w_lo, WPREP[name])
                act.wait_ge(gathered, GA[name])
                pipeline(act, stage_copy(PJ[name], H), turn(PJ[name]), evac(
                    PJ[name], copy_part(lambda t: FH[:, bass.ds(t, 1), 0:D], 0, 0, D),
                    lambda t, b: act.activation(TH[:, :, cols(t)], pbank[b][1].rearrange("p (k i) -> p k i", k=4),
                                                ACT.Copy)))
                act.wait_ge(pads, 1)
                act.wait_ge(projected, PJ[name] + NT)
                pipeline(act, exp_l2(SCO[name]), hi_of_tmp(GA[name], MSK[name]))
            act.wait_ge(gathered, GA["L2b"] + NT)
            root("L3")

            def norm_h3(t):
                norm_h(t)
                act.wait_ge(h_rows, t + (NT + 1))
                act.activation(FH[:, bass.ds(t, 1), 0:D], H[:, bass.ds(t, 1), :], ACT.Copy).then_inc(f_hi, 1)

            act.activation(FH[:, :, D:D + 2], onezero[:, :, :], ACT.Copy)
            each_tile(act, norm_h3)
            act.wait_ge(adj_plus, 1)
            pipeline(act, hi_of_adj(GA["L3s"]))
            split_w("L3s", WH[:, :, 0:2 * D], raw[:, :, 0:2 * D])
            split_w("L3u", VH[:, :, :], raw[:, :, 0:2 * D])
            act.wait_ge(gather_read, GA["L3s"] + NT)
            act.wait_ge(gate_in, 2)
            act.wait_ge(w_lo, WPREP["L3u"])
            pipeline(act, stage_copy(PJ["L3s"], UG), turn(PJ["L3s"]), evac(
                PJ["L3s"], copy_part(lambda t: FH[:, bass.ds(t, 1), 0:D], 1, 0, D, rrow),
                copy_part(lambda t: G2H[:, bass.ds(t, 1), :], 1, D, D, rcol)))
            act.wait_ge(projected, PJ["L3s"] + NT)
            pipeline(act, hi_of_adj(GA["L3t"]))
            split_w("L3q", VQH[:, :, :], raw[:, :, 0:D])
            act.wait_ge(gather_read, GA["L3t"] + NT)
            act.wait_ge(w_lo, WPREP["L3q"])
            pipeline(act, stage_copy(PJ["L3q"], H), turn(PJ["L3q"]), evac(
                PJ["L3q"], lambda t, b: act.activation(FH[:, bass.ds(t, 1), 0:D], H[:, bass.ds(t, 1), :], ACT.Copy),
                lambda t, b: act.activation(TQH[:, :, cols(t)],
                                            pbank[b][0][:, 0:D].rearrange("p (k i) -> p k i", k=2), ACT.Copy)))

            def exp_a(s0):
                def step(t, b):
                    wait(act, maxed, s0 + t + 1)
                    act.activation(E[:, bass.ds(t, 1), :], [SC, TP][b][:, 0:N], ACT.Exp, bias=nmax[:, bass.ds(t, 1)],
                                   accum_out=zsum[:, bass.ds(t, 1)]).then_inc(exped, 1)
                return step

            def hi_of_turned(g0, s0):
                def step(t, b):
                    wait(act, strip_turned, s0 + t + 1)
                    wait(act, gathered, g0 + t - 1)
                    act.activation(SH[:, b, :, :], TPS, ACT.Copy).then_inc(strip_hi, 1)
                return step

            pipeline(act, exp_a(SCO["A0"]))
            act.wait_ge(projected, PJ["L3q"] + NT)
            pipeline(act, hi_of_turned(GA["A0"], SCO["A0"]))
            split_w("L3a", WH[:, :, 0:2 * D], raw[:, :, 0:2 * D])
            act.wait_ge(gather_read, GA["A0"] + NT)
            act.wait_ge(w_lo, WPREP["L3a"])
            pipeline(act, stage_copy(PJ["L3a"], UA), turn(PJ["L3a"]), evac(
                PJ["L3a"], copy_part(lambda t: FH[:, bass.ds(t, 1), 0:D], 0, D, D),
                lambda t, b: act.activation(TQH[:, :, cols(t)],
                                            pbank[b][1][:, 0:D].rearrange("p (k i) -> p k i", k=2), ACT.Copy)))
            pipeline(act, exp_a(SCO["A1"]))
            act.wait_ge(projected, PJ["L3a"] + NT)
            pipeline(act, hi_of_turned(GA["A1"], SCO["A1"]))
            act.wait_ge(var_ready, NORM["end"])
            act.activation(std[:, :], var[:, :], ACT.Sqrt).then_inc(std_ready, 1)
            act.wait_ge(norm_ready, NORM["end"])

            def last(t):
                act.activation(Y[:, bass.ds(t, 1), :], Y[:, bass.ds(t, 1), :], ACT.Identity,
                               bias=nmr[:, bass.ds(t, 1)], scale=rstd[:, bass.ds(t, 1)]).then_inc(fin_a, 1)

            each_tile(act, last)

        @block.tensor
        def _(pe):
            def turn(p0):
                def step(t, b):
                    wait(pe, staged, p0 + t + 1)
                    wait(pe, turn_hi, p0 + t - 1)
                    wait(pe, turn_lo, p0 + t - 1)
                    for k in range(KB):
                        ins = pe.transpose(TP[:, BANK * b + k * P:BANK * b + (k + 1) * P],
                                           rows_in[:, b, k * P:(k + 1) * P], ident[:, :])
                    ins.then_inc(turned, 1)
                return step

            def rows_times(b, dst, wh, wl, c0, n):
                terms = [(hT_H, wh), (hT_L, wh), (hT_H, wl)]
                for m, (left, right) in enumerate(terms):
                    for k in range(KB):
                        ins = pe.matmul(dst, left[:, b, k, :], right[:, k, c0:c0 + n], start=(m == 0 and k == 0),
                                        stop=(m == 2 and k == KB - 1))
                return ins

            def rows_times_turned(b, dst, wh, wl, c0):
                terms = [(wh, hT_H), (wh, hT_L), (wl, hT_H)]
                for m, (left, right) in enumerate(terms):
                    for k in range(KB):
                        ins = pe.matmul(dst, left[:, k, c0:c0 + P], right[:, b, k, :], start=(m == 0 and k == 0),
                                        stop=(m == 2 and k == KB - 1))
                return ins

            def project(p0, body):
                def step(t, b):
                    wait(pe, turn_lo, p0 + t + 1)
                    wait(pe, turn_hi, p0 + t + 1)
                    wait(pe, proj_read, p0 + t - 1)
                    wait(pe, proj_hi, p0 + t - 1)
                    body(b).then_inc(projected, 1)
                return step

            def gather(g0, *groups):
                def step(t, b):
                    wait(pe, strip_hi, g0 + t + 1)
                    wait(pe, strip_lo, g0 + t + 1)
                    wait(pe, gather_read, g0 + t - 1)
                    for c0, fh, fl, n in groups:
                        for m, (left, right) in enumerate([(SH, fh), (SL, fh), (SH, fl)]):
                            for j in range(NT):
                                ins = pe.matmul(OUT[b][:, c0:c0 + n], left[:, b, j, :], right[:, j, 0:n],
                                                start=(m == 0 and j == 0), stop=(m == 2 and j == NT - 1))
                    ins.then_inc(gathered, 1)
                return step

            def scores_l2(s0):
                def step(t, b):
                    wait(pe, q_staged, s0 + t + 1)
                    wait(pe, exped, s0 + t)
                    for c, n in CHUNKS:
                        for m, (q, k2) in enumerate([(QH, TH), (QL, TH), (QH, TL)]):
                            for k in range(KB):
                                ins = pe.matmul(SC[:, c:c + n], q[:, b, k, :], k2[:, KB + k, c:c + n],
                                                start=(m == 0 and k == 0), stop=(m == 2 and k == KB - 1))
                    ins.then_inc(scored, 1)
                return step

            def turn_l2(s0, m0):
                def step(t, b):
                    wait(pe, exped, s0 + t + 1)
                    wait(pe, masked, m0 + t)
                    for j in range(NT):
                        ins = pe.transpose(TP[:, j * P:(j + 1) * P], expt[b][:, j * P:(j + 1) * P], ident[:, :])
                    ins.then_inc(strip_turned, 1)
                return step

            def scores_a(s0):
                def step(t, b):
                    wait(pe, q_staged, s0 + t + 1)
                    wait(pe, exped, s0 + t - 1)
                    for c, n in CHUNKS:
                        for m, (q, k2) in enumerate([(AQH, TQH), (AQL, TQH), (AQH, TQL)]):
                            ins = pe.matmul([SC, TP][b][:, c:c + n], q[:, b, :], k2[:, 1, c:c + n], start=(m == 0),
                                            stop=(m == 2))
                    ins.then_inc(scored, 1)
                return step

            def turn_a(s0, k0, g0):
                def step(t, b):
                    wait(pe, kept, k0 + t + 1)
                    wait(pe, strip_hi, g0 + t)
                    wait(pe, strip_lo, g0 + t)
                    for j in range(NT):
                        ins = pe.transpose(TP[:, j * P:(j + 1) * P], kept_t[b][:, j * P:(j + 1) * P], ident[:, :])
                    ins.then_inc(strip_turned, 1)
                return step

            one = (0, FH, FL, D)
            pe.wait_ge(consts, 4)
            pe.wait_ge(w_lo, WPREP["L0"])
            pipeline(pe, turn(PJ["L0"]), project(PJ["L0"], lambda b: rows_times(b, pbank[b][0], WH, WL, 0, 2 * D)))
            pe.wait_ge(proj_read, PJ["L0"] + NT)
            pe.wait_ge(proj_hi, PJ["L0"] + NT)
            pipeline(pe, gather(GA["L0"], one))
            pe.wait_ge(w_lo, WPREP["L1r"])
            pe.wait_ge(gather_read, GA["L0"] + NT)

            def proj_l1(b):
                rows_times(b, pbank[b][0][:, 0:D + 6], WH, WL, 0, D + 6)
                rows_times(b, pbank[b][1][:, 0:D], WH, WL, D + 6, D)
                return rows_times_turned(b, pbank[b][2][:, 0:P], WrH, WrL, 0)

            pipeline(pe, turn(PJ["L1"]), project(PJ["L1"], proj_l1))
            pe.wait_ge(proj_read, PJ["L1"] + NT)
            pe.wait_ge(proj_hi, PJ["L1"] + NT)
            pe.wait_ge(raw_ready, WPREP["L1r"] + 0)
            pe.wait_ge(ld_w, LD["L1r"])
            for k in range(KB):
                ins = pe.transpose(TP[0:64, k * P:(k + 1) * P], raw[:, k, 0:64], ident[:, :])
            ins.then_inc(w12_t, 1)
            pe.wait_ge(w12_c, 1)
            for k in range(KB):
                ins = pe.matmul(TP[:, BANK + k * 64:BANK + (k + 1) * 64], raw[0:64, 1, 128 + k * P:128 + (k + 1) * P],
                                raw[0:64, 0, 64:128], start=True, stop=True)
            ins.then_inc(w12_m, 1)
            pipeline(pe, gather(GA["L1b"], (0, FH, FL, D + 2)))
            pipeline(pe, gather(GA["L1a"], (0, F2H, F2L, D + 2)))

            def proj_l2(b):
                rows_times(b, pbank[b][0][:, 0:D], WH, WL, 0, D)
                for k in range(4):
                    ins = rows_times_turned(b, pbank[b][1][:, k * P:(k + 1) * P], WH, WL, k * P)
                return ins

            for name in ("L2a", "L2b"):
                pe.wait_ge(w_lo, WPREP[name])
                pe.wait_ge(w12_d, 1)
                pe.wait_ge(gather_read, GA[name])
                pe.wait_ge(masked, MSK[name])
                pe.wait_ge(exped, SCO[name]) if name != "L2a" else None
                pipeline(pe, turn(PJ[name]), project(PJ[name], proj_l2))
                pe.wait_ge(proj_read, PJ[name] + NT)
                pe.wait_ge(proj_hi, PJ[name] + NT)
                pipeline(pe, scores_l2(SCO[name]), turn_l2(SCO[name], MSK[name]), gather(GA[name], one))
            pe.wait_ge(adj_plus, 2)
            pipeline(pe, gather(GA["L3s"], (0, FH, FL, D + 2)))
            pe.wait_ge(w_lo, WPREP["L3u"])
            pe.wait_ge(gather_read, GA["L3s"] + NT)

            def proj_l3s(b):
                rows_times(b, pbank[b][0], WH, WL, 0, 2 * D)
                return rows_times(b, pbank[b][1], VH, VL, 0, 2 * D)

            pipeline(pe, turn(PJ["L3s"]), project(PJ["L3s"], proj_l3s))
            pe.wait_ge(proj_read, PJ["L3s"] + NT)
            pe.wait_ge(proj_hi, PJ["L3s"] + NT)
            pipeline(pe, gather(GA["L3t"], one, (D, G2H, G2L, D)))
            pe.wait_ge(w_lo, WPREP["L3q"])
            pe.wait_ge(gather_read, GA["L3t"] + NT)

            def proj_qk(b, bank):
                rows_times_turned(b, pbank[b][bank][:, 0:P], VQH, VQL, 0)
                return rows_times_turned(b, pbank[b][bank][:, P:2 * P], VQH, VQL, P)

            def proj_l3a(b):
                rows_times(b, pbank[b][0], WH, WL, 0, 2 * D)
                return proj_qk(b, 1)

            pipeline(pe, turn(PJ["L3q"]), project(PJ["L3q"], lambda b: proj_qk(b, 0)))
            for name, pj in (("A0", "L3q"), ("A1", "L3a")):
                pe.wait_ge(proj_read, PJ[pj] + NT)
                pe.wait_ge(proj_hi, PJ[pj] + NT)
                pipeline(pe, scores_a(SCO[name]))
                pipeline(pe, turn_a(SCO[name], KEEP[name], GA[name]), gather(GA[name], one))
                if name == "A0":
                    pe.wait_ge(w_lo, WPREP["L3a"])
                    pe.wait_ge(gather_read, GA["A0"] + NT)
                    pipeline(pe, turn(PJ["L3a"]), project(PJ["L3a"], proj_l3a))

        @block.vector
        def _(dve):
            seq = [0]

            def then(ins):
                seq[0] += 1
                ins.then_inc(dve_seq, 1)
                dve.wait_ge(dve_seq, seq[0])

            base = {}

            def chain(s, per_tile):
                b0_ = base.get(id(s), 0)
                base[id(s)] = b0_ + NT * per_tile

                def link(t, k, ins):
                    ins.then_inc(s, 1)
                    dve.wait_ge(s, t * per_tile + (b0_ + k))
                return link

            def norm_stats(name, src):
                for t in range(NT):
                    ins = dve.bn_stats(stats[:, t, :], src[:, t, :])
                then(ins)
                for t in range(NT):
                    ins = dve.bn_aggr(mv[:, t, :], stats[:, t, :])
                then(ins)
                dve.tensor_scalar(var[:, :], mv[:, :, 1], LN_EPS, None, ALU.add).then_inc(var_ready, 1)
                dve.wait_ge(std_ready, NORM[name])
                then(dve.reciprocal(rstd[:, :], std[:, :]))
                dve.scalar_tensor_tensor(out=nmr[:, :], in0=mv[:, :, 0], scalar=-1.0, in1=rstd[:, :], op0=ALU.mult,
                                         op1=ALU.mult).then_inc(norm_ready, 1)

            def split_w(name, dst, src, hi):
                dve.wait_ge(w_hi, WPREP[name])
                dve.tensor_tensor(dst, src, hi.bitcast(F32), ALU.subtract).then_inc(w_lo, 1)

            def turn(p0):
                def step(t, b):
                    wait(dve, turn_hi, p0 + t + 1)
                    wait(dve, projected, p0 + t - 1)
                    dve.tensor_tensor(hT_L[:, b, :, :].rearrange("p k i -> p (k i)"), TP[:, BANK * b:BANK * b + D],
                                      hT_H[:, b, :, :].rearrange("p k i -> p (k i)").bitcast(F32),
                                      ALU.subtract).then_inc(turn_lo, 1)
                return step

            def tick():
                return dve.memset(ticks[:, 0:1], 0.0)

            def mark(s):
                tick().then_inc(s, 1)

            def nothing(t, b):
                pass

            def evac(p0, body):
                def step(t, b):
                    wait(dve, projected, p0 + t + 1)
                    wait(dve, proj_hi, p0 + t + 1)
                    body(t, b).then_inc(proj_read, 1)
                return step

            def lo(dst, src, hi):
                return dve.tensor_tensor(dst, src, hi.bitcast(F32), ALU.subtract)

            def read(g0, body):
                def step(t, b):
                    wait(dve, gathered, g0 + t + 1)
                    body(t, b).then_inc(gather_read, 1)
                return step

            one = lambda a, t: a[:, bass.ds(t, 1)]
            row = lambda a, t, n=D: a[:, bass.ds(t, 1), 0:n]

            dve.wait_ge(ld_small, 16 * 6)
            then(dve.tensor_scalar(d1[:, :], d1[:, :], 1.0, None, ALU.add))
            dve.wait_ge(ld_w, LD["L0"])
            for k in range(KB):
                ins = dve.tensor_scalar(raw[:, k, D:2 * D], raw[:, k, 0:D], d1[:, k:k + 1], None, ALU.mult)
            ins.then_inc(raw_ready, 1)
            split_w("L0", WL[:, :, 0:2 * D], raw[:, :, 0:2 * D], WH[:, :, 0:2 * D])
            dve.wait_ge(ld_x, 16)
            norm_stats("L0", X)
            link0 = chain(dve_tail, 1)

            def evac_l0(t, b):
                lo(row(FL, t), pbank[b][0][:, D:2 * D], row(FH, t))
                link0(t, 1, dve.tensor_tensor(row(X, t), row(X, t), pbank[b][0][:, 0:D], ALU.add))
                return dve.tensor_tensor(row(X, t), row(X, t), bcast[:, :], ALU.add)

            pipeline(dve, nothing, turn(PJ["L0"]), evac(PJ["L0"], evac_l0))
            dve.wait_ge(proj_read, PJ["L0"] + NT)
            dve.wait_ge(ld_w, LD["L1"])
            for k in range(KB):
                for side in range(2):
                    then(dve.tensor_tensor_reduce(out=junk[:, :], in0=raw[:, k, D + 6:D + 6 + D],
                                                  in1=abc[:, side * D:(side + 1) * D], scale=1.0, scalar=0.0,
                                                  op0=ALU.mult, op1=ALU.add, accum_out=wlr[:, k, side:side + 1]))
            dve.tensor_copy(raw[:, :, D + 4:D + 5], wlr[:, :, 1:2])
            dve.memset(raw[:, :, D + 5:D + 6], 0.0).then_inc(raw_ready, 2)
            split_w("L1", WL[:, :, 0:D + 6 + D], raw[:, :, 0:D + 6 + D], WH[:, :, 0:D + 6 + D])
            split_w("L1r", WrL[:, :, :], wlr[:, :, 0:1].broadcast_to([P, KB, P]), WrH[:, :, :])
            dve.tensor_scalar(F2L[:, :, D:D + 2], onezero[:, :, :], 0.0, None, ALU.mult)
            pipeline(dve, read(GA["L0"], lambda t, b: dve.tensor_tensor(row(X, t), row(X, t), OUT[b][:, 0:D],
                                                                        ALU.subtract)))
            dve.wait_ge(gather_read, GA["L0"] + NT)
            norm_stats("L1", X)

            def evac_l1(t, b):
                lo(row(FL, t, D + 2), pbank[b][0][:, 0:D + 2], row(FH, t, D + 2))
                lo(row(F2L, t), pbank[b][1][:, 0:D], row(F2H, t))
                return dve.tensor_copy(vab[:, bass.ds(t, 1), :], pbank[b][0][:, D + 2:D + 5])

            pipeline(dve, nothing, turn(PJ["L1"]), evac(PJ["L1"], evac_l1))
            dve.wait_ge(w12_t, 1)
            dve.tensor_copy(raw[0:64, 1, 128:128 + D], TP[0:64, 0:D]).then_inc(w12_c, 1)
            dve.wait_ge(w12_m, 1)
            dve.tensor_copy(W12[:, :, :], TP[:, BANK:BANK + 128].rearrange("p (k n) -> p k n", k=KB)).then_inc(w12_d, 1)

            def read_l1b(t, b):
                dve.tensor_copy(tab[:, bass.ds(t, 1), :], OUT[b][:, D:D + 2])
                return dve.tensor_tensor(row(U1B, t), OUT[b][:, 0:D], bgc[:, :], ALU.add)

            pipeline(dve, read(GA["L1b"], read_l1b))
            dve.wait_ge(gather_read, GA["L1b"] + NT)
            then(dve.tensor_tensor(tab[:, :, :], tab[:, :, :], vab[:, :, 0:2], ALU.add))
            for c in range(2):
                ins = dve.tensor_scalar(tab[:, :, c:c + 1], tab[:, :, c:c + 1], bab[:, c:c + 1], None, ALU.add)
            ins.then_inc(gate_in, 1)
            dve.wait_ge(ld_w, LD["L2a"])
            mark(raw_ready)
            split_w("L2a", WL[:, :, 0:2 * D], raw[:, :, 0:2 * D], WH[:, :, 0:2 * D])
            dve.wait_ge(w_lo, WPREP["L2a"])
            dve.wait_ge(gate_out, 1)
            link = chain(dve_lead, 2)
            link_t = chain(dve_tail, 4)

            def e_l1(t, b):
                wait(dve, strip_hi, GA["L1a"] + t)
                wait(dve, strip_lo, GA["L1a"] + t)
                link(t, 1, dve.tensor_tensor(
                    strip, SLB[:, cols(t)].rearrange("p (a i) -> p a i", a=1).broadcast_to([P, NT, P]),
                    vab[:, :, 2:3].broadcast_to([P, NT, P]), ALU.add))
                dve.scalar_tensor_tensor(out=TMP[:, :], in0=TMP[:, :], scalar=SLOPE, in1=TMP[:, :], op0=ALU.mult,
                                         op1=ALU.max).then_inc(scored_z, 1)
                wait(dve, e_raw, t + 1)
                link(t, 2, dve.scalar_tensor_tensor(out=strip, in0=AT[:, :, cols(t)], scalar=0.0, in1=strip,
                                                    op0=ALU.not_equal, op1=ALU.mult))
                mark(masked)

            def read_l1a(t, b):
                link_t(t, 1, dve.tensor_scalar(one(den, t), OUT[b][:, D:D + 1], 1e-5, None, ALU.add))
                link_t(t, 2, dve.reciprocal(one(rden, t), one(den, t)))
                link_t(t, 3, dve.tensor_tensor(one(ra, t), one(rden, t), tab[:, bass.ds(t, 1), 0], ALU.mult))
                link_t(t, 4, dve.tensor_scalar(row(U1B, t), row(U1B, t), tab[:, bass.ds(t, 1), 1], None, ALU.mult))
                return dve.scalar_tensor_tensor(out=row(U1B, t), in0=OUT[b][:, 0:D], scalar=one(ra, t), in1=row(U1B, t),
                                                op0=ALU.mult, op1=ALU.add)

            pipeline(dve, e_l1, read(GA["L1a"], read_l1a))

            link_x = chain(dve_mid, 1)

            def add_l1(t):
                dve.wait_ge(sig_out, t + 1)
                link_x(t, 1, dve.tensor_tensor(row(X, t), row(X, t), row(U1B, t), ALU.add))

            each_tile(dve, add_l1)
            norm_stats("L2", X)
            for b in range(2):
                ins = dve.memset(expt[b][:, N:NP], 0.0)
            ins.then_inc(pads, 1)
            mark(x_l1)

            for name in ("L2a", "L2b"):
                last = name == "L2b"
                if last:
                    dve.wait_ge(gather_read, GA["L2a"] + NT)
                    dve.wait_ge(ld_w, LD["L2b"])
                    mark(raw_ready)
                    split_w("L2b", WL[:, :, 0:2 * D], raw[:, :, 0:2 * D], WH[:, :, 0:2 * D])

                def evac_l2(t, b):
                    lo(row(FL, t), pbank[b][0][:, 0:D], row(FH, t))
                    return lo(TL[:, :, cols(t)], pbank[b][1].rearrange("p (k i) -> p k i", k=4), TH[:, :, cols(t)])

                pipeline(dve, nothing, turn(PJ[name]), evac(PJ[name], evac_l2))

                def top(t, b):
                    wait(dve, scored, SCO[name] + t + 1)
                    dve.tensor_reduce(one(nmax, t), SC[:, 0:N], AX.X, ALU.max, negate=True).then_inc(maxed, 1)

                def mask(t, b):
                    wait(dve, strip_turned, SCO[name] + t + 1)
                    wait(dve, strip_hi, GA[name] + t)
                    wait(dve, strip_lo, GA[name] + t)
                    dve.tensor_tensor(strip, TPS, AT[:, :, cols(t)], ALU.mult).then_inc(masked, 1)

                link2 = chain(dve_tail, 3 if last else 2)

                def read_l2(t, b):
                    wait(dve, exped, SCO[name] + t + 1)
                    link2(t, 1, dve.reciprocal(one(rz, t), one(zsum, t)))
                    link2(t, 2, dve.scalar_tensor_tensor(out=vrow[:, :], in0=OUT[b][:, 0:D], scalar=one(rz, t),
                                                         in1=row(H, t), op0=ALU.mult, op1=ALU.add))
                    ins = dve.scalar_tensor_tensor(out=row(H, t), in0=vrow[:, :], scalar=SLOPE, in1=vrow[:, :],
                                                   op0=ALU.mult, op1=ALU.max)
                    if last:
                        link2(t, 3, ins)
                        ins = dve.tensor_tensor(row(X, t), row(X, t), row(H, t), ALU.add)
                    return ins

                pipeline(dve, top, mask, read(GA[name], read_l2))
            dve.wait_ge(gather_read, GA["L2b"] + NT)
            norm_stats("L3", X)
            link_i = chain(dve_mid, 1)
            for t in range(NT):
                then(dve.tensor_tensor(AT[:, t, t * P:(t + 1) * P], AT[:, t, t * P:(t + 1) * P], ident[:, :], ALU.add))
            dve.tensor_scalar(FL[:, :, D:D + 2], onezero[:, :, :], 0.0, None, ALU.mult).then_inc(adj_plus, 1)

            def lo_h(t):
                dve.wait_ge(f_hi, t + 1)
                link_i(t, 1, lo(row(FL, t), row(H, t), row(FH, t)))

            each_tile(dve, lo_h)
            mark(adj_plus)
            then(dve.tensor_reduce(colsum, AT[:, :, :], AX.X, ALU.add))
            then(dve.tensor_scalar(colsum, colsum, 1e-12, None, ALU.max))
            then(dve.reciprocal(rcol, colsum))
            dve.wait_ge(ld_w, LD["L3s"])
            mark(raw_ready)

            def read_l3s(t, b):
                dve.tensor_copy(one(rowsum, t), OUT[b][:, D:D + 1])
                return dve.tensor_copy(row(UG, t), OUT[b][:, 0:D])

            pipeline(dve, read(GA["L3s"], read_l3s))
            dve.wait_ge(gather_read, GA["L3s"] + NT)
            then(dve.tensor_scalar(rowsum, rowsum, 1e-12, None, ALU.max))
            dve.reciprocal(rrow, rowsum).then_inc(gate_in, 1)
            split_w("L3s", WL[:, :, 0:2 * D], raw[:, :, 0:2 * D], WH[:, :, 0:2 * D])
            dve.wait_ge(ld_w, LD["L3u"])
            dve.wait_ge(gate_in, 2)
            mark(raw_ready)
            split_w("L3u", VL[:, :, :], raw[:, :, 0:2 * D], VH[:, :, :])
            link_s = chain(dve_tail, 1)

            def evac_l3s(t, b):
                dve.scalar_tensor_tensor(out=row(FL, t), in0=pbank[b][1][:, 0:D], scalar=one(rrow, t),
                                         in1=row(FH, t).bitcast(F32), op0=ALU.mult, op1=ALU.subtract)
                dve.scalar_tensor_tensor(out=row(G2L, t), in0=pbank[b][1][:, D:2 * D], scalar=one(rcol, t),
                                         in1=row(G2H, t).bitcast(F32), op0=ALU.mult, op1=ALU.subtract)
                link_s(t, 1, dve.scalar_tensor_tensor(out=row(Y, t), in0=pbank[b][0][:, 0:D], scalar=one(rrow, t),
                                                      in1=row(H, t), op0=ALU.mult, op1=ALU.add))
                return dve.scalar_tensor_tensor(out=row(Y, t), in0=pbank[b][0][:, D:2 * D], scalar=one(rcol, t),
                                                in1=row(Y, t), op0=ALU.mult, op1=ALU.add)

            pipeline(dve, nothing, turn(PJ["L3s"]), evac(PJ["L3s"], evac_l3s))
            dve.wait_ge(proj_read, PJ["L3s"] + NT)
            link_t3 = chain(dve_tail, 1)

            def read_l3t(t, b):
                link_t3(t, 1, dve.scalar_tensor_tensor(out=row(Y, t), in0=OUT[b][:, 0:D], scalar=one(rrow, t),
                                                       in1=row(Y, t), op0=ALU.mult, op1=ALU.add))
                return dve.scalar_tensor_tensor(out=row(Y, t), in0=OUT[b][:, D:2 * D], scalar=one(rcol, t),
                                                in1=row(Y, t), op0=ALU.mult, op1=ALU.add)

            pipeline(dve, read(GA["L3t"], read_l3t))
            dve.wait_ge(gather_read, GA["L3t"] + NT)
            dve.wait_ge(ld_w, LD["L3q"])
            dve.tensor_copy(raw[:, :, 0:64], W12[:, :, :])
            dve.memset(raw[:, :, 64:128], 0.0)
            dve.memset(raw[:, :, 192:256], 0.0).then_inc(raw_ready, 1)
            split_w("L3q", VQL[:, :, :], raw[:, :, 0:D], VQH[:, :, :])

            def evac_l3q(t, b):
                lo(row(FL, t), row(H, t), row(FH, t))
                return lo(TQL[:, :, cols(t)], pbank[b][0][:, 0:D].rearrange("p (k i) -> p k i", k=2), TQH[:, :, cols(t)])

            pipeline(dve, nothing, turn(PJ["L3q"]), evac(PJ["L3q"], evac_l3q))

            for name in ("A0", "A1"):
                def top_a(t, b):
                    wait(dve, scored, SCO[name] + t + 1)
                    dve.tensor_reduce(one(nmax, t), [SC, TP][b][:, 0:N], AX.X, ALU.max, negate=True).then_inc(maxed, 1)

                pipeline(dve, top_a)
                dve.wait_ge(exped, SCO[name] + NT)
                dve.tensor_scalar(target, zsum, P_NUC, None, ALU.mult)
                dve.memset(cut.bitcast(U32), BASE_BITS)
                for kt in kept_t:
                    ins = dve.memset(kt[:, N:NP], 0.0)
                then(ins)
                then(dve.memset(bits.bitcast(U32), 1 << TOP_BIT))
                loop_steps = NT + 5
                base_s = seq[0]
                with dve.Fori(0, SEARCH_BITS, 1) as i:
                    def counted(ins):
                        ins.then_inc(dve_seq, 1)

                    def reached(k):
                        dve.wait_ge(dve_seq, i * loop_steps + (base_s + k))

                    counted(dve.tensor_tensor(cand.bitcast(U32), cut.bitcast(U32), bits.bitcast(U32), ALU.bitwise_or))
                    reached(1)
                    for t in range(NT):
                        if t >= 2:
                            reached(t)
                        counted(dve.scalar_tensor_tensor(out=kept_t[t % 2][:, 0:N], in0=E[:, t, :],
                                                         scalar=cand[:, t:t + 1], in1=E[:, t, :], op0=ALU.is_gt,
                                                         op1=ALU.mult, accum_out=mass[:, t:t + 1]))
                    counted(dve.tensor_single_scalar(bits.bitcast(U32), bits.bitcast(U32), 1,
                                                     ALU.logical_shift_right))
                    reached(NT + 1)
                    counted(dve.tensor_tensor(keep, mass, target, ALU.is_ge))
                    reached(NT + 3)
                    counted(dve.tensor_tensor(cand, cand, keep, ALU.mult))
                    reached(NT + 4)
                    counted(dve.tensor_tensor(cut, cut, cand, ALU.max))
                    reached(NT + 5)
                seq[0] += loop_steps * SEARCH_BITS

                def keep_e(t, b):
                    wait(dve, strip_turned, SCO[name] + t - 1)
                    dve.scalar_tensor_tensor(out=kept_t[b][:, 0:N], in0=E[:, bass.ds(t, 1), :], scalar=one(cut, t),
                                             in1=E[:, bass.ds(t, 1), :], op0=ALU.is_gt, op1=ALU.mult,
                                             accum_out=one(zkept, t)).then_inc(kept, 1)

                def lo_turned(t, b):
                    wait(dve, strip_hi, GA[name] + t + 1)
                    wait(dve, gathered, GA[name] + t - 1)
                    lo(SL[:, b, :, :], TPS, SH[:, b, :, :]).then_inc(strip_lo, 1)

                link_a = chain(dve_tail, 1)

                def read_a(t, b):
                    wait(dve, kept, KEEP[name] + t + 1)
                    link_a(t, 1, dve.reciprocal(one(rkept, t), one(zkept, t)))
                    if name == "A0":
                        return dve.tensor_scalar(row(UA, t), OUT[b][:, 0:D], one(rkept, t), None, ALU.mult)
                    return dve.scalar_tensor_tensor(out=row(Y, t), in0=OUT[b][:, 0:D], scalar=one(rkept, t),
                                                    in1=row(Y, t), op0=ALU.mult, op1=ALU.add)

                pipeline(dve, keep_e, lo_turned, read(GA[name], read_a))
                dve.wait_ge(gather_read, GA[name] + NT)
                if name == "A0":
                    dve.wait_ge(ld_w, LD["L3a"])
                    mark(raw_ready)
                    split_w("L3a", WL[:, :, 0:2 * D], raw[:, :, 0:2 * D], WH[:, :, 0:2 * D])

                    def evac_l3a(t, b):
                        lo(row(FL, t), pbank[b][0][:, D:2 * D], row(FH, t))
                        lo(TQL[:, :, cols(t)], pbank[b][1][:, 0:D].rearrange("p (k i) -> p k i", k=2),
                           TQH[:, :, cols(t)])
                        return dve.tensor_tensor(row(Y, t), row(Y, t), pbank[b][0][:, 0:D], ALU.add)

                    pipeline(dve, nothing, turn(PJ["L3a"]), evac(PJ["L3a"], evac_l3a))
            norm_stats("end", Y)
            dve.wait_ge(ld_late, 32)
            link_f = chain(dve_tail, 2)

            def final(t):
                dve.wait_ge(fin_a, t + 1)
                link_f(t, 1, dve.tensor_tensor(row(Y, t), row(Y, t), gam[:, :], ALU.mult))
                dve.tensor_tensor(row(X, t), row(X, t), bet[:, :], ALU.add)
                link_f(t, 2, tick())
                dve.tensor_tensor(row(Y, t), row(Y, t), row(X, t), ALU.add).then_inc(fin, 1)

            each_tile(dve, final)


_ORDER = ["x", "adjT", "L0_gnn_weight", "L0_gnn_learnable_diag_1", "L0_gnn_bias", "L1_gnn_W_sa", "L1_gnn_a_sa",
          "L1_gnn_W_gcnb", "L1_gnn_b_gcnb", "L1_gnn_Wa", "L1_gnn_ba", "L1_gnn_Wb", "L1_gnn_bb", "L2_gnn_W_stack",
          "L3_gnn_W1", "L3_gnn_W2", "L3_gnn_W3", "L3_gnn_U1", "L3_gnn_U2", "L3_gnn_U3", "L3_gnn_gamma", "L3_gnn_beta"]


def kernel(**inputs):
    import numpy as _np
    import concourse.bacc as _bacc
    from concourse import mybir as _mybir
    from concourse.bass_utils import run_bass_kernel_spmd as _run

    inputs = dict(inputs)
    x, adj = _np.asarray(inputs.pop("x")), _np.asarray(inputs.pop("adj"))
    inputs["x"] = _np.zeros((NP, D), x.dtype)
    inputs["x"][:N] = x
    inputs["adjT"] = _np.zeros((NP, NP), adj.dtype)
    inputs["adjT"][:N, :N] = adj.T
    nc = _bacc.Bacc("TRN2", target_bir_lowering=False, num_devices=1)
    arrays, args = {}, []
    for name in _ORDER:
        a = _np.ascontiguousarray(inputs[name])
        arrays[f"in_{name}"] = a
        args.append(nc.dram_tensor(f"in_{name}", a.shape, _mybir.dt.from_np(a.dtype), kind="ExternalInput").ap())
    args.append(nc.dram_tensor("out_rows", (N, D), _mybir.dt.float32, kind="ExternalOutput").ap())
    build(nc, *args)
    r = _run(nc, [arrays], core_ids=[0])
    return r.results[0]["out_rows"]
```

```python
from contextlib import ExitStack

import concourse.bass as bass
from concourse import mybir

F32 = mybir.dt.float32
F32R = mybir.dt.float32r
U32 = mybir.dt.uint32
ALU = mybir.AluOpType
ACT = mybir.ActivationFunctionType
AX = mybir.AxisListType

P = 128
N = 1354
NT = -(-N // P)
NP = NT * P
D = 256
KB = D // P
BANK = 512
CHUNKS = [(c, min(BANK, N - c)) for c in range(0, N, BANK)]
LN_EPS = 1e-5
SLOPE = 0.01
P_NUC = 0.9
BASE_BITS = 0x38000000
TOP_BIT = 26
SEARCH_BITS = 27
COARSE_BITS = 14
ACT_TILES = 4
DVE_TILES = NT - ACT_TILES

PJ = {name: NT * k for k, name in enumerate(["L0", "L1", "L2a", "L2b", "L3s", "L3q", "L3a"])}
GA = {name: NT * k for k, name in enumerate(["L0", "L1b", "L1a", "L2a", "L2b", "L3s", "L3t", "A0", "A1"])}
SCO = {name: NT * k for k, name in enumerate(["L2a", "L2b", "A0", "A1"])}
MSK = {name: NT * k for k, name in enumerate(["L1a", "L2a", "L2b"])}
KEEP = {name: NT * k for k, name in enumerate(["A0", "A1"])}
WPREP = {name: k + 1 for k, name in enumerate(["L0", "L1", "L1r", "L2a", "L2b", "L3s", "L3u", "L3q", "L3a"])}
NORM = {name: k + 1 for k, name in enumerate(["L0", "L1", "L2", "L3", "end"])}


def wait(eng, sem, value):
    if isinstance(value, int) and value <= 0:
        return
    eng.wait_ge(sem, value)


def pipeline(eng, *steps):
    def turn(t, parity, static):
        for lag, step in enumerate(steps):
            if static and not 0 <= t - lag < NT:
                continue
            step(t - lag, (parity + lag) % 2)

    for t in range(3):
        turn(t, t % 2, True)
    with eng.Fori(3, NT - 1, 2) as t:
        turn(t, 1, False)
        turn(t + 1, 0, False)
    for t in range(NT, NT + len(steps) - 1):
        turn(t, t % 2, True)


def each_tile(eng, step):
    with eng.Fori(0, NT, 1) as t:
        step(t)


def build(nc, x, adjT, w0, d0, b0, w_sa, a_sa, w_gc, b_gc, wa, ba, wb, bb, w_l2, w1, w2, w3, u1, u2, u3, gamma,
          beta, out):
    with ExitStack() as ctx:
        def sb(name, shape, dt=F32, at=ctx):
            return at.enter_context(nc.sbuf_tensor(name, shape, dt))

        def sem(name):
            return ctx.enter_context(nc.semaphore(name))

        X = sb("x_rows", [P, NT, D])
        H = sb("h_rows", [P, NT, D])
        Y = sb("y_rows", [P, NT, D])
        FH = sb("feat_hi", [P, NT, D + 2], F32R)
        FL = sb("feat_lo", [P, NT, D + 2], F32R)
        SH = sb("strip_hi_buf", [P, 2, NT, P], F32R)
        SL = sb("strip_lo_buf", [P, 2, NT, P], F32R)
        TMP = sb("tmp", [P, NP])
        WH = sb("w_hi_buf", [P, KB, 520], F32R)
        WL = sb("w_lo_buf", [P, KB, 520], F32R)
        W12 = sb("w12", [P, KB, 64])
        ident = sb("ident", [P, P])
        onezero = sb("onezero", [P, NT, 2])
        ticks = sb("ticks", [P, 40])
        bcast = sb("bcast", [P, D])
        stats = sb("stats", [P, NT, 6])
        mv = sb("mean_var", [P, NT, 2])
        var = sb("var_eps", [P, NT])
        std = sb("std", [P, NT])
        rstd = sb("rstd", [P, NT])
        nmr = sb("neg_mean_rstd", [P, NT])
        small = sb("small", [P, 36, NT])
        nmax, zsum, rz, rowsum, rrow, colsum, rcol = (small[:, k, :] for k in range(7))
        cut, mass, bits, cand, keep, zkept, rkept, target = (small[:, 7 + k, :] for k in range(8))
        den, rden, ra, rowsc, colsc = (small[:, 15 + k, :] for k in range(5))
        nudged, relu_sum, sign_sum, upper, below, above, vcut, ties, qlim, flag_a, flag_b, acc = (
            small[:, 20 + k, :] for k in range(12))
        top8 = sb("top8", [P, 3, NT, 8])
        flags = sb("flags", [P, 2])
        flag_i = sb("flag_int", [1, 2], U32)
        vab = sb("vab", [P, NT, 3])
        tab = sb("tab", [P, NT, 2])
        bab = sb("bab", [P, 2])
        d1 = sb("d1", [P, KB])
        hT_H = SH[:, :, 0:KB, :]
        hT_L = SL[:, :, 0:KB, :]
        rows_in = TMP[:, 0:2 * D].rearrange("p (b d) -> p b d", b=2)
        raw = TMP[:, 0:KB * 520].rearrange("p (k n) -> p k n", k=KB)
        strip = TMP[:, :].rearrange("p (j i) -> p j i", j=NT)
        l1_strip = [Y[:, :, :].rearrange("p t d -> p (t d)")[:, b * NP:(b + 1) * NP] for b in range(2)]
        expt = [Y[:, :, :].rearrange("p t d -> p (t d)")[:, b * NP:(b + 1) * NP] for b in range(2)]

        with ExitStack() as scope:
            AT = sb("adj_t", [P, NT, NP], F32, scope)
            with ExitStack() as s1:
                F2H = sb("feat2_hi", [P, NT, D + 2], F32R, s1)
                F2L = sb("feat2_lo", [P, NT, D + 2], F32R, s1)
                SLB = sb("s_left", [P, NP], F32, s1)
                WrH = sb("w_left_hi", [P, KB, P], F32R, s1)
                WrL = sb("w_left_lo", [P, KB, P], F32R, s1)
                wlr = sb("w_left_right", [P, KB, 2], F32, s1)
                abc = sb("a_bcast", [P, 2 * D], F32, s1)
                bgc = sb("b_gcnb_bcast", [P, D], F32, s1)
                junk = sb("junk", [P, D], F32, s1)
                U1B = sb("u_rows_l1", [P, NT, D], F32, s1)
            with ExitStack() as s2:
                TH = sb("whs_t_hi", [P, 4, NP], F32R, s2)
                TL = sb("whs_t_lo", [P, 4, NP], F32R, s2)
                QH = sb("q_hi", [P, 2, KB, P], F32R, s2)
                QL = sb("q_lo", [P, 2, KB, P], F32R, s2)
                vrow = sb("vrow", [P, D], F32, s2)
            with ExitStack() as s3:
                G2H = sb("feat3_hi", [P, NT, D], F32R, s3)
                G2L = sb("feat3_lo", [P, NT, D], F32R, s3)
                UG = sb("u_rows_l3", [P, NT, D], F32, s3)
                VH = sb("v_hi", [P, KB, BANK], F32R, s3)
                VL = sb("v_lo", [P, KB, BANK], F32R, s3)
        with ExitStack() as scope:
            E = sb("e_rows", [P, NT, N], F32, scope)
            with ExitStack() as s4:
                TQH = sb("qk_t_hi", [P, 2, NP], F32R, s4)
                TQL = sb("qk_t_lo", [P, 2, NP], F32R, s4)
            with ExitStack() as s5:
                EQ = sb("is_tie", [P, NT, N], mybir.dt.uint8, s5)
            hold = sb("qk_hold", [P, 4 * NP], F32, scope)
            AQH = sb("aq_hi", [P, 2, P], F32R, scope)
            AQL = sb("aq_lo", [P, 2, P], F32R, scope)
            VQH = sb("wqk_hi", [P, KB, D], F32R, scope)
            VQL = sb("wqk_lo", [P, KB, D], F32R, scope)
            UA = sb("u_rows_a", [P, NT, D], F32, scope)
            ET2 = sb("kept_tile", [P, NP], F32, scope)
            gam = sb("gamma_bcast", [P, D], F32, scope)
            bet = sb("beta_bcast", [P, D], F32, scope)
        kept_t = [TMP[:, :], ET2[:, :]]

        SC = ctx.enter_context(nc.psum_tensor("scores", [P, 3 * BANK], F32))
        TP = ctx.enter_context(nc.psum_tensor("turned_ps", [P, 3 * BANK], F32))
        OUT = [ctx.enter_context(nc.psum_tensor(f"out{b}", [P, BANK], F32)) for b in range(2)]
        pbank = [[SC[:, 0:BANK], SC[:, BANK:2 * BANK], SC[:, 2 * BANK:]],
                 [OUT[0][:, :], OUT[1][:, :], TP[:, 2 * BANK:]]]
        TPS = TP[:, 0:NP].rearrange("p (j i) -> p j i", j=NT)

        ld_x, ld_adj, ld_small, ld_l1, ld_w, ld_late, stored = (sem(n) for n in (
            "ld_x", "ld_adj", "ld_small", "ld_l1", "ld_w", "ld_late", "stored"))
        consts = sem("consts")
        d_made = sem("d_made")
        raw_ready = sem("raw_ready")
        w_hi, w_lo = sem("w_hi"), sem("w_lo")
        w12_t, w12_c, w12_m, w12_d = (sem(n) for n in ("w12_t", "w12_c", "w12_m", "w12_d"))
        var_ready, std_ready, norm_ready = sem("var_ready"), sem("std_ready"), sem("norm_ready")
        h_rows = sem("h_made")
        f_hi = sem("f_hi")
        staged = sem("rows_staged")
        turned = sem("rows_turned")
        turn_hi, turn_lo = sem("turn_hi"), sem("turn_lo")
        projected = sem("projected")
        proj_hi, proj_read = sem("proj_hi"), sem("proj_read")
        strip_hi, strip_lo = sem("strip_hi"), sem("strip_lo")
        gathered, gather_read = sem("gathered"), sem("gather_read")
        q_staged, scored, maxed, exped = (sem(n) for n in ("q_staged", "scored", "maxed", "exped"))
        strip_turned, masked, kept = sem("strip_turned"), sem("masked"), sem("kept")
        scored_z, e_raw = sem("lrelu_made"), sem("e_raw")
        gate_in, gate_out = sem("gate_in"), sem("gate_out")
        sig_out, x_l1 = sem("sig_out"), sem("x_l1")
        adj_plus = sem("adj_plus")
        cand_ready, act_mass, act_step = sem("cand_ready"), sem("act_mass"), sem("act_step")
        flag_ready, flag_sum = sem("flag_ready"), sem("flag_sum")
        general = {name: sem(f"general_{name}") for name in KEEP}
        tie_step = {name: sem(f"tie_step_{name}") for name in KEEP}
        pads = sem("pads")
        fin = sem("final_rows")
        dve_lead, dve_mid, dve_tail, dve_seq = (sem(n) for n in ("dve_lead", "dve_mid", "dve_tail", "dve_seq"))
        fin_a = sem("final_scaled")

        block = ctx.enter_context(nc.Block())

        def w_rows(w):
            return w.rearrange("(k p) n -> p k n", p=P)

        def jrows(tile):
            return tile[:, 0:NP].rearrange("p (j i) -> p j i", j=NT)

        def cols(t):
            return bass.ds(t * P, P)

        @block.sync
        def _(sp):
            sp.dma_start(X[:, :, :], x.rearrange("(t p) d -> p t d", p=P)).then_inc(ld_x, 16)
            sp.dma_start(d1[:, :], d0.rearrange("(k p) -> p k", p=P), allow_slow_non_contiguous=True).then_inc(ld_small, 16)
            sp.dma_start(bcast[:, :], b0.rearrange("(a n) -> a n", a=1).broadcast_to([P, D])).then_inc(ld_small, 16)
            sp.dma_start(raw[:, :, 0:D], w_rows(w0)).then_inc(ld_w, 16)
            for t in range(NT):
                sp.dma_start(AT[:, t, :], adjT[t * P:(t + 1) * P, :]).then_inc(ld_adj, 16)
            sp.dma_start(abc[:, :], a_sa.broadcast_to([P, 2 * D])).then_inc(ld_l1, 16)
            sp.dma_start(bgc[:, :], b_gc.rearrange("(a n) -> a n", a=1).broadcast_to([P, D])).then_inc(ld_l1, 16)
            sp.dma_start(bab[:, 0:1], ba.rearrange("(a n) -> a n", a=1).broadcast_to([P, 1])).then_inc(ld_l1, 16)
            sp.dma_start(bab[:, 1:2], bb.rearrange("(a n) -> a n", a=1).broadcast_to([P, 1])).then_inc(ld_l1, 16)
            sp.wait_ge(turned, PJ["L0"] + NT)
            sp.dma_start(raw[:, :, 0:D], w_rows(w_gc)).then_inc(ld_w, 16)
            sp.dma_start(raw[:, :, D + 6:D + 6 + D], w_rows(w_sa)).then_inc(ld_w, 16)
            for c, (w, half) in enumerate([(wa, 0), (wb, 0), (wa, 1), (wb, 1)]):
                sp.dma_start(raw[:, :, D + c:D + c + 1],
                             w[0:1, half * D:(half + 1) * D].rearrange("a (k p) -> p k a", p=P),
                             allow_slow_non_contiguous=True).then_inc(ld_w, 16)
            sp.wait_ge(turned, PJ["L1"] + NT)
            sp.dma_start(raw[:, :, 0:64], w_rows(w1)).then_inc(ld_w, 16)
            sp.dma_start(raw[0:64, 0, 64:128], w2).then_inc(ld_w, 16)
            sp.wait_ge(w12_m, 1)
            sp.dma_start(raw[:, :, 0:2 * D], w_rows(w_l2[0])).then_inc(ld_w, 16)
            sp.wait_ge(strip_lo, GA["L2a"] + NT)
            sp.wait_ge(strip_hi, GA["L2a"] + NT)
            sp.dma_start(raw[:, :, 0:2 * D], w_rows(w_l2[1])).then_inc(ld_w, 16)
            sp.wait_ge(strip_lo, GA["L2b"] + NT)
            sp.wait_ge(strip_hi, GA["L2b"] + NT)
            sp.dma_start(raw[:, :, 0:D], w_rows(u1[0])).then_inc(ld_w, 16)
            sp.dma_start(raw[:, :, D:2 * D], w_rows(u2[0])).then_inc(ld_w, 16)
            sp.wait_ge(w_hi, WPREP["L3s"])
            sp.wait_ge(w_lo, WPREP["L3s"])
            sp.dma_start(raw[:, :, 0:D], w_rows(u1[1])).then_inc(ld_w, 16)
            sp.dma_start(raw[:, :, D:2 * D], w_rows(u2[1])).then_inc(ld_w, 16)
            sp.wait_ge(gathered, GA["L3t"] + NT)
            sp.dma_start(raw[:, :, 128:192], w_rows(w3)).then_inc(ld_w, 16)
            sp.dma_start(gam[:, :], gamma.rearrange("(a n) -> a n", a=1).broadcast_to([P, D])).then_inc(ld_late, 16)
            sp.dma_start(bet[:, :], beta.rearrange("(a n) -> a n", a=1).broadcast_to([P, D])).then_inc(ld_late, 16)
            sp.wait_ge(strip_turned, SCO["A0"] + NT)
            sp.dma_start(raw[:, :, 0:D], w_rows(u3[0])).then_inc(ld_w, 16)
            sp.dma_start(raw[:, :, D:2 * D], w_rows(u3[1])).then_inc(ld_w, 16)
            for t in range(NT):
                rows = min(P, N - t * P)
                sp.wait_ge(fin, t + 1)
                sp.dma_start(out[t * P:t * P + rows, :], Y[0:rows, t, :]).then_inc(stored, 16)
            sp.wait_ge(stored, 16 * NT)

        LD = {}
        n = 0
        for name, count in (("L0", 1), ("L1", 6), ("L1r", 2), ("L2a", 1), ("L2b", 1), ("L3s", 2), ("L3u", 2),
                            ("L3q", 1), ("L3a", 2)):
            n += 16 * count
            LD[name] = n

        @block.gpsimd
        def _(pool):
            pool.memset(ident[:, :], 0.0).then_inc(consts, 1)
            pool.memset(onezero[:, :, :], 0.0).then_inc(consts, 1)
            pool.wait_ge(consts, 2)
            pool.affine_select(out=ident[:, :], in_=ident[:, :], compare_op=ALU.not_equal, fill=1.0, base=0,
                               pattern=[[-1, P]], channel_multiplier=1).then_inc(consts, 1)
            pool.memset(onezero[:, :, 0:1], 1.0).then_inc(consts, 1)

            def ahead(t, b):
                pass

            def lo_of_adj(g0):
                def step(t, b):
                    wait(pool, strip_hi, g0 + t + 1)
                    wait(pool, gathered, g0 + t - 1)
                    pool.tensor_tensor(SL[:, b, :, :], AT[:, :, cols(t)], SH[:, b, :, :].bitcast(F32),
                                       ALU.subtract).then_inc(strip_lo, 1)
                return step

            def lo_of_tmp(g0, src):
                def step(t, b):
                    wait(pool, strip_hi, g0 + t + 1)
                    wait(pool, gathered, g0 + t - 1)
                    pool.tensor_tensor(SL[:, b, :, :], jrows(src[b]), SH[:, b, :, :].bitcast(F32),
                                       ALU.subtract).then_inc(strip_lo, 1)
                return step

            def stage_q(s0, kb, src_hi, src_lo, dst_hi, dst_lo):
                def step(t, b):
                    wait(pool, scored, s0 + t - 1)
                    pool.tensor_copy(dst_hi(b), src_hi[:, 0:kb, cols(t)])
                    pool.tensor_copy(dst_lo(b), src_lo[:, 0:kb, cols(t)]).then_inc(q_staged, 1)
                return step

            def q_l2(s0):
                return stage_q(s0, KB, TH, TL, lambda b: QH[:, b, :, :], lambda b: QL[:, b, :, :])

            def q_a(s0):
                return stage_q(s0, 1, TQH, TQL, lambda b: AQH[:, b:b + 1, :], lambda b: AQL[:, b:b + 1, :])

            pool.wait_ge(ld_adj, 16 * NT)
            pool.wait_ge(projected, PJ["L0"] + NT)
            pipeline(pool, lo_of_adj(GA["L0"]))
            pool.wait_ge(projected, PJ["L1"] + NT)
            pipeline(pool, lo_of_adj(GA["L1b"]))
            pipeline(pool, lo_of_tmp(GA["L1a"], l1_strip))
            for name in ("L2a", "L2b"):
                pool.wait_ge(proj_read, PJ[name] + NT)
                pool.wait_ge(proj_hi, PJ[name] + NT)
                pipeline(pool, q_l2(SCO[name]), ahead, lo_of_tmp(GA[name], [TMP, TMP]))
            pool.wait_ge(adj_plus, 1)
            pipeline(pool, lo_of_adj(GA["L3s"]))
            pool.wait_ge(projected, PJ["L3s"] + NT)
            pipeline(pool, lo_of_adj(GA["L3t"]))
            for name, pj in (("A0", "L3q"), ("A1", "L3a")):
                pool.wait_ge(proj_read, PJ[pj] + NT)
                pool.wait_ge(proj_hi, PJ[pj] + NT)
                pipeline(pool, q_a(SCO[name]))

        @block.scalar
        def _(act):
            def split_w(name, dst, src):
                act.wait_ge(raw_ready, WPREP[name])
                act.activation(dst, src, ACT.Copy).then_inc(w_hi, 1)

            def root(name):
                act.wait_ge(var_ready, NORM[name])
                act.activation(std[:, :], var[:, :], ACT.Sqrt).then_inc(std_ready, 1)
                act.wait_ge(norm_ready, NORM[name])

            def stage_norm(p0):
                def step(t, b):
                    wait(act, turned, p0 + t - 1)
                    act.activation(rows_in[:, b:b + 1, :], X[:, bass.ds(t, 1), :], ACT.Relu,
                                   bias=nmr[:, bass.ds(t, 1)], scale=rstd[:, bass.ds(t, 1)]).then_inc(staged, 1)
                return step

            def stage_copy(p0, src):
                def step(t, b):
                    wait(act, turned, p0 + t - 1)
                    act.activation(rows_in[:, b:b + 1, :], src[:, bass.ds(t, 1), :], ACT.Copy).then_inc(staged, 1)
                return step

            def turn(p0):
                def step(t, b):
                    wait(act, turned, p0 + t + 1)
                    wait(act, projected, p0 + t - 1)
                    act.activation(hT_H[:, b, :, :].rearrange("p k i -> p (k i)"),
                                   TP[:, BANK * b:BANK * b + D], ACT.Copy).then_inc(turn_hi, 1)
                return step

            def evac(p0, *parts):
                def step(t, b):
                    wait(act, projected, p0 + t + 1)
                    for k, part in enumerate(parts):
                        ins = part(t, b)
                    ins.then_inc(proj_hi, 1)
                return step

            def copy_part(dst, bank, c0, n, scale=None):
                def part(t, b):
                    if scale is None:
                        return act.activation(dst(t), pbank[b][bank][:, c0:c0 + n], ACT.Copy)
                    return act.activation(dst(t), pbank[b][bank][:, c0:c0 + n], ACT.Copy,
                                          scale=scale[:, bass.ds(t, 1)])
                return part

            def hi_of_adj(g0):
                def step(t, b):
                    wait(act, gathered, g0 + t - 1)
                    act.activation(SH[:, b, :, :], AT[:, :, cols(t)], ACT.Copy).then_inc(strip_hi, 1)
                return step

            def hi_of_tmp(g0, m0, src):
                def step(t, b):
                    wait(act, masked, m0 + t + 1)
                    wait(act, gathered, g0 + t - 1)
                    act.activation(SH[:, b, :, :], jrows(src[b]), ACT.Copy).then_inc(strip_hi, 1)
                return step

            def exp_l2(s0):
                def step(t, b):
                    wait(act, maxed, s0 + t + 1)
                    wait(act, strip_turned, s0 + t - 1)
                    act.activation(expt[b][:, 0:N], SC[:, 0:N], ACT.Exp, bias=nmax[:, bass.ds(t, 1)],
                                   accum_out=zsum[:, bass.ds(t, 1)]).then_inc(exped, 1)
                return step

            fh = lambda n: (lambda t: FH[:, t, 0:n] if isinstance(t, int) else FH[:, bass.ds(t, 1), 0:n])

            split_w("L0", WH[:, :, 0:2 * D], raw[:, :, 0:2 * D])
            act.wait_ge(ld_x, 16)
            root("L0")
            act.wait_ge(w_lo, WPREP["L0"])
            pipeline(act, stage_norm(PJ["L0"]), turn(PJ["L0"]), evac(
                PJ["L0"], copy_part(lambda t: FH[:, bass.ds(t, 1), 0:D], 0, D, D)))
            act.wait_ge(projected, PJ["L0"] + NT)
            split_w("L1", WH[:, :, 0:D + 6 + D], raw[:, :, 0:D + 6 + D])
            act.activation(WrH[:, :, :], wlr[:, :, 0:1].broadcast_to([P, KB, P]), ACT.Copy).then_inc(w_hi, 1)
            act.activation(F2H[:, :, D:D + 2], onezero[:, :, :], ACT.Copy)
            act.wait_ge(ld_adj, 16 * NT)
            pipeline(act, hi_of_adj(GA["L0"]))
            act.wait_ge(gathered, GA["L0"] + NT)
            root("L1")
            act.wait_ge(w_lo, WPREP["L1r"])
            pipeline(act, stage_norm(PJ["L1"]), turn(PJ["L1"]), evac(
                PJ["L1"], copy_part(lambda t: FH[:, bass.ds(t, 1), 0:D + 2], 0, 0, D + 2),
                copy_part(lambda t: F2H[:, bass.ds(t, 1), 0:D], 1, 0, D),
                copy_part(lambda t: SLB[:, cols(t)], 2, 0, P)))
            act.wait_ge(projected, PJ["L1"] + NT)
            pipeline(act, hi_of_adj(GA["L1b"]))
            split_w("L2a", WH[:, :, 0:2 * D], raw[:, :, 0:2 * D])
            act.wait_ge(gate_in, 1)
            act.activation(tab[:, :, :], tab[:, :, :], ACT.Sigmoid).then_inc(gate_out, 1)

            def exp_l1(t, b):
                wait(act, scored_z, t + 1)
                act.activation(l1_strip[b], l1_strip[b], ACT.Exp, scale=-1.0).then_inc(e_raw, 1)

            pipeline(act, exp_l1, hi_of_tmp(GA["L1a"], MSK["L1a"], l1_strip))

            def sig(t):
                act.wait_ge(gather_read, GA["L1a"] + NT)
                act.activation(U1B[:, bass.ds(t, 1), :], U1B[:, bass.ds(t, 1), :], ACT.Sigmoid).then_inc(sig_out, 1)

            each_tile(act, sig)
            root("L2")
            act.wait_ge(x_l1, 1)

            def norm_h(t):
                act.activation(H[:, bass.ds(t, 1), :], X[:, bass.ds(t, 1), :], ACT.Relu, bias=nmr[:, bass.ds(t, 1)],
                               scale=rstd[:, bass.ds(t, 1)]).then_inc(h_rows, 1)

            each_tile(act, norm_h)
            act.wait_ge(h_rows, NT)
            for name in ("L2a", "L2b"):
                if name == "L2b":
                    split_w("L2b", WH[:, :, 0:2 * D], raw[:, :, 0:2 * D])
                    act.wait_ge(gather_read, GA["L2a"] + NT)
                act.wait_ge(w_lo, WPREP[name])
                act.wait_ge(gathered, GA[name])
                pipeline(act, stage_copy(PJ[name], H), turn(PJ[name]), evac(
                    PJ[name], copy_part(lambda t: FH[:, bass.ds(t, 1), 0:D], 0, 0, D),
                    lambda t, b: act.activation(TH[:, :, cols(t)], pbank[b][1].rearrange("p (k i) -> p k i", k=4),
                                                ACT.Copy)))
                act.wait_ge(pads, 1)
                act.wait_ge(projected, PJ[name] + NT)
                pipeline(act, exp_l2(SCO[name]), hi_of_tmp(GA[name], MSK[name], [TMP, TMP]))
            act.wait_ge(gathered, GA["L2b"] + NT)
            root("L3")

            def norm_h3(t):
                norm_h(t)
                act.wait_ge(h_rows, t + (NT + 1))
                act.activation(FH[:, bass.ds(t, 1), 0:D], H[:, bass.ds(t, 1), :], ACT.Copy).then_inc(f_hi, 1)

            act.activation(FH[:, :, D:D + 2], onezero[:, :, :], ACT.Copy)
            each_tile(act, norm_h3)
            act.wait_ge(adj_plus, 1)
            pipeline(act, hi_of_adj(GA["L3s"]))
            split_w("L3s", WH[:, :, 0:2 * D], raw[:, :, 0:2 * D])
            split_w("L3u", VH[:, :, :], raw[:, :, 0:2 * D])
            act.wait_ge(gather_read, GA["L3s"] + NT)
            act.wait_ge(gate_in, 2)
            act.wait_ge(w_lo, WPREP["L3u"])
            pipeline(act, stage_copy(PJ["L3s"], UG), turn(PJ["L3s"]), evac(
                PJ["L3s"], copy_part(lambda t: FH[:, bass.ds(t, 1), 0:D], 1, 0, D, rrow),
                copy_part(lambda t: G2H[:, bass.ds(t, 1), :], 1, D, D, rcol)))
            act.wait_ge(projected, PJ["L3s"] + NT)
            pipeline(act, hi_of_adj(GA["L3t"]))
            split_w("L3q", VQH[:, :, :], raw[:, :, 0:D])
            act.wait_ge(gather_read, GA["L3t"] + NT)
            act.wait_ge(w_lo, WPREP["L3q"])
            pipeline(act, stage_copy(PJ["L3q"], H), turn(PJ["L3q"]), evac(
                PJ["L3q"], lambda t, b: act.activation(FH[:, bass.ds(t, 1), 0:D], H[:, bass.ds(t, 1), :], ACT.Copy),
                lambda t, b: act.activation(TQH[:, :, cols(t)],
                                            pbank[b][0][:, 0:D].rearrange("p (k i) -> p k i", k=2), ACT.Copy)))

            def exp_a(s0):
                def step(t, b):
                    wait(act, maxed, s0 + t + 1)
                    act.activation(E[:, bass.ds(t, 1), :], [SC, TP][b][:, 0:N], ACT.Exp, bias=nmax[:, bass.ds(t, 1)],
                                   accum_out=zsum[:, bass.ds(t, 1)]).then_inc(exped, 1)
                return step

            def coarse(n):
                out2 = UA[:, :, :].rearrange("p t d -> p (t d)")
                with act.Fori(0, COARSE_BITS, 1) as i:
                    act.wait_ge(cand_ready, i + (n * COARSE_BITS + 1))
                    for k in range(2 * ACT_TILES):
                        t = DVE_TILES + k // 2
                        if k >= 2:
                            act.wait_ge(act_step, i * (2 * ACT_TILES) + (n * COARSE_BITS * 2 * ACT_TILES + k - 1))
                        act.activation(out2[:, (k % 2) * N:(k % 2 + 1) * N], E[:, t, :],
                                       [ACT.Relu, ACT.Sign][k % 2], bias=nudged[:, t:t + 1],
                                       accum_out=[relu_sum, sign_sum][k % 2][:, t:t + 1]).then_inc(act_step, 1)

            def hi_of_turned(g0, s0):
                def step(t, b):
                    wait(act, strip_turned, s0 + t + 1)
                    wait(act, gathered, g0 + t - 1)
                    act.activation(SH[:, b, :, :], TPS, ACT.Copy).then_inc(strip_hi, 1)
                return step

            pipeline(act, exp_a(SCO["A0"]))
            coarse(0)
            act.wait_ge(projected, PJ["L3q"] + NT)
            pipeline(act, hi_of_turned(GA["A0"], SCO["A0"]))
            split_w("L3a", WH[:, :, 0:2 * D], raw[:, :, 0:2 * D])
            act.wait_ge(gather_read, GA["A0"] + NT)
            act.wait_ge(w_lo, WPREP["L3a"])
            pipeline(act, stage_copy(PJ["L3a"], UA), turn(PJ["L3a"]), evac(
                PJ["L3a"], copy_part(lambda t: FH[:, bass.ds(t, 1), 0:D], 0, D, D),
                lambda t, b: act.activation(TQH[:, :, cols(t)],
                                            pbank[b][1][:, 0:D].rearrange("p (k i) -> p k i", k=2), ACT.Copy)))
            pipeline(act, exp_a(SCO["A1"]))
            coarse(1)
            act.wait_ge(projected, PJ["L3a"] + NT)
            pipeline(act, hi_of_turned(GA["A1"], SCO["A1"]))
            act.wait_ge(var_ready, NORM["end"])
            act.activation(std[:, :], var[:, :], ACT.Sqrt).then_inc(std_ready, 1)
            act.wait_ge(norm_ready, NORM["end"])

            def last(t):
                act.activation(Y[:, bass.ds(t, 1), :], Y[:, bass.ds(t, 1), :], ACT.Identity,
                               bias=nmr[:, bass.ds(t, 1)], scale=rstd[:, bass.ds(t, 1)]).then_inc(fin_a, 1)

            each_tile(act, last)

        @block.tensor
        def _(pe):
            def turn(p0):
                def step(t, b):
                    wait(pe, staged, p0 + t + 1)
                    wait(pe, turn_hi, p0 + t - 1)
                    wait(pe, turn_lo, p0 + t - 1)
                    for k in range(KB):
                        ins = pe.transpose(TP[:, BANK * b + k * P:BANK * b + (k + 1) * P],
                                           rows_in[:, b, k * P:(k + 1) * P], ident[:, :])
                    ins.then_inc(turned, 1)
                return step

            def rows_times(b, dst, wh, wl, c0, n):
                terms = [(hT_H, wh), (hT_L, wh), (hT_H, wl)]
                for m, (left, right) in enumerate(terms):
                    for k in range(KB):
                        ins = pe.matmul(dst, left[:, b, k, :], right[:, k, c0:c0 + n], start=(m == 0 and k == 0),
                                        stop=(m == 2 and k == KB - 1))
                return ins

            def rows_times_turned(b, dst, wh, wl, c0):
                terms = [(wh, hT_H), (wh, hT_L), (wl, hT_H)]
                for m, (left, right) in enumerate(terms):
                    for k in range(KB):
                        ins = pe.matmul(dst, left[:, k, c0:c0 + P], right[:, b, k, :], start=(m == 0 and k == 0),
                                        stop=(m == 2 and k == KB - 1))
                return ins

            def project(p0, body):
                def step(t, b):
                    wait(pe, turn_lo, p0 + t + 1)
                    wait(pe, turn_hi, p0 + t + 1)
                    wait(pe, proj_read, p0 + t - 1)
                    wait(pe, proj_hi, p0 + t - 1)
                    body(b).then_inc(projected, 1)
                return step

            def gather(g0, *groups):
                def step(t, b):
                    wait(pe, strip_hi, g0 + t + 1)
                    wait(pe, strip_lo, g0 + t + 1)
                    wait(pe, gather_read, g0 + t - 1)
                    for c0, fh, fl, n in groups:
                        for m, (left, right) in enumerate([(SH, fh), (SL, fh), (SH, fl)]):
                            for j in range(NT):
                                ins = pe.matmul(OUT[b][:, c0:c0 + n], left[:, b, j, :], right[:, j, 0:n],
                                                start=(m == 0 and j == 0), stop=(m == 2 and j == NT - 1))
                    ins.then_inc(gathered, 1)
                return step

            def scores_l2(s0):
                def step(t, b):
                    wait(pe, q_staged, s0 + t + 1)
                    wait(pe, exped, s0 + t)
                    for c, n in CHUNKS:
                        for m, (q, k2) in enumerate([(QH, TH), (QL, TH), (QH, TL)]):
                            for k in range(KB):
                                ins = pe.matmul(SC[:, c:c + n], q[:, b, k, :], k2[:, KB + k, c:c + n],
                                                start=(m == 0 and k == 0), stop=(m == 2 and k == KB - 1))
                    ins.then_inc(scored, 1)
                return step

            def turn_l2(s0, m0):
                def step(t, b):
                    wait(pe, exped, s0 + t + 1)
                    wait(pe, masked, m0 + t)
                    for j in range(NT):
                        ins = pe.transpose(TP[:, j * P:(j + 1) * P], expt[b][:, j * P:(j + 1) * P], ident[:, :])
                    ins.then_inc(strip_turned, 1)
                return step

            def scores_a(s0):
                def step(t, b):
                    wait(pe, q_staged, s0 + t + 1)
                    wait(pe, exped, s0 + t - 1)
                    for c, n in CHUNKS:
                        for m, (q, k2) in enumerate([(AQH, TQH), (AQL, TQH), (AQH, TQL)]):
                            ins = pe.matmul([SC, TP][b][:, c:c + n], q[:, b, :], k2[:, 1, c:c + n], start=(m == 0),
                                            stop=(m == 2))
                    ins.then_inc(scored, 1)
                return step

            def turn_a(s0, k0, g0):
                def step(t, b):
                    wait(pe, kept, k0 + t + 1)
                    wait(pe, strip_hi, g0 + t)
                    wait(pe, strip_lo, g0 + t)
                    for j in range(NT):
                        ins = pe.transpose(TP[:, j * P:(j + 1) * P], kept_t[b][:, j * P:(j + 1) * P], ident[:, :])
                    ins.then_inc(strip_turned, 1)
                return step

            one = (0, FH, FL, D)
            pe.wait_ge(consts, 4)
            pe.wait_ge(w_lo, WPREP["L0"])
            pipeline(pe, turn(PJ["L0"]), project(PJ["L0"], lambda b: rows_times(b, pbank[b][0], WH, WL, 0, 2 * D)))
            pe.wait_ge(proj_read, PJ["L0"] + NT)
            pe.wait_ge(proj_hi, PJ["L0"] + NT)
            pipeline(pe, gather(GA["L0"], one))
            pe.wait_ge(w_lo, WPREP["L1r"])
            pe.wait_ge(gather_read, GA["L0"] + NT)

            def proj_l1(b):
                rows_times(b, pbank[b][0][:, 0:D + 6], WH, WL, 0, D + 6)
                rows_times(b, pbank[b][1][:, 0:D], WH, WL, D + 6, D)
                return rows_times_turned(b, pbank[b][2][:, 0:P], WrH, WrL, 0)

            pipeline(pe, turn(PJ["L1"]), project(PJ["L1"], proj_l1))
            pe.wait_ge(proj_read, PJ["L1"] + NT)
            pe.wait_ge(proj_hi, PJ["L1"] + NT)
            pe.wait_ge(raw_ready, WPREP["L1r"] + 0)
            pe.wait_ge(ld_w, LD["L1r"])
            for k in range(KB):
                ins = pe.transpose(TP[0:64, k * P:(k + 1) * P], raw[:, k, 0:64], ident[:, :])
            ins.then_inc(w12_t, 1)
            pe.wait_ge(w12_c, 1)
            for k in range(KB):
                ins = pe.matmul(TP[:, BANK + k * 64:BANK + (k + 1) * 64], raw[0:64, 1, 128 + k * P:128 + (k + 1) * P],
                                raw[0:64, 0, 64:128], start=True, stop=True)
            ins.then_inc(w12_m, 1)
            pipeline(pe, gather(GA["L1b"], (0, FH, FL, D + 2)))
            pipeline(pe, gather(GA["L1a"], (0, F2H, F2L, D + 2)))

            def proj_l2(b):
                rows_times(b, pbank[b][0][:, 0:D], WH, WL, 0, D)
                for k in range(4):
                    ins = rows_times_turned(b, pbank[b][1][:, k * P:(k + 1) * P], WH, WL, k * P)
                return ins

            for name in ("L2a", "L2b"):
                pe.wait_ge(w_lo, WPREP[name])
                pe.wait_ge(w12_d, 1)
                pe.wait_ge(gather_read, GA[name])
                pe.wait_ge(masked, MSK[name])
                pe.wait_ge(exped, SCO[name]) if name != "L2a" else None
                pipeline(pe, turn(PJ[name]), project(PJ[name], proj_l2))
                pe.wait_ge(proj_read, PJ[name] + NT)
                pe.wait_ge(proj_hi, PJ[name] + NT)
                pipeline(pe, scores_l2(SCO[name]), turn_l2(SCO[name], MSK[name]), gather(GA[name], one))
            pe.wait_ge(adj_plus, 2)
            pipeline(pe, gather(GA["L3s"], (0, FH, FL, D + 2)))
            pe.wait_ge(w_lo, WPREP["L3u"])
            pe.wait_ge(gather_read, GA["L3s"] + NT)

            def proj_l3s(b):
                rows_times(b, pbank[b][0], WH, WL, 0, 2 * D)
                return rows_times(b, pbank[b][1], VH, VL, 0, 2 * D)

            pipeline(pe, turn(PJ["L3s"]), project(PJ["L3s"], proj_l3s))
            pe.wait_ge(proj_read, PJ["L3s"] + NT)
            pe.wait_ge(proj_hi, PJ["L3s"] + NT)
            pipeline(pe, gather(GA["L3t"], one, (D, G2H, G2L, D)))
            pe.wait_ge(w_lo, WPREP["L3q"])
            pe.wait_ge(gather_read, GA["L3t"] + NT)

            def proj_qk(b, bank):
                rows_times_turned(b, pbank[b][bank][:, 0:P], VQH, VQL, 0)
                return rows_times_turned(b, pbank[b][bank][:, P:2 * P], VQH, VQL, P)

            def proj_l3a(b):
                rows_times(b, pbank[b][0], WH, WL, 0, 2 * D)
                return proj_qk(b, 1)

            pipeline(pe, turn(PJ["L3q"]), project(PJ["L3q"], lambda b: proj_qk(b, 0)))
            for name, pj in (("A0", "L3q"), ("A1", "L3a")):
                pe.wait_ge(proj_read, PJ[pj] + NT)
                pe.wait_ge(proj_hi, PJ[pj] + NT)
                pipeline(pe, scores_a(SCO[name]))
                for k in range(2):
                    pe.wait_ge(flag_ready, 2 * (name == "A1") + k + 1)
                    pe.matmul(OUT[0][0:1, k:k + 1], onezero[:, 0, 0:1], flags[:, k:k + 1], start=True,
                              stop=True).then_inc(flag_sum, 1)
                pipeline(pe, turn_a(SCO[name], KEEP[name], GA[name]), gather(GA[name], one))
                if name == "A0":
                    pe.wait_ge(w_lo, WPREP["L3a"])
                    pe.wait_ge(gather_read, GA["A0"] + NT)
                    pipeline(pe, turn(PJ["L3a"]), project(PJ["L3a"], proj_l3a))

        @block.vector
        def _(dve):
            seq = [0]

            def then(ins):
                seq[0] += 1
                ins.then_inc(dve_seq, 1)
                dve.wait_ge(dve_seq, seq[0])

            base = {}

            def chain(s, per_tile):
                b0_ = base.get(id(s), 0)
                base[id(s)] = b0_ + NT * per_tile

                def link(t, k, ins):
                    ins.then_inc(s, 1)
                    dve.wait_ge(s, t * per_tile + (b0_ + k))
                return link

            def norm_stats(name, src):
                for t in range(NT):
                    ins = dve.bn_stats(stats[:, t, :], src[:, t, :])
                then(ins)
                for t in range(NT):
                    ins = dve.bn_aggr(mv[:, t, :], stats[:, t, :])
                then(ins)
                dve.tensor_scalar(var[:, :], mv[:, :, 1], LN_EPS, None, ALU.add).then_inc(var_ready, 1)
                dve.wait_ge(std_ready, NORM[name])
                then(dve.reciprocal(rstd[:, :], std[:, :]))
                dve.scalar_tensor_tensor(out=nmr[:, :], in0=mv[:, :, 0], scalar=-1.0, in1=rstd[:, :], op0=ALU.mult,
                                         op1=ALU.mult).then_inc(norm_ready, 1)

            def split_w(name, dst, src, hi):
                dve.wait_ge(w_hi, WPREP[name])
                dve.tensor_tensor(dst, src, hi.bitcast(F32), ALU.subtract).then_inc(w_lo, 1)

            def turn(p0):
                def step(t, b):
                    wait(dve, turn_hi, p0 + t + 1)
                    wait(dve, projected, p0 + t - 1)
                    dve.tensor_tensor(hT_L[:, b, :, :].rearrange("p k i -> p (k i)"), TP[:, BANK * b:BANK * b + D],
                                      hT_H[:, b, :, :].rearrange("p k i -> p (k i)").bitcast(F32),
                                      ALU.subtract).then_inc(turn_lo, 1)
                return step

            tick_at = [-1]

            def tick():
                tick_at[0] += 1
                return dve.memset(ticks[:, tick_at[0]:tick_at[0] + 1], 0.0)

            def mark(s):
                tick().then_inc(s, 1)

            def nothing(t, b):
                pass

            def evac(p0, body):
                def step(t, b):
                    wait(dve, projected, p0 + t + 1)
                    wait(dve, proj_hi, p0 + t + 1)
                    body(t, b).then_inc(proj_read, 1)
                return step

            def lo(dst, src, hi):
                return dve.tensor_tensor(dst, src, hi.bitcast(F32), ALU.subtract)

            def read(g0, body):
                def step(t, b):
                    wait(dve, gathered, g0 + t + 1)
                    body(t, b).then_inc(gather_read, 1)
                return step

            one = lambda a, t: a[:, bass.ds(t, 1)]
            row = lambda a, t, n=D: a[:, bass.ds(t, 1), 0:n]

            dve.wait_ge(ld_small, 16 * 2)
            then(dve.tensor_scalar(d1[:, :], d1[:, :], 1.0, None, ALU.add))
            dve.wait_ge(ld_w, LD["L0"])
            for k in range(KB):
                ins = dve.tensor_scalar(raw[:, k, D:2 * D], raw[:, k, 0:D], d1[:, k:k + 1], None, ALU.mult)
            ins.then_inc(raw_ready, 1)
            split_w("L0", WL[:, :, 0:2 * D], raw[:, :, 0:2 * D], WH[:, :, 0:2 * D])
            dve.wait_ge(ld_x, 16)
            norm_stats("L0", X)
            link0 = chain(dve_tail, 1)

            def evac_l0(t, b):
                lo(row(FL, t), pbank[b][0][:, D:2 * D], row(FH, t))
                link0(t, 1, dve.tensor_tensor(row(X, t), row(X, t), pbank[b][0][:, 0:D], ALU.add))
                return dve.tensor_tensor(row(X, t), row(X, t), bcast[:, :], ALU.add)

            pipeline(dve, nothing, turn(PJ["L0"]), evac(PJ["L0"], evac_l0))
            dve.wait_ge(proj_read, PJ["L0"] + NT)
            dve.wait_ge(ld_w, LD["L1"])
            dve.wait_ge(ld_l1, 16 * 4)
            for k in range(KB):
                for side in range(2):
                    then(dve.tensor_tensor_reduce(out=junk[:, :], in0=raw[:, k, D + 6:D + 6 + D],
                                                  in1=abc[:, side * D:(side + 1) * D], scale=1.0, scalar=0.0,
                                                  op0=ALU.mult, op1=ALU.add, accum_out=wlr[:, k, side:side + 1]))
            dve.tensor_copy(raw[:, :, D + 4:D + 5], wlr[:, :, 1:2])
            dve.memset(raw[:, :, D + 5:D + 6], 0.0).then_inc(raw_ready, 2)
            split_w("L1", WL[:, :, 0:D + 6 + D], raw[:, :, 0:D + 6 + D], WH[:, :, 0:D + 6 + D])
            split_w("L1r", WrL[:, :, :], wlr[:, :, 0:1].broadcast_to([P, KB, P]), WrH[:, :, :])
            dve.tensor_scalar(F2L[:, :, D:D + 2], onezero[:, :, :], 0.0, None, ALU.mult)
            dve.wait_ge(ld_adj, 16 * NT)
            then(dve.tensor_reduce(colsum, AT[:, :, :], AX.X, ALU.add))
            then(dve.tensor_scalar(colsum, colsum, 1.0, 1e-12, ALU.add, ALU.max))
            then(dve.reciprocal(rcol, colsum))
            pipeline(dve, read(GA["L0"], lambda t, b: dve.tensor_tensor(row(X, t), row(X, t), OUT[b][:, 0:D],
                                                                        ALU.subtract)))
            dve.wait_ge(gather_read, GA["L0"] + NT)
            norm_stats("L1", X)

            def evac_l1(t, b):
                lo(row(FL, t, D + 2), pbank[b][0][:, 0:D + 2], row(FH, t, D + 2))
                lo(row(F2L, t), pbank[b][1][:, 0:D], row(F2H, t))
                return dve.tensor_copy(vab[:, bass.ds(t, 1), :], pbank[b][0][:, D + 2:D + 5])

            pipeline(dve, nothing, turn(PJ["L1"]), evac(PJ["L1"], evac_l1))
            dve.wait_ge(w12_t, 1)
            dve.tensor_copy(raw[0:64, 1, 128:128 + D], TP[0:64, 0:D]).then_inc(w12_c, 1)
            dve.wait_ge(w12_m, 1)
            dve.tensor_copy(W12[:, :, :], TP[:, BANK:BANK + 128].rearrange("p (k n) -> p k n", k=KB)).then_inc(w12_d, 1)

            def read_l1b(t, b):
                dve.tensor_copy(tab[:, bass.ds(t, 1), :], OUT[b][:, D:D + 2])
                return dve.tensor_tensor(row(U1B, t), OUT[b][:, 0:D], bgc[:, :], ALU.add)

            pipeline(dve, read(GA["L1b"], read_l1b))
            dve.wait_ge(gather_read, GA["L1b"] + NT)
            then(dve.tensor_tensor(tab[:, :, :], tab[:, :, :], vab[:, :, 0:2], ALU.add))
            for c in range(2):
                ins = dve.tensor_scalar(tab[:, :, c:c + 1], tab[:, :, c:c + 1], bab[:, c:c + 1], None, ALU.add)
            ins.then_inc(gate_in, 1)
            dve.wait_ge(ld_w, LD["L2a"])
            mark(raw_ready)
            split_w("L2a", WL[:, :, 0:2 * D], raw[:, :, 0:2 * D], WH[:, :, 0:2 * D])
            dve.wait_ge(w_lo, WPREP["L2a"])
            dve.wait_ge(gate_out, 1)
            link = chain(dve_lead, 1)
            link_t = chain(dve_tail, 4)

            def z_l1(t, b):
                wait(dve, strip_hi, GA["L1a"] + t - 1)
                wait(dve, strip_lo, GA["L1a"] + t - 1)
                link(t, 1, dve.tensor_tensor(
                    jrows(l1_strip[b]), SLB[:, cols(t)].rearrange("p (a i) -> p a i", a=1).broadcast_to([P, NT, P]),
                    vab[:, :, 2:3].broadcast_to([P, NT, P]), ALU.add))
                dve.scalar_tensor_tensor(out=l1_strip[b], in0=l1_strip[b], scalar=SLOPE, in1=l1_strip[b],
                                         op0=ALU.mult, op1=ALU.max).then_inc(scored_z, 1)

            def mask_l1(t, b):
                wait(dve, e_raw, t + 1)
                dve.scalar_tensor_tensor(out=jrows(l1_strip[b]), in0=AT[:, :, cols(t)], scalar=0.0,
                                         in1=jrows(l1_strip[b]), op0=ALU.not_equal, op1=ALU.mult).then_inc(masked, 1)

            def read_l1a(t, b):
                link_t(t, 1, dve.tensor_scalar(one(den, t), OUT[b][:, D:D + 1], 1e-5, None, ALU.add))
                link_t(t, 2, dve.reciprocal(one(rden, t), one(den, t)))
                link_t(t, 3, dve.tensor_tensor(one(ra, t), one(rden, t), tab[:, bass.ds(t, 1), 0], ALU.mult))
                link_t(t, 4, dve.tensor_scalar(row(U1B, t), row(U1B, t), tab[:, bass.ds(t, 1), 1], None, ALU.mult))
                return dve.scalar_tensor_tensor(out=row(U1B, t), in0=OUT[b][:, 0:D], scalar=one(ra, t), in1=row(U1B, t),
                                                op0=ALU.mult, op1=ALU.add)

            pipeline(dve, z_l1, mask_l1, read(GA["L1a"], read_l1a))

            link_x = chain(dve_mid, 1)

            def add_l1(t):
                dve.wait_ge(sig_out, t + 1)
                link_x(t, 1, dve.tensor_tensor(row(X, t), row(X, t), row(U1B, t), ALU.add))

            each_tile(dve, add_l1)
            norm_stats("L2", X)
            for b in range(2):
                ins = dve.memset(expt[b][:, N:NP], 0.0)
            ins.then_inc(pads, 1)
            mark(x_l1)

            for name in ("L2a", "L2b"):
                last = name == "L2b"
                if last:
                    dve.wait_ge(gather_read, GA["L2a"] + NT)
                    dve.wait_ge(ld_w, LD["L2b"])
                    mark(raw_ready)
                    split_w("L2b", WL[:, :, 0:2 * D], raw[:, :, 0:2 * D], WH[:, :, 0:2 * D])

                def evac_l2(t, b):
                    lo(row(FL, t), pbank[b][0][:, 0:D], row(FH, t))
                    return lo(TL[:, :, cols(t)], pbank[b][1].rearrange("p (k i) -> p k i", k=4), TH[:, :, cols(t)])

                pipeline(dve, nothing, turn(PJ[name]), evac(PJ[name], evac_l2))

                def top(t, b):
                    wait(dve, scored, SCO[name] + t + 1)
                    dve.tensor_reduce(one(nmax, t), SC[:, 0:N], AX.X, ALU.max, negate=True).then_inc(maxed, 1)

                def mask(t, b):
                    wait(dve, strip_turned, SCO[name] + t + 1)
                    wait(dve, strip_hi, GA[name] + t)
                    wait(dve, strip_lo, GA[name] + t)
                    dve.tensor_tensor(strip, TPS, AT[:, :, cols(t)], ALU.mult).then_inc(masked, 1)

                link2 = chain(dve_tail, 3 if last else 2)

                def read_l2(t, b):
                    wait(dve, exped, SCO[name] + t + 1)
                    link2(t, 1, dve.reciprocal(one(rz, t), one(zsum, t)))
                    link2(t, 2, dve.scalar_tensor_tensor(out=vrow[:, :], in0=OUT[b][:, 0:D], scalar=one(rz, t),
                                                         in1=row(H, t), op0=ALU.mult, op1=ALU.add))
                    ins = dve.scalar_tensor_tensor(out=row(H, t), in0=vrow[:, :], scalar=SLOPE, in1=vrow[:, :],
                                                   op0=ALU.mult, op1=ALU.max)
                    if last:
                        link2(t, 3, ins)
                        ins = dve.tensor_tensor(row(X, t), row(X, t), row(H, t), ALU.add)
                    return ins

                pipeline(dve, top, mask, read(GA[name], read_l2))
            dve.wait_ge(gather_read, GA["L2b"] + NT)
            norm_stats("L3", X)
            link_i = chain(dve_mid, 1)
            for t in range(NT):
                then(dve.tensor_tensor(AT[:, t, t * P:(t + 1) * P], AT[:, t, t * P:(t + 1) * P], ident[:, :], ALU.add))
            dve.tensor_scalar(FL[:, :, D:D + 2], onezero[:, :, :], 0.0, None, ALU.mult).then_inc(adj_plus, 1)

            def lo_h(t):
                dve.wait_ge(f_hi, t + 1)
                link_i(t, 1, lo(row(FL, t), row(H, t), row(FH, t)))

            each_tile(dve, lo_h)
            mark(adj_plus)
            dve.wait_ge(ld_w, LD["L3s"])
            mark(raw_ready)

            def read_l3s(t, b):
                dve.tensor_copy(one(rowsum, t), OUT[b][:, D:D + 1])
                return dve.tensor_copy(row(UG, t), OUT[b][:, 0:D])

            pipeline(dve, read(GA["L3s"], read_l3s))
            dve.wait_ge(gather_read, GA["L3s"] + NT)
            then(dve.tensor_scalar(rowsum, rowsum, 1e-12, None, ALU.max))
            dve.reciprocal(rrow, rowsum).then_inc(gate_in, 1)
            split_w("L3s", WL[:, :, 0:2 * D], raw[:, :, 0:2 * D], WH[:, :, 0:2 * D])
            dve.wait_ge(ld_w, LD["L3u"])
            dve.wait_ge(gate_in, 2)
            mark(raw_ready)
            split_w("L3u", VL[:, :, :], raw[:, :, 0:2 * D], VH[:, :, :])
            link_s = chain(dve_tail, 1)

            def evac_l3s(t, b):
                dve.scalar_tensor_tensor(out=row(FL, t), in0=pbank[b][1][:, 0:D], scalar=one(rrow, t),
                                         in1=row(FH, t).bitcast(F32), op0=ALU.mult, op1=ALU.subtract)
                dve.scalar_tensor_tensor(out=row(G2L, t), in0=pbank[b][1][:, D:2 * D], scalar=one(rcol, t),
                                         in1=row(G2H, t).bitcast(F32), op0=ALU.mult, op1=ALU.subtract)
                link_s(t, 1, dve.scalar_tensor_tensor(out=row(Y, t), in0=pbank[b][0][:, 0:D], scalar=one(rrow, t),
                                                      in1=row(H, t), op0=ALU.mult, op1=ALU.add))
                return dve.scalar_tensor_tensor(out=row(Y, t), in0=pbank[b][0][:, D:2 * D], scalar=one(rcol, t),
                                                in1=row(Y, t), op0=ALU.mult, op1=ALU.add)

            pipeline(dve, nothing, turn(PJ["L3s"]), evac(PJ["L3s"], evac_l3s))
            dve.wait_ge(proj_read, PJ["L3s"] + NT)
            link_t3 = chain(dve_tail, 1)

            def read_l3t(t, b):
                link_t3(t, 1, dve.scalar_tensor_tensor(out=row(Y, t), in0=OUT[b][:, 0:D], scalar=one(rrow, t),
                                                       in1=row(Y, t), op0=ALU.mult, op1=ALU.add))
                return dve.scalar_tensor_tensor(out=row(Y, t), in0=OUT[b][:, D:2 * D], scalar=one(rcol, t),
                                                in1=row(Y, t), op0=ALU.mult, op1=ALU.add)

            pipeline(dve, read(GA["L3t"], read_l3t))
            dve.wait_ge(gather_read, GA["L3t"] + NT)
            dve.wait_ge(ld_w, LD["L3q"])
            dve.tensor_copy(raw[:, :, 0:64], W12[:, :, :])
            dve.memset(raw[:, :, 64:128], 0.0)
            dve.memset(raw[:, :, 192:256], 0.0).then_inc(raw_ready, 1)
            split_w("L3q", VQL[:, :, :], raw[:, :, 0:D], VQH[:, :, :])

            def evac_l3q(t, b):
                lo(row(FL, t), row(H, t), row(FH, t))
                return lo(TQL[:, :, cols(t)], pbank[b][0][:, 0:D].rearrange("p (k i) -> p k i", k=2), TQH[:, :, cols(t)])

            pipeline(dve, nothing, turn(PJ["L3q"]), evac(PJ["L3q"], evac_l3q))

            for name in ("A0", "A1"):
                def top_a(t, b):
                    wait(dve, scored, SCO[name] + t + 1)
                    dve.tensor_reduce(one(nmax, t), [SC, TP][b][:, 0:N], AX.X, ALU.max, negate=True).then_inc(maxed, 1)

                pipeline(dve, top_a)
                dve.wait_ge(exped, SCO[name] + NT)
                n = int(name == "A1")
                dve.tensor_scalar(target, zsum, P_NUC, None, ALU.mult)
                for kt in kept_t:
                    ins = dve.memset(kt[:, N:NP], 0.0)
                then(ins)

                def search(s, turns, base, own):
                    dve.memset(cut.bitcast(U32), BASE_BITS).then_inc(s, 1)
                    dve.memset(bits.bitcast(U32), 1 << TOP_BIT).then_inc(s, 1)
                    dve.wait_ge(s, base + 2)
                    steps = own + (7 if own < NT else 5)

                    with dve.Fori(0, turns, 1) as i:
                        done = [0]

                        def counted(ins):
                            ins.then_inc(s, 1)
                            done[0] += 1
                            return done[0]

                        def reached(k):
                            dve.wait_ge(s, i * steps + (base + 2 + k))

                        reached(counted(dve.tensor_tensor(cand.bitcast(U32), cut.bitcast(U32), bits.bitcast(U32),
                                                          ALU.bitwise_or)))
                        if own < NT:
                            dve.tensor_scalar(nudged, cand, -(1.0 - 2.0 ** -20), None,
                                              ALU.mult).then_inc(cand_ready, 1)
                        first = done[0]
                        for t in range(own):
                            if t >= 2:
                                reached(first + t - 1)
                            last = counted(dve.scalar_tensor_tensor(
                                out=kept_t[t % 2][:, 0:N], in0=E[:, t, :], scalar=cand[:, t:t + 1], in1=E[:, t, :],
                                op0=ALU.is_ge, op1=ALU.mult, accum_out=mass[:, t:t + 1]))
                        counted(dve.tensor_single_scalar(bits.bitcast(U32), bits.bitcast(U32), 1,
                                                         ALU.logical_shift_right))
                        if own < NT:
                            dve.wait_ge(act_step, i * (2 * ACT_TILES) + ((n * COARSE_BITS + 1) * 2 * ACT_TILES))
                            reached(counted(dve.scalar_tensor_tensor(
                                out=acc[:, own:], in0=sign_sum[:, own:], scalar=float(N), in1=nudged[:, own:],
                                op0=ALU.add, op1=ALU.mult)))
                            last = counted(dve.scalar_tensor_tensor(
                                out=mass[:, own:], in0=acc[:, own:], scalar=-0.5, in1=relu_sum[:, own:],
                                op0=ALU.mult, op1=ALU.add))
                        reached(last)
                        reached(counted(dve.tensor_tensor(keep, mass, target, ALU.is_ge)))
                        reached(counted(dve.tensor_tensor(cand, cand, keep, ALU.mult)))
                        reached(counted(dve.tensor_tensor(cut, cut, cand, ALU.max)))
                        assert done[0] == steps
                    return 2 + steps * turns

                seq[0] += search(dve_seq, COARSE_BITS, seq[0], DVE_TILES)
                then(dve.tensor_single_scalar(upper.bitcast(U32), cut.bitcast(U32),
                                              (1 << (TOP_BIT + 1 - COARSE_BITS)) - 1, ALU.bitwise_or))
                start = seq[0]

                def below_upper(t):
                    if t >= 2:
                        dve.wait_ge(dve_seq, start + 2 * t - 1)
                    dve.scalar_tensor_tensor(out=kept_t[t % 2][:, 0:N], in0=E[:, t, :], scalar=upper[:, t:t + 1],
                                             in1=E[:, t, :], op0=ALU.is_le, op1=ALU.mult,
                                             accum_out=below[:, t:t + 1]).then_inc(dve_seq, 1)

                below_upper(0)
                for t in range(NT):
                    if t + 1 < NT:
                        below_upper(t + 1)
                    dve.wait_ge(dve_seq, start + max(2 * t, 1))
                    dve.max(top8[:, 0, t, :], kept_t[t % 2][:, 0:N]).then_inc(dve_seq, 1)
                seq[0] += 2 * NT
                dve.wait_ge(dve_seq, seq[0])
                t8, c8, x8 = (top8[:, k, :, :] for k in range(3))

                def wide(a):
                    return a.rearrange("p (t o) -> p t o", o=1).broadcast_to([P, NT, 8])

                then(dve.tensor_tensor(above, zsum, below, ALU.subtract))
                then(dve.tensor_tensor(c8[:, :, 0], above, t8[:, :, 0], ALU.add))
                for k in range(1, 8):
                    then(dve.tensor_tensor(c8[:, :, k], c8[:, :, k - 1], t8[:, :, k], ALU.add))
                then(dve.tensor_tensor(x8, c8, wide(target), ALU.is_ge))
                then(dve.tensor_tensor(x8, x8, t8, ALU.mult))
                then(dve.tensor_reduce(vcut, x8, AX.X, ALU.max))
                then(dve.tensor_tensor(vcut, vcut, t8[:, :, 7], ALU.max))
                then(dve.tensor_tensor(x8, t8, wide(vcut), ALU.is_gt))
                then(dve.tensor_tensor(x8, x8, t8, ALU.mult))
                then(dve.tensor_reduce(acc, x8, AX.X, ALU.add))
                then(dve.tensor_tensor(above, above, acc, ALU.add))

                def mark_ties(s):
                    for t in range(NT):
                        dve.tensor_scalar(EQ[:, t, :], E[:, t, :], vcut[:, t:t + 1], 0.0, ALU.is_equal, ALU.add,
                                          accum_out=ties[:, t:t + 1]).then_inc(s, 1)

                def raise_flag(k, flag):
                    then(dve.tensor_reduce(flags[:, k:k + 1], flag, AX.X, ALU.max))
                    mark(flag_ready)
                    dve.wait_ge(flag_sum, 2 * n + k + 1)
                    then(dve.tensor_copy(flag_i[:, k:k + 1], OUT[0][0:1, k:k + 1]))
                    return dve.value_load(flag_i[0:1, k:k + 1], min_val=0, max_val=P)

                mark_ties(dve_seq)
                seq[0] += NT
                dve.wait_ge(dve_seq, seq[0])
                then(dve.tensor_tensor(acc, vcut, ties, ALU.mult))
                then(dve.tensor_tensor(acc, acc, above, ALU.add))
                then(dve.tensor_tensor(flag_a, acc, target, ALU.is_lt))
                then(dve.tensor_tensor(flag_b, above, target, ALU.is_ge))
                then(dve.tensor_tensor(flag_a, flag_a, flag_b, ALU.max))
                unsettled = raise_flag(0, flag_a)
                with dve.If(unsettled >= 1):
                    g = general[name]
                    b1 = search(g, SEARCH_BITS, 0, NT)
                    dve.tensor_copy(vcut, cut).then_inc(g, 1)
                    dve.wait_ge(g, b1 + 1)
                    for t in range(NT):
                        if t >= 2:
                            dve.wait_ge(g, b1 + 1 + t - 1)
                        dve.scalar_tensor_tensor(out=kept_t[t % 2][:, 0:N], in0=E[:, t, :], scalar=vcut[:, t:t + 1],
                                                 in1=E[:, t, :], op0=ALU.is_gt, op1=ALU.mult,
                                                 accum_out=above[:, t:t + 1]).then_inc(g, 1)
                    mark_ties(g)
                    dve.wait_ge(g, b1 + 1 + 2 * NT)
                then(dve.reciprocal(acc, vcut))
                then(dve.tensor_tensor(qlim, target, above, ALU.subtract))
                then(dve.tensor_tensor(qlim, qlim, acc, ALU.mult))
                then(dve.tensor_scalar(qlim, qlim, 1.0, None, ALU.add))
                then(dve.tensor_tensor(flag_a, ties, qlim, ALU.is_ge))
                partly = raise_flag(1, flag_a)
                with dve.If(partly >= 1):
                    ts = tie_step[name]
                    for t in range(NT):
                        dve.tensor_tensor_scan(kept_t[0][:, 0:N], EQ[:, t, :], EQ[:, t, :], 0.0, ALU.add,
                                               ALU.max).then_inc(ts, 1)
                        dve.wait_ge(ts, 3 * t + 1)
                        dve.scalar_tensor_tensor(out=kept_t[1][:, 0:N], in0=kept_t[0][:, 0:N], scalar=qlim[:, t:t + 1],
                                                 in1=EQ[:, t, :], op0=ALU.is_ge, op1=ALU.mult).then_inc(ts, 1)
                        dve.wait_ge(ts, 3 * t + 2)
                        dve.scalar_tensor_tensor(out=E[:, t, :], in0=kept_t[1][:, 0:N], scalar=-2.0, in1=E[:, t, :],
                                                 op0=ALU.mult, op1=ALU.add).then_inc(ts, 1)
                        dve.wait_ge(ts, 3 * t + 3)
                then(tick())

                def keep_e(t, b):
                    wait(dve, strip_turned, SCO[name] + t - 1)
                    dve.scalar_tensor_tensor(out=kept_t[b][:, 0:N], in0=E[:, bass.ds(t, 1), :], scalar=one(vcut, t),
                                             in1=E[:, bass.ds(t, 1), :], op0=ALU.is_ge, op1=ALU.mult,
                                             accum_out=one(zkept, t)).then_inc(kept, 1)

                def lo_turned(t, b):
                    wait(dve, strip_hi, GA[name] + t + 1)
                    wait(dve, gathered, GA[name] + t - 1)
                    lo(SL[:, b, :, :], TPS, SH[:, b, :, :]).then_inc(strip_lo, 1)

                link_a = chain(dve_tail, 1)

                def read_a(t, b):
                    wait(dve, kept, KEEP[name] + t + 1)
                    link_a(t, 1, dve.reciprocal(one(rkept, t), one(zkept, t)))
                    if name == "A0":
                        return dve.tensor_scalar(row(UA, t), OUT[b][:, 0:D], one(rkept, t), None, ALU.mult)
                    return dve.scalar_tensor_tensor(out=row(Y, t), in0=OUT[b][:, 0:D], scalar=one(rkept, t),
                                                    in1=row(Y, t), op0=ALU.mult, op1=ALU.add)

                pipeline(dve, keep_e, lo_turned, read(GA[name], read_a))
                dve.wait_ge(gather_read, GA[name] + NT)
                if name == "A0":
                    dve.wait_ge(ld_w, LD["L3a"])
                    mark(raw_ready)
                    split_w("L3a", WL[:, :, 0:2 * D], raw[:, :, 0:2 * D], WH[:, :, 0:2 * D])

                    def evac_l3a(t, b):
                        lo(row(FL, t), pbank[b][0][:, D:2 * D], row(FH, t))
                        lo(TQL[:, :, cols(t)], pbank[b][1][:, 0:D].rearrange("p (k i) -> p k i", k=2),
                           TQH[:, :, cols(t)])
                        return dve.tensor_tensor(row(Y, t), row(Y, t), pbank[b][0][:, 0:D], ALU.add)

                    pipeline(dve, nothing, turn(PJ["L3a"]), evac(PJ["L3a"], evac_l3a))
            norm_stats("end", Y)
            dve.wait_ge(ld_late, 32)
            link_f = chain(dve_tail, 2)

            def final(t):
                dve.wait_ge(fin_a, t + 1)
                link_f(t, 1, dve.tensor_tensor(row(Y, t), row(Y, t), gam[:, :], ALU.mult))
                dve.tensor_tensor(row(X, t), row(X, t), bet[:, :], ALU.add)
                link_f(t, 2, tick())
                dve.tensor_tensor(row(Y, t), row(Y, t), row(X, t), ALU.add).then_inc(fin, 1)

            each_tile(dve, final)


_ORDER = ["x", "adjT", "L0_gnn_weight", "L0_gnn_learnable_diag_1", "L0_gnn_bias", "L1_gnn_W_sa", "L1_gnn_a_sa",
          "L1_gnn_W_gcnb", "L1_gnn_b_gcnb", "L1_gnn_Wa", "L1_gnn_ba", "L1_gnn_Wb", "L1_gnn_bb", "L2_gnn_W_stack",
          "L3_gnn_W1", "L3_gnn_W2", "L3_gnn_W3", "L3_gnn_U1", "L3_gnn_U2", "L3_gnn_U3", "L3_gnn_gamma", "L3_gnn_beta"]


def kernel(**inputs):
    import numpy as _np
    import concourse.bacc as _bacc
    from concourse import mybir as _mybir
    from concourse.bass_utils import run_bass_kernel_spmd as _run

    inputs = dict(inputs)
    x, adj = _np.asarray(inputs.pop("x")), _np.asarray(inputs.pop("adj"))
    inputs["x"] = _np.zeros((NP, D), x.dtype)
    inputs["x"][:N] = x
    inputs["adjT"] = _np.zeros((NP, NP), adj.dtype)
    inputs["adjT"][:N, :N] = adj.T
    nc = _bacc.Bacc("TRN2", target_bir_lowering=False, num_devices=1)
    arrays, args = {}, []
    for name in _ORDER:
        a = _np.ascontiguousarray(inputs[name])
        arrays[f"in_{name}"] = a
        args.append(nc.dram_tensor(f"in_{name}", a.shape, _mybir.dt.from_np(a.dtype), kind="ExternalInput").ap())
    args.append(nc.dram_tensor("out_rows", (N, D), _mybir.dt.float32, kind="ExternalOutput").ap())
    build(nc, *args)
    r = _run(nc, [arrays], core_ids=[0])
    return r.results[0]["out_rows"]
```

```python
from contextlib import ExitStack

import concourse.bass as bass
from concourse import mybir

F32 = mybir.dt.float32
F32R = mybir.dt.float32r
U32 = mybir.dt.uint32
ALU = mybir.AluOpType
ACT = mybir.ActivationFunctionType
AX = mybir.AxisListType

P = 128
N = 1354
NT = -(-N // P)
NP = NT * P
D = 256
KB = D // P
BANK = 512
CHUNKS = [(c, min(BANK, N - c)) for c in range(0, N, BANK)]
LN_EPS = 1e-5
SLOPE = 0.01
P_NUC = 0.9
SIG_PIECES = [(0, 4), (4, 8), (8, NT)]
BASE_BITS = 0x38000000
TOP_BIT = 26
SEARCH_BITS = 27
COARSE_BITS = 14
ACT_TILES = 4
DVE_TILES = NT - ACT_TILES

PJ = {name: NT * k for k, name in enumerate(["L0", "L1", "L2a", "L2b", "L3s", "L3q", "L3a"])}
GA = {name: NT * k for k, name in enumerate(["L0", "L1b", "L1a", "L2a", "L2b", "L3s", "L3t", "A0", "A1"])}
SCO = {name: NT * k for k, name in enumerate(["L2a", "L2b", "A0", "A1"])}
MSK = {name: NT * k for k, name in enumerate(["L1a", "L2a", "L2b"])}
KEEP = {name: NT * k for k, name in enumerate(["A0", "A1"])}
WPREP = {name: k + 1 for k, name in enumerate(["L0", "L1", "L1r", "L2a", "L2b", "L3s", "L3u", "L3q", "L3a"])}
NORM = {name: k + 1 for k, name in enumerate(["L0", "L1", "L2", "L3", "end"])}


def wait(eng, sem, value):
    if isinstance(value, int) and value <= 0:
        return
    eng.wait_ge(sem, value)


def pipeline(eng, *steps, peel=3):
    def turn(t, parity, static):
        for lag, step in steps:
            if static and not 0 <= t - lag < NT:
                continue
            step(t - lag, (parity + lag) % 2)

    for t in range(peel):
        turn(t, t % 2, True)
    with eng.Fori(peel, NT - 1, 2) as t:
        turn(t, 1, False)
        turn(t + 1, 0, False)
    for t in range(NT, NT + max(lag for lag, _ in steps)):
        turn(t, t % 2, True)


def each_tile(eng, step):
    with eng.Fori(0, NT, 1) as t:
        step(t)


def build(nc, x, adjT, w0, d0, b0, w_sa, a_sa, w_gc, b_gc, wa, ba, wb, bb, w_l2, w1, w2, w3, u1, u2, u3, gamma,
          beta, out):
    with ExitStack() as ctx:
        def sb(name, shape, dt=F32, at=ctx):
            return at.enter_context(nc.sbuf_tensor(name, shape, dt))

        def sem(name):
            return ctx.enter_context(nc.semaphore(name))

        X = sb("x_rows", [P, NT, D])
        H = sb("h_rows", [P, NT, D])
        Y = sb("y_rows", [P, NT, D])
        FH = sb("feat_hi", [P, NT, D + 2], F32R)
        FL = sb("feat_lo", [P, NT, D + 2], F32R)
        SH = sb("strip_hi_buf", [P, 2, NT, P], F32R)
        SL = sb("strip_lo_buf", [P, 2, NT, P], F32R)
        TMP = sb("tmp", [P, NP])
        WH = sb("w_hi_buf", [P, KB, 520], F32R)
        WL = sb("w_lo_buf", [P, KB, 520], F32R)
        W12 = sb("w12", [P, KB, 64])
        ident = sb("ident", [P, P])
        onezero = sb("onezero", [P, NT, 2])
        ticks = sb("ticks", [P, 40])
        bcast = sb("bcast", [P, D])
        stats = sb("stats", [P, NT, 6])
        mv = sb("mean_var", [P, NT, 2])
        var = sb("var_eps", [P, NT])
        std = sb("std", [P, NT])
        rstd = sb("rstd", [P, NT])
        nmr = sb("neg_mean_rstd", [P, NT])
        small = sb("small", [P, 36, NT])
        nmax, zsum, rz, rowsum, rrow, colsum, rcol = (small[:, k, :] for k in range(7))
        cut, mass, bits, cand, keep, zkept, rkept, target = (small[:, 7 + k, :] for k in range(8))
        den, rden, ra, rowsc, colsc = (small[:, 15 + k, :] for k in range(5))
        nudged, relu_sum, sign_sum, upper, below, above, vcut, ties, qlim, flag_a, flag_b, acc = (
            small[:, 20 + k, :] for k in range(12))
        top8 = sb("top8", [P, 3, NT, 8])
        flags = sb("flags", [P, 2])
        flag_i = sb("flag_int", [1, 2], U32)
        vab = sb("vab", [P, NT, 3])
        tab = sb("tab", [P, NT, 2])
        bab = sb("bab", [P, 2])
        d1 = sb("d1", [P, KB])
        hT_H = SH[:, :, 0:KB, :]
        hT_L = SL[:, :, 0:KB, :]
        rows_in = TMP[:, 0:2 * D].rearrange("p (b d) -> p b d", b=2)
        raw = TMP[:, 0:KB * 520].rearrange("p (k n) -> p k n", k=KB)
        strip = TMP[:, :].rearrange("p (j i) -> p j i", j=NT)
        l1_strip = [Y[:, :, :].rearrange("p t d -> p (t d)")[:, b * NP:(b + 1) * NP] for b in range(2)]
        expt = [Y[:, :, :].rearrange("p t d -> p (t d)")[:, b * NP:(b + 1) * NP] for b in range(2)]

        with ExitStack() as scope:
            AT = sb("adj_t", [P, NT, NP], F32, scope)
            with ExitStack() as s1:
                F2H = sb("feat2_hi", [P, NT, D + 2], F32R, s1)
                F2L = sb("feat2_lo", [P, NT, D + 2], F32R, s1)
                SLB = sb("s_left", [P, NP], F32, s1)
                WrH = sb("w_left_hi", [P, KB, P], F32R, s1)
                WrL = sb("w_left_lo", [P, KB, P], F32R, s1)
                wlr = sb("w_left_right", [P, KB, 2], F32, s1)
                abc = sb("a_bcast", [P, 2 * D], F32, s1)
                bgc = sb("b_gcnb_bcast", [P, D], F32, s1)
                junk = sb("junk", [P, D], F32, s1)
                U1B = sb("u_rows_l1", [P, NT, D], F32, s1)
            with ExitStack() as s2:
                TH = sb("whs_t_hi", [P, 4, NP], F32R, s2)
                TL = sb("whs_t_lo", [P, 4, NP], F32R, s2)
                QH = sb("q_hi", [P, 2, KB, P], F32R, s2)
                QL = sb("q_lo", [P, 2, KB, P], F32R, s2)
                vrow = sb("vrow", [P, D], F32, s2)
            with ExitStack() as s3:
                G2H = sb("feat3_hi", [P, NT, D], F32R, s3)
                G2L = sb("feat3_lo", [P, NT, D], F32R, s3)
                UG = sb("u_rows_l3", [P, NT, D], F32, s3)
                VH = sb("v_hi", [P, KB, BANK], F32R, s3)
                VL = sb("v_lo", [P, KB, BANK], F32R, s3)
        with ExitStack() as scope:
            E = sb("e_rows", [P, NT, N], F32, scope)
            with ExitStack() as s4:
                TQH = sb("qk_t_hi", [P, 2, NP], F32R, s4)
                TQL = sb("qk_t_lo", [P, 2, NP], F32R, s4)
            with ExitStack() as s5:
                EQ = sb("is_tie", [P, NT, N], mybir.dt.uint8, s5)
            hold = sb("qk_hold", [P, 4 * NP], F32, scope)
            AQH = sb("aq_hi", [P, 2, P], F32R, scope)
            AQL = sb("aq_lo", [P, 2, P], F32R, scope)
            VQH = sb("wqk_hi", [P, KB, D], F32R, scope)
            VQL = sb("wqk_lo", [P, KB, D], F32R, scope)
            UA = sb("u_rows_a", [P, NT, D], F32, scope)
            ET2 = sb("kept_tile", [P, NP], F32, scope)
            gam = sb("gamma_bcast", [P, D], F32, scope)
            bet = sb("beta_bcast", [P, D], F32, scope)
        kept_t = [TMP[:, :], ET2[:, :]]

        SC = ctx.enter_context(nc.psum_tensor("scores", [P, 3 * BANK], F32))
        TP = ctx.enter_context(nc.psum_tensor("turned_ps", [P, 3 * BANK], F32))
        OUT = [ctx.enter_context(nc.psum_tensor(f"out{b}", [P, BANK], F32)) for b in range(2)]
        pbank = [[SC[:, 0:BANK], SC[:, BANK:2 * BANK], SC[:, 2 * BANK:]],
                 [OUT[0][:, :], OUT[1][:, :], TP[:, 2 * BANK:]]]
        TPS = TP[:, 0:NP].rearrange("p (j i) -> p j i", j=NT)

        ld_x, ld_adj, ld_small, ld_l1, ld_w, ld_late, stored = (sem(n) for n in (
            "ld_x", "ld_adj", "ld_small", "ld_l1", "ld_w", "ld_late", "stored"))
        consts = sem("consts")
        d_made = sem("d_made")
        raw_ready = sem("raw_ready")
        w_hi, w_lo = sem("w_hi"), sem("w_lo")
        w12_t, w12_c, w12_m, w12_d = (sem(n) for n in ("w12_t", "w12_c", "w12_m", "w12_d"))
        var_ready, std_ready, norm_ready = sem("var_ready"), sem("std_ready"), sem("norm_ready")
        h_rows = sem("h_made")
        staged = sem("rows_staged")
        turned = sem("rows_turned")
        turn_hi, turn_lo = sem("turn_hi"), sem("turn_lo")
        projected = sem("projected")
        proj_hi, proj_read = sem("proj_hi"), sem("proj_read")
        strip_hi, strip_lo = sem("strip_hi"), sem("strip_lo")
        gathered, gather_read = sem("gathered"), sem("gather_read")
        q_staged, scored, maxed, exped = (sem(n) for n in ("q_staged", "scored", "maxed", "exped"))
        strip_turned, masked, kept = sem("strip_turned"), sem("masked"), sem("kept")
        scored_z, e_raw = sem("lrelu_made"), sem("e_raw")
        gate_in, gate_out = sem("gate_in"), sem("gate_out")
        sig_out, x_l1 = sem("sig_out"), sem("x_l1")
        adj_plus = sem("adj_plus")
        cand_ready, act_mass, act_step = sem("cand_ready"), sem("act_mass"), sem("act_step")
        flag_ready, flag_sum = sem("flag_ready"), sem("flag_sum")
        general = {name: sem(f"general_{name}") for name in KEEP}
        tie_step = {name: sem(f"tie_step_{name}") for name in KEEP}
        pads = sem("pads")
        fin = sem("final_rows")
        dve_lead, dve_mid, dve_tail, dve_seq = (sem(n) for n in ("dve_lead", "dve_mid", "dve_tail", "dve_seq"))
        fin_a = sem("final_scaled")

        block = ctx.enter_context(nc.Block())

        def w_rows(w):
            return w.rearrange("(k p) n -> p k n", p=P)

        def jrows(tile):
            return tile[:, 0:NP].rearrange("p (j i) -> p j i", j=NT)

        def cols(t):
            return bass.ds(t * P, P)

        @block.sync
        def _(sp):
            sp.dma_start(X[:, :, :], x.rearrange("(t p) d -> p t d", p=P)).then_inc(ld_x, 16)
            sp.dma_start(d1[:, :], d0.rearrange("(k p) -> p k", p=P), allow_slow_non_contiguous=True).then_inc(ld_small, 16)
            sp.dma_start(bcast[:, :], b0.rearrange("(a n) -> a n", a=1).broadcast_to([P, D])).then_inc(ld_small, 16)
            sp.dma_start(raw[:, :, 0:D], w_rows(w0)).then_inc(ld_w, 16)
            for t in range(NT):
                sp.dma_start(AT[:, t, :], adjT[t * P:(t + 1) * P, :]).then_inc(ld_adj, 16)
            sp.dma_start(abc[:, :], a_sa.broadcast_to([P, 2 * D])).then_inc(ld_l1, 16)
            sp.dma_start(bgc[:, :], b_gc.rearrange("(a n) -> a n", a=1).broadcast_to([P, D])).then_inc(ld_l1, 16)
            sp.dma_start(bab[:, 0:1], ba.rearrange("(a n) -> a n", a=1).broadcast_to([P, 1])).then_inc(ld_l1, 16)
            sp.dma_start(bab[:, 1:2], bb.rearrange("(a n) -> a n", a=1).broadcast_to([P, 1])).then_inc(ld_l1, 16)
            sp.wait_ge(turned, PJ["L0"] + NT)
            sp.dma_start(raw[:, :, 0:D], w_rows(w_gc)).then_inc(ld_w, 16)
            sp.dma_start(raw[:, :, D + 6:D + 6 + D], w_rows(w_sa)).then_inc(ld_w, 16)
            for c, (w, half) in enumerate([(wa, 0), (wb, 0), (wa, 1), (wb, 1)]):
                sp.dma_start(raw[:, :, D + c:D + c + 1],
                             w[0:1, half * D:(half + 1) * D].rearrange("a (k p) -> p k a", p=P),
                             allow_slow_non_contiguous=True).then_inc(ld_w, 16)
            sp.wait_ge(turned, PJ["L1"] + NT)
            sp.dma_start(raw[:, :, 0:64], w_rows(w1)).then_inc(ld_w, 16)
            sp.dma_start(raw[0:64, 0, 64:128], w2).then_inc(ld_w, 16)
            sp.wait_ge(w12_m, 1)
            sp.dma_start(raw[:, :, 0:2 * D], w_rows(w_l2[0])).then_inc(ld_w, 16)
            sp.wait_ge(strip_lo, GA["L2a"] + NT)
            sp.wait_ge(strip_hi, GA["L2a"] + NT)
            sp.dma_start(raw[:, :, 0:2 * D], w_rows(w_l2[1])).then_inc(ld_w, 16)
            sp.wait_ge(strip_lo, GA["L2b"] + NT)
            sp.wait_ge(strip_hi, GA["L2b"] + NT)
            sp.dma_start(raw[:, :, 0:D], w_rows(u1[0])).then_inc(ld_w, 16)
            sp.dma_start(raw[:, :, D:2 * D], w_rows(u2[0])).then_inc(ld_w, 16)
            sp.wait_ge(w_hi, WPREP["L3s"])
            sp.wait_ge(w_lo, WPREP["L3s"])
            sp.dma_start(raw[:, :, 0:D], w_rows(u1[1])).then_inc(ld_w, 16)
            sp.dma_start(raw[:, :, D:2 * D], w_rows(u2[1])).then_inc(ld_w, 16)
            sp.wait_ge(gathered, GA["L3t"] + NT)
            sp.dma_start(raw[:, :, 128:192], w_rows(w3)).then_inc(ld_w, 16)
            sp.dma_start(gam[:, :], gamma.rearrange("(a n) -> a n", a=1).broadcast_to([P, D])).then_inc(ld_late, 16)
            sp.dma_start(bet[:, :], beta.rearrange("(a n) -> a n", a=1).broadcast_to([P, D])).then_inc(ld_late, 16)
            sp.wait_ge(strip_turned, SCO["A0"] + NT)
            sp.dma_start(raw[:, :, 0:D], w_rows(u3[0])).then_inc(ld_w, 16)
            sp.dma_start(raw[:, :, D:2 * D], w_rows(u3[1])).then_inc(ld_w, 16)
            for t in range(NT):
                rows = min(P, N - t * P)
                sp.wait_ge(fin, t + 1)
                sp.dma_start(out[t * P:t * P + rows, :], Y[0:rows, t, :]).then_inc(stored, 16)
            sp.wait_ge(stored, 16 * NT)

        LD = {}
        n = 0
        for name, count in (("L0", 1), ("L1", 6), ("L1r", 2), ("L2a", 1), ("L2b", 1), ("L3s", 2), ("L3u", 2),
                            ("L3q", 1), ("L3a", 2)):
            n += 16 * count
            LD[name] = n

        @block.gpsimd
        def _(pool):
            pool.memset(ident[:, :], 0.0).then_inc(consts, 1)
            pool.memset(onezero[:, :, :], 0.0).then_inc(consts, 1)
            pool.wait_ge(consts, 2)
            pool.affine_select(out=ident[:, :], in_=ident[:, :], compare_op=ALU.not_equal, fill=1.0, base=0,
                               pattern=[[-1, P]], channel_multiplier=1).then_inc(consts, 1)
            pool.memset(onezero[:, :, 0:1], 1.0).then_inc(consts, 1)

            def lo_of_adj(g0):
                def step(t, b):
                    wait(pool, strip_hi, g0 + t + 1)
                    wait(pool, gathered, g0 + t - 1)
                    pool.tensor_tensor(SL[:, b, :, :], AT[:, :, cols(t)], SH[:, b, :, :].bitcast(F32),
                                       ALU.subtract).then_inc(strip_lo, 1)
                return step

            def lo_of_tmp(g0, src):
                def step(t, b):
                    wait(pool, strip_hi, g0 + t + 1)
                    wait(pool, gathered, g0 + t - 1)
                    pool.tensor_tensor(SL[:, b, :, :], jrows(src[b]), SH[:, b, :, :].bitcast(F32),
                                       ALU.subtract).then_inc(strip_lo, 1)
                return step

            def stage_q(s0, kb, src_hi, src_lo, dst_hi, dst_lo):
                def step(t, b):
                    wait(pool, scored, s0 + t - 1)
                    pool.tensor_copy(dst_hi(b), src_hi[:, 0:kb, cols(t)])
                    pool.tensor_copy(dst_lo(b), src_lo[:, 0:kb, cols(t)]).then_inc(q_staged, 1)
                return step

            def q_l2(s0):
                return stage_q(s0, KB, TH, TL, lambda b: QH[:, b, :, :], lambda b: QL[:, b, :, :])

            def q_a(s0):
                return stage_q(s0, 1, TQH, TQL, lambda b: AQH[:, b:b + 1, :], lambda b: AQL[:, b:b + 1, :])

            pool.wait_ge(ld_adj, 16 * NT)
            pool.wait_ge(projected, PJ["L0"] + NT)
            pipeline(pool, (0, lo_of_adj(GA["L0"])))
            pool.wait_ge(projected, PJ["L1"] + NT)
            pipeline(pool, (0, lo_of_adj(GA["L1b"])))
            pipeline(pool, (0, lo_of_tmp(GA["L1a"], l1_strip)))
            for name in ("L2a", "L2b"):
                pool.wait_ge(proj_read, PJ[name] + NT)
                pool.wait_ge(proj_hi, PJ[name] + NT)
                pipeline(pool, (0, q_l2(SCO[name])), (2, lo_of_tmp(GA[name], [TMP, TMP])))
            pool.wait_ge(adj_plus, 1)
            pipeline(pool, (0, lo_of_adj(GA["L3s"])))
            pool.wait_ge(projected, PJ["L3s"] + NT)
            pipeline(pool, (0, lo_of_adj(GA["L3t"])))
            for name, pj in (("A0", "L3q"), ("A1", "L3a")):
                pool.wait_ge(proj_read, PJ[pj] + NT)
                pool.wait_ge(proj_hi, PJ[pj] + NT)
                pipeline(pool, (0, q_a(SCO[name])))

        @block.scalar
        def _(act):
            def split_w(name, dst, src):
                act.wait_ge(raw_ready, WPREP[name])
                act.activation(dst, src, ACT.Copy).then_inc(w_hi, 1)

            def root(name):
                act.wait_ge(var_ready, NORM[name])
                act.activation(std[:, :], var[:, :], ACT.Sqrt).then_inc(std_ready, 1)
                act.wait_ge(norm_ready, NORM[name])

            def stage_norm(p0):
                def step(t, b):
                    wait(act, turned, p0 + t - 1)
                    act.activation(rows_in[:, b:b + 1, :], X[:, bass.ds(t, 1), :], ACT.Relu,
                                   bias=nmr[:, bass.ds(t, 1)], scale=rstd[:, bass.ds(t, 1)]).then_inc(staged, 1)
                return step

            def stage_copy(p0, src):
                def step(t, b):
                    wait(act, turned, p0 + t - 1)
                    act.activation(rows_in[:, b:b + 1, :], src[:, bass.ds(t, 1), :], ACT.Copy).then_inc(staged, 1)
                return step

            def turn(p0):
                def step(t, b):
                    wait(act, turned, p0 + t + 1)
                    wait(act, projected, p0 + t - 1)
                    act.activation(hT_H[:, b, :, :].rearrange("p k i -> p (k i)"),
                                   TP[:, BANK * b:BANK * b + D], ACT.Copy).then_inc(turn_hi, 1)
                return step

            def evac(p0, *parts):
                def step(t, b):
                    wait(act, projected, p0 + t + 1)
                    for k, part in enumerate(parts):
                        ins = part(t, b)
                    ins.then_inc(proj_hi, 1)
                return step

            def project_rows(p0, stage, *parts, peel=3):
                pipeline(act, (0, stage), (1, turn(p0)), (3, evac(p0, *parts)), peel=peel)

            def copy_part(dst, bank, c0, n, scale=None):
                def part(t, b):
                    if scale is None:
                        return act.activation(dst(t), pbank[b][bank][:, c0:c0 + n], ACT.Copy)
                    return act.activation(dst(t), pbank[b][bank][:, c0:c0 + n], ACT.Copy,
                                          scale=scale[:, bass.ds(t, 1)])
                return part

            def hi_of_adj(g0):
                def step(t, b):
                    wait(act, gathered, g0 + t - 1)
                    act.activation(SH[:, b, :, :], AT[:, :, cols(t)], ACT.Copy).then_inc(strip_hi, 1)
                return step

            def hi_of_tmp(g0, m0, src):
                def step(t, b):
                    wait(act, masked, m0 + t + 1)
                    wait(act, gathered, g0 + t - 1)
                    act.activation(SH[:, b, :, :], jrows(src[b]), ACT.Copy).then_inc(strip_hi, 1)
                return step

            def exp_l2(s0):
                def step(t, b):
                    wait(act, maxed, s0 + t + 1)
                    wait(act, strip_turned, s0 + t - 1)
                    act.activation(expt[b][:, 0:N], SC[:, 0:N], ACT.Exp, bias=nmax[:, bass.ds(t, 1)],
                                   accum_out=zsum[:, bass.ds(t, 1)]).then_inc(exped, 1)
                return step

            fh = lambda n: (lambda t: FH[:, t, 0:n] if isinstance(t, int) else FH[:, bass.ds(t, 1), 0:n])

            split_w("L0", WH[:, :, 0:2 * D], raw[:, :, 0:2 * D])
            act.wait_ge(ld_x, 16)
            root("L0")
            act.wait_ge(w_lo, WPREP["L0"])
            project_rows(PJ["L0"], stage_norm(PJ["L0"]), copy_part(lambda t: FH[:, bass.ds(t, 1), 0:D], 0, D, D), peel=5)
            act.wait_ge(projected, PJ["L0"] + NT)
            split_w("L1", WH[:, :, 0:D + 6 + D], raw[:, :, 0:D + 6 + D])
            act.activation(WrH[:, :, :], wlr[:, :, 0:1].broadcast_to([P, KB, P]), ACT.Copy).then_inc(w_hi, 1)
            act.activation(F2H[:, :, D:D + 2], onezero[:, :, :], ACT.Copy)
            act.wait_ge(ld_adj, 16 * NT)
            pipeline(act, (0, hi_of_adj(GA["L0"])))
            act.wait_ge(gathered, GA["L0"] + NT)
            root("L1")
            act.wait_ge(w_lo, WPREP["L1r"])
            project_rows(
                PJ["L1"], stage_norm(PJ["L1"]), copy_part(lambda t: FH[:, bass.ds(t, 1), 0:D + 2], 0, 0, D + 2),
                copy_part(lambda t: F2H[:, bass.ds(t, 1), 0:D], 1, 0, D),
                copy_part(lambda t: SLB[:, cols(t)], 2, 0, P))
            act.wait_ge(projected, PJ["L1"] + NT)
            pipeline(act, (0, hi_of_adj(GA["L1b"])))
            split_w("L2a", WH[:, :, 0:2 * D], raw[:, :, 0:2 * D])
            act.wait_ge(gate_in, 1)
            act.activation(tab[:, :, :], tab[:, :, :], ACT.Sigmoid).then_inc(gate_out, 1)

            def exp_l1(t, b):
                wait(act, scored_z, t + 1)
                act.activation(l1_strip[b], l1_strip[b], ACT.Exp, scale=-1.0).then_inc(e_raw, 1)

            pipeline(act, (0, exp_l1), (1, hi_of_tmp(GA["L1a"], MSK["L1a"], l1_strip)))

            act.wait_ge(gather_read, GA["L1a"] + NT)
            for t0, t1 in SIG_PIECES:
                act.activation(U1B[:, t0:t1, :], U1B[:, t0:t1, :], ACT.Sigmoid).then_inc(sig_out, 1)
            root("L2")
            act.wait_ge(x_l1, 1)

            def norm_h(t):
                act.activation(H[:, bass.ds(t, 1), :], X[:, bass.ds(t, 1), :], ACT.Relu, bias=nmr[:, bass.ds(t, 1)],
                               scale=rstd[:, bass.ds(t, 1)]).then_inc(h_rows, 1)

            each_tile(act, norm_h)
            act.wait_ge(h_rows, NT)
            for name in ("L2a", "L2b"):
                if name == "L2b":
                    split_w("L2b", WH[:, :, 0:2 * D], raw[:, :, 0:2 * D])
                    act.wait_ge(gather_read, GA["L2a"] + NT)
                act.wait_ge(w_lo, WPREP[name])
                act.wait_ge(gathered, GA[name])
                project_rows(
                    PJ[name], stage_copy(PJ[name], H), copy_part(lambda t: FH[:, bass.ds(t, 1), 0:D], 0, 0, D),
                    lambda t, b: act.activation(TH[:, :, cols(t)], pbank[b][1].rearrange("p (k i) -> p k i", k=4),
                                                ACT.Copy))
                act.wait_ge(pads, 1)
                act.wait_ge(projected, PJ[name] + NT)
                pipeline(act, (0, exp_l2(SCO[name])), (1, hi_of_tmp(GA[name], MSK[name], [TMP, TMP])))
            act.wait_ge(gathered, GA["L2b"] + NT)
            root("L3")

            each_tile(act, norm_h)
            act.wait_ge(adj_plus, 1)
            pipeline(act, (0, hi_of_adj(GA["L3s"])))
            split_w("L3s", WH[:, :, 0:2 * D], raw[:, :, 0:2 * D])
            split_w("L3u", VH[:, :, :], raw[:, :, 0:2 * D])
            act.wait_ge(gather_read, GA["L3s"] + NT)
            act.wait_ge(gate_in, 2)
            act.wait_ge(w_lo, WPREP["L3u"])
            project_rows(
                PJ["L3s"], stage_copy(PJ["L3s"], UG), copy_part(lambda t: FH[:, bass.ds(t, 1), 0:D], 1, 0, D, rrow),
                copy_part(lambda t: G2H[:, bass.ds(t, 1), :], 1, D, D, rcol))
            act.wait_ge(projected, PJ["L3s"] + NT)
            pipeline(act, (0, hi_of_adj(GA["L3t"])))
            split_w("L3q", VQH[:, :, :], raw[:, :, 0:D])
            act.wait_ge(gather_read, GA["L3t"] + NT)
            act.wait_ge(w_lo, WPREP["L3q"])
            project_rows(
                PJ["L3q"], stage_copy(PJ["L3q"], H), lambda t, b: act.activation(FH[:, bass.ds(t, 1), 0:D], H[:, bass.ds(t, 1), :], ACT.Copy),
                lambda t, b: act.activation(TQH[:, :, cols(t)],
                                            pbank[b][0][:, 0:D].rearrange("p (k i) -> p k i", k=2), ACT.Copy))

            def exp_a(s0):
                def step(t, b):
                    wait(act, maxed, s0 + t + 1)
                    act.activation(E[:, bass.ds(t, 1), :], [SC, TP][b][:, 0:N], ACT.Exp, bias=nmax[:, bass.ds(t, 1)],
                                   accum_out=zsum[:, bass.ds(t, 1)]).then_inc(exped, 1)
                return step

            def coarse(n):
                out2 = UA[:, :, :].rearrange("p t d -> p (t d)")
                with act.Fori(0, COARSE_BITS, 1) as i:
                    act.wait_ge(cand_ready, i + (n * COARSE_BITS + 1))
                    for k in range(2 * ACT_TILES):
                        t = DVE_TILES + k // 2
                        if k >= 2:
                            act.wait_ge(act_step, i * (2 * ACT_TILES) + (n * COARSE_BITS * 2 * ACT_TILES + k - 1))
                        act.activation(out2[:, (k % 2) * N:(k % 2 + 1) * N], E[:, t, :],
                                       [ACT.Relu, ACT.Sign][k % 2], bias=nudged[:, t:t + 1],
                                       accum_out=[relu_sum, sign_sum][k % 2][:, t:t + 1]).then_inc(act_step, 1)

            def hi_of_turned(g0, s0):
                def step(t, b):
                    wait(act, strip_turned, s0 + t + 1)
                    wait(act, gathered, g0 + t - 1)
                    act.activation(SH[:, b, :, :], TPS, ACT.Copy).then_inc(strip_hi, 1)
                return step

            pipeline(act, (0, exp_a(SCO["A0"])))
            coarse(0)
            act.wait_ge(projected, PJ["L3q"] + NT)
            pipeline(act, (0, hi_of_turned(GA["A0"], SCO["A0"])))
            split_w("L3a", WH[:, :, 0:2 * D], raw[:, :, 0:2 * D])
            act.wait_ge(gather_read, GA["A0"] + NT)
            act.wait_ge(w_lo, WPREP["L3a"])
            project_rows(
                PJ["L3a"], stage_copy(PJ["L3a"], UA), copy_part(lambda t: FH[:, bass.ds(t, 1), 0:D], 0, D, D),
                lambda t, b: act.activation(TQH[:, :, cols(t)],
                                            pbank[b][1][:, 0:D].rearrange("p (k i) -> p k i", k=2), ACT.Copy))
            pipeline(act, (0, exp_a(SCO["A1"])))
            coarse(1)
            act.wait_ge(projected, PJ["L3a"] + NT)
            pipeline(act, (0, hi_of_turned(GA["A1"], SCO["A1"])))
            act.wait_ge(var_ready, NORM["end"])
            act.activation(std[:, :], var[:, :], ACT.Sqrt).then_inc(std_ready, 1)
            act.wait_ge(norm_ready, NORM["end"])

            def last(t):
                act.activation(Y[:, bass.ds(t, 1), :], Y[:, bass.ds(t, 1), :], ACT.Identity,
                               bias=nmr[:, bass.ds(t, 1)], scale=rstd[:, bass.ds(t, 1)]).then_inc(fin_a, 1)

            each_tile(act, last)

        @block.tensor
        def _(pe):
            def turn(p0):
                def step(t, b):
                    wait(pe, staged, p0 + t + 1)
                    wait(pe, turn_hi, p0 + t - 1)
                    wait(pe, turn_lo, p0 + t - 1)
                    for k in range(KB):
                        ins = pe.transpose(TP[:, BANK * b + k * P:BANK * b + (k + 1) * P],
                                           rows_in[:, b, k * P:(k + 1) * P], ident[:, :])
                    ins.then_inc(turned, 1)
                return step

            def rows_times(b, dst, wh, wl, c0, n):
                terms = [(hT_H, wh), (hT_L, wh), (hT_H, wl)]
                for m, (left, right) in enumerate(terms):
                    for k in range(KB):
                        ins = pe.matmul(dst, left[:, b, k, :], right[:, k, c0:c0 + n], start=(m == 0 and k == 0),
                                        stop=(m == 2 and k == KB - 1))
                return ins

            def rows_times_turned(b, dst, wh, wl, c0):
                terms = [(wh, hT_H), (wh, hT_L), (wl, hT_H)]
                for m, (left, right) in enumerate(terms):
                    for k in range(KB):
                        ins = pe.matmul(dst, left[:, k, c0:c0 + P], right[:, b, k, :], start=(m == 0 and k == 0),
                                        stop=(m == 2 and k == KB - 1))
                return ins

            def project(p0, body):
                def step(t, b):
                    wait(pe, turn_lo, p0 + t + 1)
                    wait(pe, turn_hi, p0 + t + 1)
                    wait(pe, proj_read, p0 + t - 1)
                    wait(pe, proj_hi, p0 + t - 1)
                    body(b).then_inc(projected, 1)
                return step

            def project_rows(p0, body, peel=3):
                pipeline(pe, (0, turn(p0)), (2, project(p0, body)), peel=peel)

            def gather(g0, *groups):
                def step(t, b):
                    wait(pe, strip_hi, g0 + t + 1)
                    wait(pe, strip_lo, g0 + t + 1)
                    wait(pe, gather_read, g0 + t - 1)
                    for c0, fh, fl, n in groups:
                        for m, (left, right) in enumerate([(SH, fh), (SL, fh), (SH, fl)]):
                            for j in range(NT):
                                ins = pe.matmul(OUT[b][:, c0:c0 + n], left[:, b, j, :], right[:, j, 0:n],
                                                start=(m == 0 and j == 0), stop=(m == 2 and j == NT - 1))
                    ins.then_inc(gathered, 1)
                return step

            def scores_l2(s0):
                def step(t, b):
                    wait(pe, q_staged, s0 + t + 1)
                    wait(pe, exped, s0 + t)
                    for c, n in CHUNKS:
                        for m, (q, k2) in enumerate([(QH, TH), (QL, TH), (QH, TL)]):
                            for k in range(KB):
                                ins = pe.matmul(SC[:, c:c + n], q[:, b, k, :], k2[:, KB + k, c:c + n],
                                                start=(m == 0 and k == 0), stop=(m == 2 and k == KB - 1))
                    ins.then_inc(scored, 1)
                return step

            def turn_l2(s0, m0):
                def step(t, b):
                    wait(pe, exped, s0 + t + 1)
                    wait(pe, masked, m0 + t)
                    for j in range(NT):
                        ins = pe.transpose(TP[:, j * P:(j + 1) * P], expt[b][:, j * P:(j + 1) * P], ident[:, :])
                    ins.then_inc(strip_turned, 1)
                return step

            def scores_a(s0):
                def step(t, b):
                    wait(pe, q_staged, s0 + t + 1)
                    wait(pe, exped, s0 + t - 1)
                    for c, n in CHUNKS:
                        for m, (q, k2) in enumerate([(AQH, TQH), (AQL, TQH), (AQH, TQL)]):
                            ins = pe.matmul([SC, TP][b][:, c:c + n], q[:, b, :], k2[:, 1, c:c + n], start=(m == 0),
                                            stop=(m == 2))
                    ins.then_inc(scored, 1)
                return step

            def turn_a(s0, k0, g0):
                def step(t, b):
                    wait(pe, kept, k0 + t + 1)
                    wait(pe, strip_hi, g0 + t)
                    wait(pe, strip_lo, g0 + t)
                    for j in range(NT):
                        ins = pe.transpose(TP[:, j * P:(j + 1) * P], kept_t[b][:, j * P:(j + 1) * P], ident[:, :])
                    ins.then_inc(strip_turned, 1)
                return step

            one = (0, FH, FL, D)
            pe.wait_ge(consts, 4)
            pe.wait_ge(w_lo, WPREP["L0"])
            project_rows(PJ["L0"], lambda b: rows_times(b, pbank[b][0], WH, WL, 0, 2 * D), peel=5)
            pe.wait_ge(proj_read, PJ["L0"] + NT)
            pe.wait_ge(proj_hi, PJ["L0"] + NT)
            pipeline(pe, (0, gather(GA["L0"], one)))
            pe.wait_ge(w_lo, WPREP["L1r"])
            pe.wait_ge(gather_read, GA["L0"] + NT)

            def proj_l1(b):
                rows_times(b, pbank[b][0][:, 0:D + 6], WH, WL, 0, D + 6)
                rows_times(b, pbank[b][1][:, 0:D], WH, WL, D + 6, D)
                return rows_times_turned(b, pbank[b][2][:, 0:P], WrH, WrL, 0)

            project_rows(PJ["L1"], proj_l1)
            pe.wait_ge(proj_read, PJ["L1"] + NT)
            pe.wait_ge(proj_hi, PJ["L1"] + NT)
            pe.wait_ge(raw_ready, WPREP["L1r"] + 0)
            pe.wait_ge(ld_w, LD["L1r"])
            for k in range(KB):
                ins = pe.transpose(TP[0:64, k * P:(k + 1) * P], raw[:, k, 0:64], ident[:, :])
            ins.then_inc(w12_t, 1)
            pe.wait_ge(w12_c, 1)
            for k in range(KB):
                ins = pe.matmul(TP[:, BANK + k * 64:BANK + (k + 1) * 64], raw[0:64, 1, 128 + k * P:128 + (k + 1) * P],
                                raw[0:64, 0, 64:128], start=True, stop=True)
            ins.then_inc(w12_m, 1)
            pipeline(pe, (0, gather(GA["L1b"], (0, FH, FL, D + 2))))
            pipeline(pe, (0, gather(GA["L1a"], (0, F2H, F2L, D + 2))))

            def proj_l2(b):
                rows_times(b, pbank[b][0][:, 0:D], WH, WL, 0, D)
                for k in range(4):
                    ins = rows_times_turned(b, pbank[b][1][:, k * P:(k + 1) * P], WH, WL, k * P)
                return ins

            for name in ("L2a", "L2b"):
                pe.wait_ge(w_lo, WPREP[name])
                pe.wait_ge(w12_d, 1)
                pe.wait_ge(gather_read, GA[name])
                pe.wait_ge(masked, MSK[name])
                pe.wait_ge(exped, SCO[name]) if name != "L2a" else None
                project_rows(PJ[name], proj_l2)
                pe.wait_ge(proj_read, PJ[name] + NT)
                pe.wait_ge(proj_hi, PJ[name] + NT)
                pipeline(pe, (0, scores_l2(SCO[name])), (1, turn_l2(SCO[name], MSK[name])), (2, gather(GA[name], one)))
            pe.wait_ge(adj_plus, 2)
            pipeline(pe, (0, gather(GA["L3s"], (0, FH, FL, D + 2))))
            pe.wait_ge(w_lo, WPREP["L3u"])
            pe.wait_ge(gather_read, GA["L3s"] + NT)

            def proj_l3s(b):
                rows_times(b, pbank[b][0], WH, WL, 0, 2 * D)
                return rows_times(b, pbank[b][1], VH, VL, 0, 2 * D)

            project_rows(PJ["L3s"], proj_l3s)
            pe.wait_ge(proj_read, PJ["L3s"] + NT)
            pe.wait_ge(proj_hi, PJ["L3s"] + NT)
            pipeline(pe, (0, gather(GA["L3t"], one, (D, G2H, G2L, D))))
            pe.wait_ge(w_lo, WPREP["L3q"])
            pe.wait_ge(gather_read, GA["L3t"] + NT)

            def proj_qk(b, bank):
                rows_times_turned(b, pbank[b][bank][:, 0:P], VQH, VQL, 0)
                return rows_times_turned(b, pbank[b][bank][:, P:2 * P], VQH, VQL, P)

            def proj_l3a(b):
                rows_times(b, pbank[b][0], WH, WL, 0, 2 * D)
                return proj_qk(b, 1)

            project_rows(PJ["L3q"], lambda b: proj_qk(b, 0))
            for name, pj in (("A0", "L3q"), ("A1", "L3a")):
                pe.wait_ge(proj_read, PJ[pj] + NT)
                pe.wait_ge(proj_hi, PJ[pj] + NT)
                pipeline(pe, (0, scores_a(SCO[name])))
                for k in range(2):
                    pe.wait_ge(flag_ready, 2 * (name == "A1") + k + 1)
                    pe.matmul(OUT[0][0:1, k:k + 1], onezero[:, 0, 0:1], flags[:, k:k + 1], start=True,
                              stop=True).then_inc(flag_sum, 1)
                pipeline(pe, (0, turn_a(SCO[name], KEEP[name], GA[name])), (1, gather(GA[name], one)))
                if name == "A0":
                    pe.wait_ge(w_lo, WPREP["L3a"])
                    pe.wait_ge(gather_read, GA["A0"] + NT)
                    project_rows(PJ["L3a"], proj_l3a)

        @block.vector
        def _(dve):
            seq = [0]

            def then(ins):
                seq[0] += 1
                ins.then_inc(dve_seq, 1)
                dve.wait_ge(dve_seq, seq[0])

            base = {}

            def chain(s, per_tile):
                b0_ = base.get(id(s), 0)
                base[id(s)] = b0_ + NT * per_tile

                def link(t, k, ins):
                    ins.then_inc(s, 1)
                    dve.wait_ge(s, t * per_tile + (b0_ + k))
                return link

            def stat(t, src):
                return dve.bn_stats(stats[:, bass.ds(t, 1), :], src[:, bass.ds(t, 1), :])

            def norm_stats(name, src=None):
                if src is not None:
                    for t in range(NT):
                        ins = stat(t, src)
                    then(ins)
                for t in range(NT):
                    ins = dve.bn_aggr(mv[:, t, :], stats[:, t, :])
                then(ins)
                dve.tensor_scalar(var[:, :], mv[:, :, 1], LN_EPS, None, ALU.add).then_inc(var_ready, 1)
                dve.wait_ge(std_ready, NORM[name])
                then(dve.reciprocal(rstd[:, :], std[:, :]))
                dve.scalar_tensor_tensor(out=nmr[:, :], in0=mv[:, :, 0], scalar=-1.0, in1=rstd[:, :], op0=ALU.mult,
                                         op1=ALU.mult).then_inc(norm_ready, 1)

            def split_w(name, dst, src, hi):
                dve.wait_ge(w_hi, WPREP[name])
                dve.tensor_tensor(dst, src, hi.bitcast(F32), ALU.subtract).then_inc(w_lo, 1)

            def turn(p0):
                def step(t, b):
                    wait(dve, turn_hi, p0 + t + 1)
                    wait(dve, projected, p0 + t - 1)
                    dve.tensor_tensor(hT_L[:, b, :, :].rearrange("p k i -> p (k i)"), TP[:, BANK * b:BANK * b + D],
                                      hT_H[:, b, :, :].rearrange("p k i -> p (k i)").bitcast(F32),
                                      ALU.subtract).then_inc(turn_lo, 1)
                return step

            tick_at = [-1]

            def tick():
                tick_at[0] += 1
                return dve.memset(ticks[:, tick_at[0]:tick_at[0] + 1], 0.0)

            def mark(s):
                tick().then_inc(s, 1)

            def evac(p0, body):
                def step(t, b):
                    wait(dve, projected, p0 + t + 1)
                    wait(dve, proj_hi, p0 + t + 1)
                    body(t, b).then_inc(proj_read, 1)
                return step

            def project_rows(p0, body, peel=3):
                pipeline(dve, (1, turn(p0)), (3, evac(p0, body)), peel=peel)

            def lo(dst, src, hi):
                return dve.tensor_tensor(dst, src, hi.bitcast(F32), ALU.subtract)

            def read(g0, body):
                def step(t, b):
                    wait(dve, gathered, g0 + t + 1)
                    body(t, b).then_inc(gather_read, 1)
                return step

            one = lambda a, t: a[:, bass.ds(t, 1)]
            row = lambda a, t, n=D: a[:, bass.ds(t, 1), 0:n]

            dve.wait_ge(ld_small, 16 * 2)
            then(dve.tensor_scalar(d1[:, :], d1[:, :], 1.0, None, ALU.add))
            dve.wait_ge(ld_w, LD["L0"])
            for k in range(KB):
                ins = dve.tensor_scalar(raw[:, k, D:2 * D], raw[:, k, 0:D], d1[:, k:k + 1], None, ALU.mult)
            ins.then_inc(raw_ready, 1)
            split_w("L0", WL[:, :, 0:2 * D], raw[:, :, 0:2 * D], WH[:, :, 0:2 * D])
            dve.wait_ge(ld_x, 16)
            norm_stats("L0", X)
            link0 = chain(dve_tail, 1)

            def evac_l0(t, b):
                lo(row(FL, t), pbank[b][0][:, D:2 * D], row(FH, t))
                link0(t, 1, dve.tensor_tensor(row(X, t), row(X, t), pbank[b][0][:, 0:D], ALU.add))
                return dve.tensor_tensor(row(X, t), row(X, t), bcast[:, :], ALU.add)

            project_rows(PJ["L0"], evac_l0, peel=5)
            dve.wait_ge(proj_read, PJ["L0"] + NT)
            dve.wait_ge(ld_w, LD["L1"])
            dve.wait_ge(ld_l1, 16 * 4)
            for k in range(KB):
                for side in range(2):
                    then(dve.tensor_tensor_reduce(out=junk[:, :], in0=raw[:, k, D + 6:D + 6 + D],
                                                  in1=abc[:, side * D:(side + 1) * D], scale=1.0, scalar=0.0,
                                                  op0=ALU.mult, op1=ALU.add, accum_out=wlr[:, k, side:side + 1]))
            dve.tensor_copy(raw[:, :, D + 4:D + 5], wlr[:, :, 1:2])
            dve.memset(raw[:, :, D + 5:D + 6], 0.0).then_inc(raw_ready, 2)
            split_w("L1", WL[:, :, 0:D + 6 + D], raw[:, :, 0:D + 6 + D], WH[:, :, 0:D + 6 + D])
            split_w("L1r", WrL[:, :, :], wlr[:, :, 0:1].broadcast_to([P, KB, P]), WrH[:, :, :])
            dve.tensor_scalar(F2L[:, :, D:D + 2], onezero[:, :, :], 0.0, None, ALU.mult)
            dve.wait_ge(ld_adj, 16 * NT)
            then(dve.tensor_reduce(colsum, AT[:, :, :], AX.X, ALU.add))
            then(dve.tensor_scalar(colsum, colsum, 1.0, 1e-12, ALU.add, ALU.max))
            then(dve.reciprocal(rcol, colsum))
            link_x0 = chain(dve_mid, 1)

            def read_l0(t, b):
                link_x0(t, 1, dve.tensor_tensor(row(X, t), row(X, t), OUT[b][:, 0:D], ALU.subtract))
                return stat(t, X)

            pipeline(dve, (0, read(GA["L0"], read_l0)))
            dve.wait_ge(gather_read, GA["L0"] + NT)
            norm_stats("L1")

            def evac_l1(t, b):
                lo(row(FL, t, D + 2), pbank[b][0][:, 0:D + 2], row(FH, t, D + 2))
                lo(row(F2L, t), pbank[b][1][:, 0:D], row(F2H, t))
                return dve.tensor_copy(vab[:, bass.ds(t, 1), :], pbank[b][0][:, D + 2:D + 5])

            project_rows(PJ["L1"], evac_l1)
            dve.wait_ge(w12_t, 1)
            dve.tensor_copy(raw[0:64, 1, 128:128 + D], TP[0:64, 0:D]).then_inc(w12_c, 1)
            dve.wait_ge(w12_m, 1)
            dve.tensor_copy(W12[:, :, :], TP[:, BANK:BANK + 128].rearrange("p (k n) -> p k n", k=KB)).then_inc(w12_d, 1)

            def read_l1b(t, b):
                dve.tensor_copy(tab[:, bass.ds(t, 1), :], OUT[b][:, D:D + 2])
                return dve.tensor_tensor(row(U1B, t), OUT[b][:, 0:D], bgc[:, :], ALU.add)

            pipeline(dve, (0, read(GA["L1b"], read_l1b)))
            dve.wait_ge(gather_read, GA["L1b"] + NT)
            then(dve.tensor_tensor(tab[:, :, :], tab[:, :, :], vab[:, :, 0:2], ALU.add))
            for c in range(2):
                ins = dve.tensor_scalar(tab[:, :, c:c + 1], tab[:, :, c:c + 1], bab[:, c:c + 1], None, ALU.add)
            ins.then_inc(gate_in, 1)
            dve.wait_ge(ld_w, LD["L2a"])
            mark(raw_ready)
            split_w("L2a", WL[:, :, 0:2 * D], raw[:, :, 0:2 * D], WH[:, :, 0:2 * D])
            dve.wait_ge(w_lo, WPREP["L2a"])
            dve.wait_ge(gate_out, 1)
            link = chain(dve_lead, 1)
            link_t = chain(dve_tail, 4)

            def z_l1(t, b):
                wait(dve, strip_hi, GA["L1a"] + t - 1)
                wait(dve, strip_lo, GA["L1a"] + t - 1)
                link(t, 1, dve.tensor_tensor(
                    jrows(l1_strip[b]), SLB[:, cols(t)].rearrange("p (a i) -> p a i", a=1).broadcast_to([P, NT, P]),
                    vab[:, :, 2:3].broadcast_to([P, NT, P]), ALU.add))
                dve.scalar_tensor_tensor(out=l1_strip[b], in0=l1_strip[b], scalar=SLOPE, in1=l1_strip[b],
                                         op0=ALU.mult, op1=ALU.max).then_inc(scored_z, 1)

            def mask_l1(t, b):
                wait(dve, e_raw, t + 1)
                dve.scalar_tensor_tensor(out=jrows(l1_strip[b]), in0=AT[:, :, cols(t)], scalar=0.0,
                                         in1=jrows(l1_strip[b]), op0=ALU.not_equal, op1=ALU.mult).then_inc(masked, 1)

            def read_l1a(t, b):
                link_t(t, 1, dve.tensor_scalar(one(den, t), OUT[b][:, D:D + 1], 1e-5, None, ALU.add))
                link_t(t, 2, dve.reciprocal(one(rden, t), one(den, t)))
                link_t(t, 3, dve.tensor_tensor(one(ra, t), one(rden, t), tab[:, bass.ds(t, 1), 0], ALU.mult))
                link_t(t, 4, dve.tensor_scalar(row(U1B, t), row(U1B, t), tab[:, bass.ds(t, 1), 1], None, ALU.mult))
                return dve.scalar_tensor_tensor(out=row(U1B, t), in0=OUT[b][:, 0:D], scalar=one(ra, t), in1=row(U1B, t),
                                                op0=ALU.mult, op1=ALU.add)

            pipeline(dve, (1, mask_l1), (0, z_l1), (2, read(GA["L1a"], read_l1a)))

            for k, (t0, t1) in enumerate(SIG_PIECES):
                dve.wait_ge(sig_out, k + 1)
                then(dve.tensor_tensor(X[:, t0:t1, :], X[:, t0:t1, :], U1B[:, t0:t1, :], ALU.add))
                for t in range(t0, t1):
                    ins = stat(t, X)
            then(ins)
            norm_stats("L2")
            for b in range(2):
                ins = dve.memset(expt[b][:, N:NP], 0.0)
            ins.then_inc(pads, 1)
            mark(x_l1)

            for name in ("L2a", "L2b"):
                last = name == "L2b"
                if last:
                    dve.wait_ge(gather_read, GA["L2a"] + NT)
                    dve.wait_ge(ld_w, LD["L2b"])
                    mark(raw_ready)
                    split_w("L2b", WL[:, :, 0:2 * D], raw[:, :, 0:2 * D], WH[:, :, 0:2 * D])

                def evac_l2(t, b):
                    lo(row(FL, t), pbank[b][0][:, 0:D], row(FH, t))
                    return lo(TL[:, :, cols(t)], pbank[b][1].rearrange("p (k i) -> p k i", k=4), TH[:, :, cols(t)])

                project_rows(PJ[name], evac_l2)

                def top(t, b):
                    wait(dve, scored, SCO[name] + t + 1)
                    dve.tensor_reduce(one(nmax, t), SC[:, 0:N], AX.X, ALU.max, negate=True).then_inc(maxed, 1)

                def mask(t, b):
                    wait(dve, strip_turned, SCO[name] + t + 1)
                    wait(dve, strip_hi, GA[name] + t)
                    wait(dve, strip_lo, GA[name] + t)
                    dve.tensor_tensor(strip, TPS, AT[:, :, cols(t)], ALU.mult).then_inc(masked, 1)

                link2 = chain(dve_tail, 4 if last else 2)

                def read_l2(t, b):
                    wait(dve, exped, SCO[name] + t + 1)
                    link2(t, 1, dve.reciprocal(one(rz, t), one(zsum, t)))
                    link2(t, 2, dve.scalar_tensor_tensor(out=vrow[:, :], in0=OUT[b][:, 0:D], scalar=one(rz, t),
                                                         in1=row(H, t), op0=ALU.mult, op1=ALU.add))
                    ins = dve.scalar_tensor_tensor(out=row(H, t), in0=vrow[:, :], scalar=SLOPE, in1=vrow[:, :],
                                                   op0=ALU.mult, op1=ALU.max)
                    if last:
                        link2(t, 3, ins)
                        link2(t, 4, dve.tensor_tensor(row(X, t), row(X, t), row(H, t), ALU.add))
                        ins = stat(t, X)
                    return ins

                pipeline(dve, (0, top), (1, mask), (2, read(GA[name], read_l2)))
            dve.wait_ge(gather_read, GA["L2b"] + NT)
            norm_stats("L3")
            for t in range(NT):
                ins = dve.tensor_tensor(AT[:, t, t * P:(t + 1) * P], AT[:, t, t * P:(t + 1) * P], ident[:, :], ALU.add)
            ins.then_inc(adj_plus, 1)
            dve.tensor_copy(FH[:, :, D:D + 2], onezero[:, :, :])
            dve.tensor_scalar(FL[:, :, D:D + 2], onezero[:, :, :], 0.0, None, ALU.mult)
            link_i = chain(dve_mid, 2)

            def split_h(t):
                dve.wait_ge(h_rows, t + (NT + 1))
                link_i(t, 1, dve.tensor_copy(row(FH, t), row(H, t)))
                link_i(t, 2, lo(row(FL, t), row(H, t), row(FH, t)))

            each_tile(dve, split_h)
            mark(adj_plus)
            dve.wait_ge(ld_w, LD["L3s"])
            mark(raw_ready)

            def read_l3s(t, b):
                dve.tensor_copy(one(rowsum, t), OUT[b][:, D:D + 1])
                return dve.tensor_copy(row(UG, t), OUT[b][:, 0:D])

            pipeline(dve, (0, read(GA["L3s"], read_l3s)))
            dve.wait_ge(gather_read, GA["L3s"] + NT)
            then(dve.tensor_scalar(rowsum, rowsum, 1e-12, None, ALU.max))
            dve.reciprocal(rrow, rowsum).then_inc(gate_in, 1)
            split_w("L3s", WL[:, :, 0:2 * D], raw[:, :, 0:2 * D], WH[:, :, 0:2 * D])
            dve.wait_ge(ld_w, LD["L3u"])
            dve.wait_ge(gate_in, 2)
            mark(raw_ready)
            split_w("L3u", VL[:, :, :], raw[:, :, 0:2 * D], VH[:, :, :])
            link_s = chain(dve_tail, 1)

            def evac_l3s(t, b):
                dve.scalar_tensor_tensor(out=row(FL, t), in0=pbank[b][1][:, 0:D], scalar=one(rrow, t),
                                         in1=row(FH, t).bitcast(F32), op0=ALU.mult, op1=ALU.subtract)
                dve.scalar_tensor_tensor(out=row(G2L, t), in0=pbank[b][1][:, D:2 * D], scalar=one(rcol, t),
                                         in1=row(G2H, t).bitcast(F32), op0=ALU.mult, op1=ALU.subtract)
                link_s(t, 1, dve.scalar_tensor_tensor(out=row(Y, t), in0=pbank[b][0][:, 0:D], scalar=one(rrow, t),
                                                      in1=row(H, t), op0=ALU.mult, op1=ALU.add))
                return dve.scalar_tensor_tensor(out=row(Y, t), in0=pbank[b][0][:, D:2 * D], scalar=one(rcol, t),
                                                in1=row(Y, t), op0=ALU.mult, op1=ALU.add)

            project_rows(PJ["L3s"], evac_l3s)
            dve.wait_ge(proj_read, PJ["L3s"] + NT)
            link_t3 = chain(dve_tail, 1)

            def read_l3t(t, b):
                link_t3(t, 1, dve.scalar_tensor_tensor(out=row(Y, t), in0=OUT[b][:, 0:D], scalar=one(rrow, t),
                                                       in1=row(Y, t), op0=ALU.mult, op1=ALU.add))
                return dve.scalar_tensor_tensor(out=row(Y, t), in0=OUT[b][:, D:2 * D], scalar=one(rcol, t),
                                                in1=row(Y, t), op0=ALU.mult, op1=ALU.add)

            pipeline(dve, (0, read(GA["L3t"], read_l3t)))
            dve.wait_ge(gather_read, GA["L3t"] + NT)
            dve.wait_ge(ld_w, LD["L3q"])
            dve.tensor_copy(raw[:, :, 0:64], W12[:, :, :])
            dve.memset(raw[:, :, 64:128], 0.0)
            dve.memset(raw[:, :, 192:256], 0.0).then_inc(raw_ready, 1)
            split_w("L3q", VQL[:, :, :], raw[:, :, 0:D], VQH[:, :, :])

            def evac_l3q(t, b):
                lo(row(FL, t), row(H, t), row(FH, t))
                return lo(TQL[:, :, cols(t)], pbank[b][0][:, 0:D].rearrange("p (k i) -> p k i", k=2), TQH[:, :, cols(t)])

            project_rows(PJ["L3q"], evac_l3q)

            for name in ("A0", "A1"):
                def top_a(t, b):
                    wait(dve, scored, SCO[name] + t + 1)
                    dve.tensor_reduce(one(nmax, t), [SC, TP][b][:, 0:N], AX.X, ALU.max, negate=True).then_inc(maxed, 1)

                pipeline(dve, (0, top_a))
                dve.wait_ge(exped, SCO[name] + NT)
                n = int(name == "A1")
                dve.tensor_scalar(target, zsum, P_NUC, None, ALU.mult)
                for kt in kept_t:
                    ins = dve.memset(kt[:, N:NP], 0.0)
                then(ins)

                def search(s, turns, base, own):
                    dve.memset(cut.bitcast(U32), BASE_BITS).then_inc(s, 1)
                    dve.memset(bits.bitcast(U32), 1 << TOP_BIT).then_inc(s, 1)
                    dve.wait_ge(s, base + 2)
                    steps = own + (7 if own < NT else 5)

                    with dve.Fori(0, turns, 1) as i:
                        done = [0]

                        def counted(ins):
                            ins.then_inc(s, 1)
                            done[0] += 1
                            return done[0]

                        def reached(k):
                            dve.wait_ge(s, i * steps + (base + 2 + k))

                        reached(counted(dve.tensor_tensor(cand.bitcast(U32), cut.bitcast(U32), bits.bitcast(U32),
                                                          ALU.bitwise_or)))
                        if own < NT:
                            dve.tensor_scalar(nudged, cand, -(1.0 - 2.0 ** -20), None,
                                              ALU.mult).then_inc(cand_ready, 1)
                        first = done[0]
                        for t in range(own):
                            if t >= 2:
                                reached(first + t - 1)
                            last = counted(dve.scalar_tensor_tensor(
                                out=kept_t[t % 2][:, 0:N], in0=E[:, t, :], scalar=cand[:, t:t + 1], in1=E[:, t, :],
                                op0=ALU.is_ge, op1=ALU.mult, accum_out=mass[:, t:t + 1]))
                        counted(dve.tensor_single_scalar(bits.bitcast(U32), bits.bitcast(U32), 1,
                                                         ALU.logical_shift_right))
                        if own < NT:
                            dve.wait_ge(act_step, i * (2 * ACT_TILES) + ((n * COARSE_BITS + 1) * 2 * ACT_TILES))
                            reached(counted(dve.scalar_tensor_tensor(
                                out=acc[:, own:], in0=sign_sum[:, own:], scalar=float(N), in1=nudged[:, own:],
                                op0=ALU.add, op1=ALU.mult)))
                            last = counted(dve.scalar_tensor_tensor(
                                out=mass[:, own:], in0=acc[:, own:], scalar=-0.5, in1=relu_sum[:, own:],
                                op0=ALU.mult, op1=ALU.add))
                        reached(last)
                        reached(counted(dve.tensor_tensor(keep, mass, target, ALU.is_ge)))
                        reached(counted(dve.tensor_tensor(cand, cand, keep, ALU.mult)))
                        reached(counted(dve.tensor_tensor(cut, cut, cand, ALU.max)))
                        assert done[0] == steps
                    return 2 + steps * turns

                seq[0] += search(dve_seq, COARSE_BITS, seq[0], DVE_TILES)
                then(dve.tensor_single_scalar(upper.bitcast(U32), cut.bitcast(U32),
                                              (1 << (TOP_BIT + 1 - COARSE_BITS)) - 1, ALU.bitwise_or))
                start = seq[0]

                def below_upper(t):
                    if t >= 2:
                        dve.wait_ge(dve_seq, start + 2 * t - 1)
                    dve.scalar_tensor_tensor(out=kept_t[t % 2][:, 0:N], in0=E[:, t, :], scalar=upper[:, t:t + 1],
                                             in1=E[:, t, :], op0=ALU.is_le, op1=ALU.mult,
                                             accum_out=below[:, t:t + 1]).then_inc(dve_seq, 1)

                below_upper(0)
                for t in range(NT):
                    if t + 1 < NT:
                        below_upper(t + 1)
                    dve.wait_ge(dve_seq, start + max(2 * t, 1))
                    dve.max(top8[:, 0, t, :], kept_t[t % 2][:, 0:N]).then_inc(dve_seq, 1)
                seq[0] += 2 * NT
                dve.wait_ge(dve_seq, seq[0])
                t8, c8, x8 = (top8[:, k, :, :] for k in range(3))

                def wide(a):
                    return a.rearrange("p (t o) -> p t o", o=1).broadcast_to([P, NT, 8])

                then(dve.tensor_tensor(above, zsum, below, ALU.subtract))
                then(dve.tensor_tensor(c8[:, :, 0], above, t8[:, :, 0], ALU.add))
                for k in range(1, 8):
                    then(dve.tensor_tensor(c8[:, :, k], c8[:, :, k - 1], t8[:, :, k], ALU.add))
                then(dve.tensor_tensor(x8, c8, wide(target), ALU.is_ge))
                then(dve.tensor_tensor(x8, x8, t8, ALU.mult))
                then(dve.tensor_reduce(vcut, x8, AX.X, ALU.max))
                then(dve.tensor_tensor(vcut, vcut, t8[:, :, 7], ALU.max))
                then(dve.tensor_tensor(x8, t8, wide(vcut), ALU.is_gt))
                then(dve.tensor_tensor(x8, x8, t8, ALU.mult))
                then(dve.tensor_reduce(acc, x8, AX.X, ALU.add))
                then(dve.tensor_tensor(above, above, acc, ALU.add))

                def mark_ties(s):
                    for t in range(NT):
                        dve.tensor_scalar(EQ[:, t, :], E[:, t, :], vcut[:, t:t + 1], 0.0, ALU.is_equal, ALU.add,
                                          accum_out=ties[:, t:t + 1]).then_inc(s, 1)

                def raise_flag(k, flag):
                    then(dve.tensor_reduce(flags[:, k:k + 1], flag, AX.X, ALU.max))
                    mark(flag_ready)
                    dve.wait_ge(flag_sum, 2 * n + k + 1)
                    then(dve.tensor_copy(flag_i[:, k:k + 1], OUT[0][0:1, k:k + 1]))
                    return dve.value_load(flag_i[0:1, k:k + 1], min_val=0, max_val=P)

                mark_ties(dve_seq)
                seq[0] += NT
                dve.wait_ge(dve_seq, seq[0])
                then(dve.tensor_tensor(acc, vcut, ties, ALU.mult))
                then(dve.tensor_tensor(acc, acc, above, ALU.add))
                then(dve.tensor_tensor(flag_a, acc, target, ALU.is_lt))
                then(dve.tensor_tensor(flag_b, above, target, ALU.is_ge))
                then(dve.tensor_tensor(flag_a, flag_a, flag_b, ALU.max))
                unsettled = raise_flag(0, flag_a)
                with dve.If(unsettled >= 1):
                    g = general[name]
                    b1 = search(g, SEARCH_BITS, 0, NT)
                    dve.tensor_copy(vcut, cut).then_inc(g, 1)
                    dve.wait_ge(g, b1 + 1)
                    for t in range(NT):
                        if t >= 2:
                            dve.wait_ge(g, b1 + 1 + t - 1)
                        dve.scalar_tensor_tensor(out=kept_t[t % 2][:, 0:N], in0=E[:, t, :], scalar=vcut[:, t:t + 1],
                                                 in1=E[:, t, :], op0=ALU.is_gt, op1=ALU.mult,
                                                 accum_out=above[:, t:t + 1]).then_inc(g, 1)
                    mark_ties(g)
                    dve.wait_ge(g, b1 + 1 + 2 * NT)
                then(dve.reciprocal(acc, vcut))
                then(dve.tensor_tensor(qlim, target, above, ALU.subtract))
                then(dve.tensor_tensor(qlim, qlim, acc, ALU.mult))
                then(dve.tensor_scalar(qlim, qlim, 1.0, None, ALU.add))
                then(dve.tensor_tensor(flag_a, ties, qlim, ALU.is_ge))
                partly = raise_flag(1, flag_a)
                with dve.If(partly >= 1):
                    ts = tie_step[name]
                    for t in range(NT):
                        dve.tensor_tensor_scan(kept_t[0][:, 0:N], EQ[:, t, :], EQ[:, t, :], 0.0, ALU.add,
                                               ALU.max).then_inc(ts, 1)
                        dve.wait_ge(ts, 3 * t + 1)
                        dve.scalar_tensor_tensor(out=kept_t[1][:, 0:N], in0=kept_t[0][:, 0:N], scalar=qlim[:, t:t + 1],
                                                 in1=EQ[:, t, :], op0=ALU.is_ge, op1=ALU.mult).then_inc(ts, 1)
                        dve.wait_ge(ts, 3 * t + 2)
                        dve.scalar_tensor_tensor(out=E[:, t, :], in0=kept_t[1][:, 0:N], scalar=-2.0, in1=E[:, t, :],
                                                 op0=ALU.mult, op1=ALU.add).then_inc(ts, 1)
                        dve.wait_ge(ts, 3 * t + 3)
                then(tick())

                def keep_e(t, b):
                    wait(dve, strip_turned, SCO[name] + t - 1)
                    dve.scalar_tensor_tensor(out=kept_t[b][:, 0:N], in0=E[:, bass.ds(t, 1), :], scalar=one(vcut, t),
                                             in1=E[:, bass.ds(t, 1), :], op0=ALU.is_ge, op1=ALU.mult,
                                             accum_out=one(zkept, t)).then_inc(kept, 1)

                def lo_turned(t, b):
                    wait(dve, strip_hi, GA[name] + t + 1)
                    wait(dve, gathered, GA[name] + t - 1)
                    lo(SL[:, b, :, :], TPS, SH[:, b, :, :]).then_inc(strip_lo, 1)

                link_a = chain(dve_tail, 1)
                link_y = chain(dve_mid, 1) if name == "A1" else None

                def read_a(t, b):
                    wait(dve, kept, KEEP[name] + t + 1)
                    link_a(t, 1, dve.reciprocal(one(rkept, t), one(zkept, t)))
                    if name == "A0":
                        return dve.tensor_scalar(row(UA, t), OUT[b][:, 0:D], one(rkept, t), None, ALU.mult)
                    link_y(t, 1, dve.scalar_tensor_tensor(out=row(Y, t), in0=OUT[b][:, 0:D], scalar=one(rkept, t),
                                                          in1=row(Y, t), op0=ALU.mult, op1=ALU.add))
                    return stat(t, Y)

                pipeline(dve, (0, keep_e), (1, lo_turned), (2, read(GA[name], read_a)))
                dve.wait_ge(gather_read, GA[name] + NT)
                if name == "A0":
                    dve.wait_ge(ld_w, LD["L3a"])
                    mark(raw_ready)
                    split_w("L3a", WL[:, :, 0:2 * D], raw[:, :, 0:2 * D], WH[:, :, 0:2 * D])

                    def evac_l3a(t, b):
                        lo(row(FL, t), pbank[b][0][:, D:2 * D], row(FH, t))
                        lo(TQL[:, :, cols(t)], pbank[b][1][:, 0:D].rearrange("p (k i) -> p k i", k=2),
                           TQH[:, :, cols(t)])
                        return dve.tensor_tensor(row(Y, t), row(Y, t), pbank[b][0][:, 0:D], ALU.add)

                    project_rows(PJ["L3a"], evac_l3a)
            norm_stats("end")
            dve.wait_ge(ld_late, 32)
            link_f = chain(dve_tail, 2)

            def final(t):
                dve.wait_ge(fin_a, t + 1)
                link_f(t, 1, dve.tensor_tensor(row(Y, t), row(Y, t), gam[:, :], ALU.mult))
                dve.tensor_tensor(row(X, t), row(X, t), bet[:, :], ALU.add)
                link_f(t, 2, tick())
                dve.tensor_tensor(row(Y, t), row(Y, t), row(X, t), ALU.add).then_inc(fin, 1)

            each_tile(dve, final)


_ORDER = ["x", "adjT", "L0_gnn_weight", "L0_gnn_learnable_diag_1", "L0_gnn_bias", "L1_gnn_W_sa", "L1_gnn_a_sa",
          "L1_gnn_W_gcnb", "L1_gnn_b_gcnb", "L1_gnn_Wa", "L1_gnn_ba", "L1_gnn_Wb", "L1_gnn_bb", "L2_gnn_W_stack",
          "L3_gnn_W1", "L3_gnn_W2", "L3_gnn_W3", "L3_gnn_U1", "L3_gnn_U2", "L3_gnn_U3", "L3_gnn_gamma", "L3_gnn_beta"]


def kernel(**inputs):
    import numpy as _np
    import concourse.bacc as _bacc
    from concourse import mybir as _mybir
    from concourse.bass_utils import run_bass_kernel_spmd as _run

    inputs = dict(inputs)
    x, adj = _np.asarray(inputs.pop("x")), _np.asarray(inputs.pop("adj"))
    inputs["x"] = _np.zeros((NP, D), x.dtype)
    inputs["x"][:N] = x
    inputs["adjT"] = _np.zeros((NP, NP), adj.dtype)
    inputs["adjT"][:N, :N] = adj.T
    nc = _bacc.Bacc("TRN2", target_bir_lowering=False, num_devices=1)
    arrays, args = {}, []
    for name in _ORDER:
        a = _np.ascontiguousarray(inputs[name])
        arrays[f"in_{name}"] = a
        args.append(nc.dram_tensor(f"in_{name}", a.shape, _mybir.dt.from_np(a.dtype), kind="ExternalInput").ap())
    args.append(nc.dram_tensor("out_rows", (N, D), _mybir.dt.float32, kind="ExternalOutput").ap())
    build(nc, *args)
    r = _run(nc, [arrays], core_ids=[0])
    return r.results[0]["out_rows"]
```
